# Optimizing a Trainium2 kernel written in Bass

```python
import numpy as np
import jax
import jax.numpy as jnp

def _softmax(x, axis=-1):
    return jax.nn.softmax(x, axis=axis)

def _gelu(x):
    return jax.nn.gelu(x, approximate=True)

def _silu(x):
    return jax.nn.silu(x)

def _sigmoid(x):
    return jax.nn.sigmoid(x)

def _layernorm(x, axis=-1, eps=1e-05):
    m = jnp.mean(x, axis=axis, keepdims=True)
    v = jnp.var(x, axis=axis, keepdims=True)
    return (x - m) / jnp.sqrt(v + eps)

def _scatter_add(tgt, idx, src, axis=0):
    return tgt.at[idx].add(src)

def _segment_sum(src, seg, n):
    return jax.ops.segment_sum(src, seg, n)
kernel_name = 'mk_flamingo_gated_d4_seqx_r4_766c80'

def setup_inputs(seed: int=0):
    np.random.seed(seed)
    _w = jnp.asarray

    def _rec_inputs():
        import jax
        import jax.numpy as jnp
        _rk = jax.random.key(seed)
        x = 7.22e-05 + 1 * jax.random.normal(jax.random.fold_in(_rk, 1), (4, 512, 512), jnp.float32)
        _lenS = 512 - jax.random.randint(jax.random.fold_in(_rk, 7), (4,), 0, max(1, 512 // 4) + 1, jnp.int32)
        _lenS2 = 512 - jax.random.randint(jax.random.fold_in(_rk, 8), (4,), 0, max(1, 512 // 4) + 1, jnp.int32)
        _ctx_1024P = jax.random.normal(jax.random.fold_in(_rk, 11), (4, 16, 256), jnp.float32)
        _ctx_1024c = jax.random.dirichlet(jax.random.fold_in(_rk, 511), 0.3 * jnp.ones((16,), jnp.float32), (4, 512))
        _ctx_1024t = jnp.einsum('bsk,bkd->bsd', _ctx_1024c, _ctx_1024P)
        _ctx_1024t = _ctx_1024t * jax.lax.rsqrt(jnp.mean(jnp.square(_ctx_1024t)) + 1e-12) * 0.953939
        ctx_1024 = -0.000673644 + 1.00013 * (_ctx_1024t + 0.3 * jax.random.normal(jax.random.fold_in(_rk, 611), (4, 512, 256), jnp.float32))
        fside_BxSx2_0 = jax.random.uniform(jax.random.fold_in(_rk, 12), (4, 512, 2), jnp.float32, 0.0, 0.999707)
        _g = jax.random.normal(jax.random.fold_in(_rk, 9001), (2, 4), jnp.float32)
        _g = jnp.sign(_g) * jnp.maximum(jnp.abs(_g), 1.0) + (_g == 0) * 1.0
        g_xattn = _g[0]
        g_ffn = _g[1]
        return (x, ctx_1024, fside_BxSx2_0, g_xattn, g_ffn)
    x, ctx_1024, fside_BxSx2_0, g_xattn, g_ffn = _rec_inputs()

    def _L0_xattn_setup():
        import jax, jax.numpy as jnp
        import numpy as np
        B, S1, S2, DCA = (2, 512, 256, 16)
        QDIM, KDIM, H = (512, 256, 16)
        HD = QDIM // H
        SCALE = HD ** (-0.5)
        EPS = 1e-06
        DCA_WEIGHT = 1.0

        def _ln(t, w, b):
            m = jnp.mean(t, axis=-1, keepdims=True)
            v = jnp.var(t, axis=-1, keepdims=True)
            return (t - m) * jax.lax.rsqrt(v + EPS) * w + b

        def _attn(q, k, v):
            s = jnp.einsum('bhqd,bhkd->bhqk', q, k) * SCALE
            p = jax.nn.softmax(s, axis=-1)
            return jnp.einsum('bhqk,bhkd->bhqd', p, v)
        key = jax.random.key(seed)
        ks = jax.random.split(key, 8)
        w = lambda k, shape: jax.random.normal(k, shape, jnp.float32) * 0.02
        return {'x': jax.random.normal(ks[0], (B, S1, QDIM), jnp.float32), 'y': jax.random.normal(ks[1], (B, S2 + DCA, KDIM), jnp.float32), 'Wq': w(ks[2], (QDIM, QDIM)), 'bq': jnp.zeros((QDIM,), jnp.float32), 'Wk': w(ks[3], (KDIM, QDIM)), 'bk': jnp.zeros((QDIM,), jnp.float32), 'Wv': w(ks[4], (KDIM, QDIM)), 'bv': jnp.zeros((QDIM,), jnp.float32), 'Wkv_dca': w(ks[5], (KDIM, 2 * QDIM)), 'bkv_dca': jnp.zeros((2 * QDIM,), jnp.float32), 'qn_w': jnp.ones((HD,), jnp.float32), 'qn_b': jnp.zeros((HD,), jnp.float32), 'kn_w': jnp.ones((HD,), jnp.float32), 'kn_b': jnp.zeros((HD,), jnp.float32), 'kn_dca_w': jnp.ones((HD,), jnp.float32), 'kn_dca_b': jnp.zeros((HD,), jnp.float32), 'Wo': w(ks[6], (QDIM, QDIM)), 'bo': jnp.zeros((QDIM,), jnp.float32)}
    _L0_xattn_all = _L0_xattn_setup()
    _L0_xattn_in = {k: v for k, v in _L0_xattn_all.items() if k in ('Wq', 'bq', 'Wk', 'bk', 'Wv', 'bv', 'Wkv_dca', 'bkv_dca', 'qn_w', 'qn_b', 'kn_w', 'kn_b', 'kn_dca_w', 'kn_dca_b', 'Wo', 'bo')}
    del _L0_xattn_all

    def _L0_ffn_setup():
        import jax, jax.numpy as jnp
        import numpy as np

        @jax.custom_vjp
        def ste_sign(x):
            return jnp.sign(x)

        def _ste_fwd(x):
            return (jnp.sign(x), None)

        def _ste_bwd(_, g):
            return (g,)
        ste_sign.defvjp(_ste_fwd, _ste_bwd)
        D_MODEL = 512
        D_HIDDEN = 2048
        key = jax.random.key(seed)
        k_x, k_up, k_dn = jax.random.split(key, 3)
        x = jax.random.normal(k_x, (2, 512, D_MODEL), dtype=jnp.float32)
        up_weight = jax.random.normal(k_up, (D_HIDDEN, D_MODEL), dtype=jnp.float32) * 0.02
        down_weight = jax.random.normal(k_dn, (D_MODEL, D_HIDDEN), dtype=jnp.float32) * 0.02
        up_scale = jnp.ones((D_HIDDEN,), dtype=jnp.float32)
        down_scale = jnp.ones((D_MODEL,), dtype=jnp.float32)
        output_scale = jnp.ones((1,), dtype=jnp.float32)
        return {'x': x, 'up_weight': up_weight, 'down_weight': down_weight, 'up_scale': up_scale, 'down_scale': down_scale, 'output_scale': output_scale}
    _L0_ffn_all = _L0_ffn_setup()
    _L0_ffn_in = {k: v for k, v in _L0_ffn_all.items() if k in ('up_weight', 'down_weight', 'up_scale', 'down_scale', 'output_scale')}
    del _L0_ffn_all

    def _L1_xattn_setup():
        import jax, jax.numpy as jnp
        import numpy as np
        key = jax.random.key(seed)
        ks = jax.random.split(key, 6)
        B, L, N, C, D = (8, 128, 512, 256, 128)
        return {'teacher_logits': jax.random.normal(ks[0], (B, L, N), dtype=jnp.float32), 'teacher_features': jax.random.normal(ks[1], (B, N, C), dtype=jnp.float32), 'Wq': jax.random.normal(ks[2], (D, C), dtype=jnp.float32) * (1.0 / np.sqrt(C)), 'bq': jnp.zeros((D,), dtype=jnp.float32), 'Wk': jax.random.normal(ks[3], (D, C), dtype=jnp.float32) * (1.0 / np.sqrt(C)), 'bk': jnp.zeros((D,), dtype=jnp.float32)}
    _L1_xattn_all = _L1_xattn_setup()
    _L1_xattn_in = {k: v for k, v in _L1_xattn_all.items() if k in ('Wq', 'bq', 'Wk', 'bk')}
    del _L1_xattn_all

    def _L1_ffn_setup():
        import jax, jax.numpy as jnp
        import numpy as np
        EPS = 1e-07

        def per_token_quant_int8(x, eps=EPS):
            absmax = jnp.max(jnp.abs(x), axis=-1, keepdims=True)
            scale = jnp.maximum(absmax, eps) / 127.0
            q = jnp.clip(jnp.round(x / scale), -128, 127).astype(jnp.int8)
            return (q, scale)
        key = jax.random.key(seed)
        k1, k2, k3, k4 = jax.random.split(key, 4)
        B, S, IN, OUT = (4, 1024, 512, 512)
        x = jax.random.normal(k1, (B, S, IN), dtype=jnp.float32)
        weight = jax.random.randint(k2, (OUT, IN), -127, 128, dtype=jnp.int32).astype(jnp.int8)
        w_scale = jax.random.uniform(k3, (OUT, 1), dtype=jnp.float32) * 0.01 + 0.0001
        bias = jax.random.normal(k4, (OUT,), dtype=jnp.float32)
        return {'x': x, 'weight': weight, 'w_scale': w_scale, 'bias': bias}
    _L1_ffn_all = _L1_ffn_setup()
    _L1_ffn_in = {k: v for k, v in _L1_ffn_all.items() if k in ('weight', 'w_scale', 'bias')}
    del _L1_ffn_all

    def _L2_xattn_setup():
        import jax, jax.numpy as jnp
        import numpy as np
        import math
        B, L, DM = (2, 512, 256)
        DS, DC, EXP = (16, 4, 2)
        DI = EXP * DM
        DR = math.ceil(DM / 16)
        DT_MIN, DT_MAX, DT_FLOOR = (0.001, 0.1, 0.0001)

        def _ssm_forward(hidden_states, z, in_proj_w, conv_w, conv_b, x_proj_w, dt_proj_w, dt_proj_b, A_log, D):
            b = hidden_states.shape[0]
            x = jnp.einsum('ed,bld->bel', in_proj_w, hidden_states)
            xp = jnp.pad(x, ((0, 0), (0, 0), (DC - 1, 0)))
            xc = jax.lax.conv_general_dilated(xp, conv_w[:, None, :], window_strides=(1,), padding='VALID', dimension_numbers=('NCH', 'OIH', 'NCH'), feature_group_count=DI)
            u = jax.nn.silu(xc + conv_b[None, :, None])
            x_dbl = jnp.einsum('ke,bel->bkl', x_proj_w, u)
            dt_lo = x_dbl[:, :DR]
            Bm = x_dbl[:, DR:DR + DS]
            Cm = x_dbl[:, DR + DS:]
            delta = jax.nn.softplus(jnp.einsum('er,brl->bel', dt_proj_w, dt_lo) + dt_proj_b[None, :, None])
            A = -jnp.exp(A_log)

            def step(state, xs):
                d_t, B_t, C_t, u_t = xs
                dA = jnp.exp(d_t[..., None] * A)
                state = state * dA + (d_t * u_t)[..., None] * B_t[:, None, :]
                y_t = jnp.einsum('ben,bn->be', state, C_t)
                return (state, y_t)
            xs = (jnp.moveaxis(delta, -1, 0), jnp.moveaxis(Bm, -1, 0), jnp.moveaxis(Cm, -1, 0), jnp.moveaxis(u, -1, 0))
            state0 = jnp.zeros((b, DI, DS), delta.dtype)
            _, ys = jax.lax.scan(step, state0, xs)
            y = jnp.moveaxis(ys, 0, -1)
            y = y + D[None, :, None] * u
            y = y * jax.nn.silu(z)
            return jnp.swapaxes(y, 1, 2)
        key = jax.random.key(seed)
        ks = jax.random.split(key, 8)
        hidden_states = jax.random.normal(ks[0], (B, L, DM), jnp.float32)
        z = jax.random.normal(ks[1], (B, DI, L), jnp.float32)
        in_proj_w = jax.random.normal(ks[2], (DI, DM), jnp.float32) * DM ** (-0.5)
        conv_w = jax.random.normal(ks[3], (DI, DC), jnp.float32) * DC ** (-0.5)
        conv_b = jnp.zeros((DI,), jnp.float32)
        x_proj_w = jax.random.normal(ks[4], (DR + 2 * DS, DI), jnp.float32) * DI ** (-0.5)
        dt_std = DR ** (-0.5)
        dt_proj_w = jax.random.uniform(ks[5], (DI, DR), jnp.float32, -dt_std, dt_std)
        dt = jnp.exp(jax.random.uniform(ks[6], (DI,), jnp.float32) * (math.log(DT_MAX) - math.log(DT_MIN)) + math.log(DT_MIN))
        dt = jnp.clip(dt, DT_FLOOR)
        dt_proj_b = dt + jnp.log(-jnp.expm1(-dt))
        A_log = jnp.log(jnp.broadcast_to(jnp.arange(1, DS + 1, dtype=jnp.float32), (DI, DS)))
        D = jnp.ones((DI,), jnp.float32)
        return dict(hidden_states=hidden_states, z=z, in_proj_w=in_proj_w, conv_w=conv_w, conv_b=conv_b, x_proj_w=x_proj_w, dt_proj_w=dt_proj_w, dt_proj_b=dt_proj_b, A_log=A_log, D=D)
    _L2_xattn_all = _L2_xattn_setup()
    _L2_xattn_in = {k: v for k, v in _L2_xattn_all.items() if k in ('in_proj_w', 'conv_w', 'conv_b', 'x_proj_w', 'dt_proj_w', 'dt_proj_b', 'A_log', 'D')}
    del _L2_xattn_all

    def _L2_ffn_setup():
        import jax, jax.numpy as jnp
        import numpy as np
        B, S, H = (4, 512, 512)
        I = 352
        E = 8
        K = 2
        key = jax.random.key(seed)
        ks = jax.random.split(key, 5)
        sc_h = 1.0 / np.sqrt(H)
        sc_i = 1.0 / np.sqrt(I)
        return {'hidden_states': jax.random.normal(ks[0], (B, S, H), dtype=jnp.float32), 'gate_w': jax.random.normal(ks[1], (E, H), dtype=jnp.float32) * sc_h, 'w_gate': jax.random.normal(ks[2], (E, H, I), dtype=jnp.float32) * sc_h, 'w_up': jax.random.normal(ks[3], (E, H, I), dtype=jnp.float32) * sc_h, 'w_down': jax.random.normal(ks[4], (E, I, H), dtype=jnp.float32) * sc_i}
    _L2_ffn_all = _L2_ffn_setup()
    _L2_ffn_in = {k: v for k, v in _L2_ffn_all.items() if k in ('gate_w', 'w_gate', 'w_up', 'w_down')}
    del _L2_ffn_all

    def _L3_xattn_setup():
        import jax, jax.numpy as jnp
        import numpy as np
        DIM = 512
        CTX_DIM = 256
        N_HEADS = 32
        HEAD_DIM = DIM // N_HEADS
        POS_DIM = 2
        B, N, CTXN = (2, 512, 512)
        ROPE_BASE = 10000.0

        def apply_axial_rope(x, pos):
            b, n, h, d = x.shape
            p = pos.shape[-1]
            dpa = d // p
            half = dpa // 2
            freqs = ROPE_BASE ** (-jnp.arange(half, dtype=x.dtype) / half)
            ang = pos[..., :, None] * freqs
            cos = jnp.cos(ang)[:, :, None, :, :]
            sin = jnp.sin(ang)[:, :, None, :, :]
            xr = x.reshape(b, n, h, p, half, 2)
            x1, x2 = (xr[..., 0], xr[..., 1])
            out = jnp.stack([x1 * cos - x2 * sin, x1 * sin + x2 * cos], axis=-1)
            return out.reshape(b, n, h, d)
        key = jax.random.key(seed)
        ks = jax.random.split(key, 8)
        x = jax.random.normal(ks[0], (B, N, DIM), jnp.float32)
        ctx = jax.random.normal(ks[1], (B, CTXN, CTX_DIM), jnp.float32)
        pos_map = jax.random.uniform(ks[2], (B, N, POS_DIM), jnp.float32)
        ctx_pos_map = jax.random.uniform(ks[3], (B, CTXN, POS_DIM), jnp.float32)
        Wq = jax.random.normal(ks[4], (DIM, DIM), jnp.float32) / np.sqrt(DIM)
        Wkv = jax.random.normal(ks[5], (CTX_DIM, 2 * DIM), jnp.float32) / np.sqrt(CTX_DIM)
        Wout = jax.random.normal(ks[6], (DIM, DIM), jnp.float32) / np.sqrt(DIM)
        bout = jnp.zeros((DIM,), jnp.float32)
        return {'x': x, 'ctx': ctx, 'pos_map': pos_map, 'ctx_pos_map': ctx_pos_map, 'Wq': Wq, 'Wkv': Wkv, 'Wout': Wout, 'bout': bout}
    _L3_xattn_all = _L3_xattn_setup()
    _L3_xattn_in = {k: v for k, v in _L3_xattn_all.items() if k in ('Wq', 'Wkv', 'Wout', 'bout')}
    del _L3_xattn_all

    def _L3_ffn_setup():
        import jax, jax.numpy as jnp
        import numpy as np
        K_TOP = 2
        key = jax.random.key(seed)
        ks = jax.random.split(key, 6)
        s = 0.02
        B, S, H, D = (4, 256, 512, 256)
        E_SH, E_RT = (2, 16)
        return {'x': jax.random.normal(ks[0], (B, S, H), dtype=jnp.float32), 'Wsh_up': jax.random.normal(ks[1], (E_SH, H, D), dtype=jnp.float32) * s, 'Wsh_down': jax.random.normal(ks[2], (E_SH, D, H), dtype=jnp.float32) * s, 'Wrt_up': jax.random.normal(ks[3], (E_RT, H, D), dtype=jnp.float32) * s, 'Wrt_down': jax.random.normal(ks[4], (E_RT, D, H), dtype=jnp.float32) * s, 'W_router': jax.random.normal(ks[5], (H, E_RT), dtype=jnp.float32) * s}
    _L3_ffn_all = _L3_ffn_setup()
    _L3_ffn_in = {k: v for k, v in _L3_ffn_all.items() if k in ('Wsh_up', 'Wsh_down', 'Wrt_up', 'Wrt_down', 'W_router')}
    del _L3_ffn_all
    return {'x': x, 'ctx_1024': ctx_1024, 'fside_BxSx2_0': fside_BxSx2_0, 'g_xattn': g_xattn, 'g_ffn': g_ffn, 'L0_xattn_Wq': _L0_xattn_in['Wq'], 'L0_xattn_bq': _L0_xattn_in['bq'], 'L0_xattn_Wk': _L0_xattn_in['Wk'], 'L0_xattn_bk': _L0_xattn_in['bk'], 'L0_xattn_Wv': _L0_xattn_in['Wv'], 'L0_xattn_bv': _L0_xattn_in['bv'], 'L0_xattn_Wkv_dca': _L0_xattn_in['Wkv_dca'], 'L0_xattn_bkv_dca': _L0_xattn_in['bkv_dca'], 'L0_xattn_qn_w': _L0_xattn_in['qn_w'], 'L0_xattn_qn_b': _L0_xattn_in['qn_b'], 'L0_xattn_kn_w': _L0_xattn_in['kn_w'], 'L0_xattn_kn_b': _L0_xattn_in['kn_b'], 'L0_xattn_kn_dca_w': _L0_xattn_in['kn_dca_w'], 'L0_xattn_kn_dca_b': _L0_xattn_in['kn_dca_b'], 'L0_xattn_Wo': _L0_xattn_in['Wo'], 'L0_xattn_bo': _L0_xattn_in['bo'], 'L0_ffn_up_weight': _L0_ffn_in['up_weight'], 'L0_ffn_down_weight': _L0_ffn_in['down_weight'], 'L0_ffn_up_scale': _L0_ffn_in['up_scale'], 'L0_ffn_down_scale': _L0_ffn_in['down_scale'], 'L0_ffn_output_scale': _L0_ffn_in['output_scale'], 'L1_xattn_Wq': _L1_xattn_in['Wq'], 'L1_xattn_bq': _L1_xattn_in['bq'], 'L1_xattn_Wk': _L1_xattn_in['Wk'], 'L1_xattn_bk': _L1_xattn_in['bk'], 'L1_ffn_weight': _L1_ffn_in['weight'], 'L1_ffn_w_scale': _L1_ffn_in['w_scale'], 'L1_ffn_bias': _L1_ffn_in['bias'], 'L2_xattn_in_proj_w': _L2_xattn_in['in_proj_w'], 'L2_xattn_conv_w': _L2_xattn_in['conv_w'], 'L2_xattn_conv_b': _L2_xattn_in['conv_b'], 'L2_xattn_x_proj_w': _L2_xattn_in['x_proj_w'], 'L2_xattn_dt_proj_w': _L2_xattn_in['dt_proj_w'], 'L2_xattn_dt_proj_b': _L2_xattn_in['dt_proj_b'], 'L2_xattn_A_log': _L2_xattn_in['A_log'], 'L2_xattn_D': _L2_xattn_in['D'], 'L2_ffn_gate_w': _L2_ffn_in['gate_w'], 'L2_ffn_w_gate': _L2_ffn_in['w_gate'], 'L2_ffn_w_up': _L2_ffn_in['w_up'], 'L2_ffn_w_down': _L2_ffn_in['w_down'], 'L3_xattn_Wq': _L3_xattn_in['Wq'], 'L3_xattn_Wkv': _L3_xattn_in['Wkv'], 'L3_xattn_Wout': _L3_xattn_in['Wout'], 'L3_xattn_bout': _L3_xattn_in['bout'], 'L3_ffn_Wsh_up': _L3_ffn_in['Wsh_up'], 'L3_ffn_Wsh_down': _L3_ffn_in['Wsh_down'], 'L3_ffn_Wrt_up': _L3_ffn_in['Wrt_up'], 'L3_ffn_Wrt_down': _L3_ffn_in['Wrt_down'], 'L3_ffn_W_router': _L3_ffn_in['W_router']}

def reference(x, ctx_1024, fside_BxSx2_0, g_xattn, g_ffn, L0_xattn_Wq, L0_xattn_bq, L0_xattn_Wk, L0_xattn_bk, L0_xattn_Wv, L0_xattn_bv, L0_xattn_Wkv_dca, L0_xattn_bkv_dca, L0_xattn_qn_w, L0_xattn_qn_b, L0_xattn_kn_w, L0_xattn_kn_b, L0_xattn_kn_dca_w, L0_xattn_kn_dca_b, L0_xattn_Wo, L0_xattn_bo, L0_ffn_up_weight, L0_ffn_down_weight, L0_ffn_up_scale, L0_ffn_down_scale, L0_ffn_output_scale, L1_xattn_Wq, L1_xattn_bq, L1_xattn_Wk, L1_xattn_bk, L1_ffn_weight, L1_ffn_w_scale, L1_ffn_bias, L2_xattn_in_proj_w, L2_xattn_conv_w, L2_xattn_conv_b, L2_xattn_x_proj_w, L2_xattn_dt_proj_w, L2_xattn_dt_proj_b, L2_xattn_A_log, L2_xattn_D, L2_ffn_gate_w, L2_ffn_w_gate, L2_ffn_w_up, L2_ffn_w_down, L3_xattn_Wq, L3_xattn_Wkv, L3_xattn_Wout, L3_xattn_bout, L3_ffn_Wsh_up, L3_ffn_Wsh_down, L3_ffn_Wrt_up, L3_ffn_Wrt_down, L3_ffn_W_router):
    import jax
    import jax.numpy as jnp

    def _L0_xattn_ref(x, y, Wq, bq, Wk, bk, Wv, bv, Wkv_dca, bkv_dca, qn_w, qn_b, kn_w, kn_b, kn_dca_w, kn_dca_b, Wo, bo):
        import jax, jax.numpy as jnp
        import numpy as np
        B, S1, S2, DCA = (2, 512, 256, 16)
        QDIM, KDIM, H = (512, 256, 16)
        HD = QDIM // H
        SCALE = HD ** (-0.5)
        EPS = 1e-06
        DCA_WEIGHT = 1.0

        def _ln(t, w, b):
            m = jnp.mean(t, axis=-1, keepdims=True)
            v = jnp.var(t, axis=-1, keepdims=True)
            return (t - m) * jax.lax.rsqrt(v + EPS) * w + b

        def _attn(q, k, v):
            s = jnp.einsum('bhqd,bhkd->bhqk', q, k) * SCALE
            p = jax.nn.softmax(s, axis=-1)
            return jnp.einsum('bhqk,bhkd->bhqd', p, v)
        b, s1, _ = x.shape
        y_dca = y[:, -DCA:, :]
        y_main = y[:, :-DCA, :]
        kv_dca = (y_dca @ Wkv_dca + bkv_dca).reshape(b, DCA, 2, H, HD)
        k_dca = _ln(kv_dca[:, :, 0], kn_dca_w, kn_dca_b)
        v_dca = kv_dca[:, :, 1]
        s2 = y_main.shape[1]
        q = _ln((x @ Wq + bq).reshape(b, s1, H, HD), qn_w, qn_b)
        kv = jnp.concatenate([y_main @ Wk + bk, y_main @ Wv + bv], axis=-1)
        kv = kv.reshape(b, s2, H, 2 * HD)
        k = _ln(kv[..., :HD], kn_w, kn_b)
        v = kv[..., HD:]
        qT = q.transpose(0, 2, 1, 3)
        ctx = _attn(qT, k.transpose(0, 2, 1, 3), v.transpose(0, 2, 1, 3))
        ctx = ctx.transpose(0, 2, 1, 3).reshape(b, s1, QDIM)
        ctx_dca = _attn(qT, k_dca.transpose(0, 2, 1, 3), v_dca.transpose(0, 2, 1, 3))
        ctx_dca = ctx_dca.transpose(0, 2, 1, 3).reshape(b, s1, QDIM)
        ctx = ctx + DCA_WEIGHT * ctx_dca
        return ctx @ Wo + bo

    def _L0_ffn_ref(x, up_weight, down_weight, up_scale, down_scale, output_scale):
        import jax, jax.numpy as jnp
        import numpy as np

        @jax.custom_vjp
        def ste_sign(x):
            return jnp.sign(x)

        def _ste_fwd(x):
            return (jnp.sign(x), None)

        def _ste_bwd(_, g):
            return (g,)
        ste_sign.defvjp(_ste_fwd, _ste_bwd)
        D_MODEL = 512
        D_HIDDEN = 2048
        up_w = ste_sign(up_weight)
        down_w = ste_sign(down_weight)
        hidden = jnp.einsum('bsd,hd->bsh', x, up_w) * up_scale
        hidden = jax.nn.relu(hidden)
        out = jnp.einsum('bsh,dh->bsd', hidden, down_w) * down_scale
        return out * output_scale

    def _L1_xattn_ref(teacher_logits, teacher_features, Wq, bq, Wk, bk):
        import jax, jax.numpy as jnp
        import numpy as np
        query = jnp.einsum('bnc,dc->bnd', teacher_features, Wq) + bq
        key = jnp.einsum('bnc,dc->bnd', teacher_features, Wk) + bk
        energy = jnp.einsum('bnd,bmd->bnm', query, key)
        attention = jax.nn.softmax(energy, axis=-1)
        x_m = jnp.einsum('bln,bmn->blm', teacher_logits, attention)
        return x_m

    def _L1_ffn_ref(x, weight, w_scale, bias):
        import jax, jax.numpy as jnp
        import numpy as np
        EPS = 1e-07

        def per_token_quant_int8(x, eps=EPS):
            absmax = jnp.max(jnp.abs(x), axis=-1, keepdims=True)
            scale = jnp.maximum(absmax, eps) / 127.0
            q = jnp.clip(jnp.round(x / scale), -128, 127).astype(jnp.int8)
            return (q, scale)
        q, in_scale = per_token_quant_int8(x)
        acc = jnp.einsum('bsk,nk->bsn', q, weight, preferred_element_type=jnp.int32)
        out = acc.astype(jnp.float32) * in_scale * w_scale[:, 0] + bias
        return out.astype(jnp.float16)

    def _L2_xattn_ref(hidden_states, z, in_proj_w, conv_w, conv_b, x_proj_w, dt_proj_w, dt_proj_b, A_log, D):
        import jax, jax.numpy as jnp
        import numpy as np
        import math
        B, L, DM = (2, 512, 256)
        DS, DC, EXP = (16, 4, 2)
        DI = EXP * DM
        DR = math.ceil(DM / 16)
        DT_MIN, DT_MAX, DT_FLOOR = (0.001, 0.1, 0.0001)

        def _ssm_forward(hidden_states, z, in_proj_w, conv_w, conv_b, x_proj_w, dt_proj_w, dt_proj_b, A_log, D):
            b = hidden_states.shape[0]
            x = jnp.einsum('ed,bld->bel', in_proj_w, hidden_states)
            xp = jnp.pad(x, ((0, 0), (0, 0), (DC - 1, 0)))
            xc = jax.lax.conv_general_dilated(xp, conv_w[:, None, :], window_strides=(1,), padding='VALID', dimension_numbers=('NCH', 'OIH', 'NCH'), feature_group_count=DI)
            u = jax.nn.silu(xc + conv_b[None, :, None])
            x_dbl = jnp.einsum('ke,bel->bkl', x_proj_w, u)
            dt_lo = x_dbl[:, :DR]
            Bm = x_dbl[:, DR:DR + DS]
            Cm = x_dbl[:, DR + DS:]
            delta = jax.nn.softplus(jnp.einsum('er,brl->bel', dt_proj_w, dt_lo) + dt_proj_b[None, :, None])
            A = -jnp.exp(A_log)

            def step(state, xs):
                d_t, B_t, C_t, u_t = xs
                dA = jnp.exp(d_t[..., None] * A)
                state = state * dA + (d_t * u_t)[..., None] * B_t[:, None, :]
                y_t = jnp.einsum('ben,bn->be', state, C_t)
                return (state, y_t)
            xs = (jnp.moveaxis(delta, -1, 0), jnp.moveaxis(Bm, -1, 0), jnp.moveaxis(Cm, -1, 0), jnp.moveaxis(u, -1, 0))
            state0 = jnp.zeros((b, DI, DS), delta.dtype)
            _, ys = jax.lax.scan(step, state0, xs)
            y = jnp.moveaxis(ys, 0, -1)
            y = y + D[None, :, None] * u
            y = y * jax.nn.silu(z)
            return jnp.swapaxes(y, 1, 2)
        return _ssm_forward(hidden_states, z, in_proj_w, conv_w, conv_b, x_proj_w, dt_proj_w, dt_proj_b, A_log, D)

    def _L2_ffn_ref(hidden_states, gate_w, w_gate, w_up, w_down):
        import jax, jax.numpy as jnp
        import numpy as np
        B, S, H = (4, 512, 512)
        I = 352
        E = 8
        K = 2
        b, s, h = hidden_states.shape
        x = hidden_states.reshape(-1, h)
        router_logits = x @ gate_w.T
        routing_weights = jax.nn.softmax(router_logits, axis=-1)
        topk_w, topk_i = jax.lax.top_k(routing_weights, K)
        topk_w = topk_w / jnp.sum(topk_w, axis=-1, keepdims=True)
        out = jnp.zeros_like(x)
        for e in range(w_gate.shape[0]):
            w_e = jnp.sum(jnp.where(topk_i == e, topk_w, 0.0), axis=-1)
            gated = jax.nn.silu(x @ w_gate[e]) * (x @ w_up[e])
            out = out + w_e[:, None] * (gated @ w_down[e])
        return out.reshape(b, s, h)

    def _L3_xattn_ref(x, ctx, pos_map, ctx_pos_map, Wq, Wkv, Wout, bout):
        import jax, jax.numpy as jnp
        import numpy as np
        DIM = 512
        CTX_DIM = 256
        N_HEADS = 32
        HEAD_DIM = DIM // N_HEADS
        POS_DIM = 2
        B, N, CTXN = (2, 512, 512)
        ROPE_BASE = 10000.0

        def apply_axial_rope(x, pos):
            b, n, h, d = x.shape
            p = pos.shape[-1]
            dpa = d // p
            half = dpa // 2
            freqs = ROPE_BASE ** (-jnp.arange(half, dtype=x.dtype) / half)
            ang = pos[..., :, None] * freqs
            cos = jnp.cos(ang)[:, :, None, :, :]
            sin = jnp.sin(ang)[:, :, None, :, :]
            xr = x.reshape(b, n, h, p, half, 2)
            x1, x2 = (xr[..., 0], xr[..., 1])
            out = jnp.stack([x1 * cos - x2 * sin, x1 * sin + x2 * cos], axis=-1)
            return out.reshape(b, n, h, d)
        b, n, _ = x.shape
        ctx_n = ctx.shape[1]
        q = (x @ Wq).reshape(b, n, N_HEADS, HEAD_DIM)
        k, v = jnp.split(ctx @ Wkv, 2, axis=-1)
        k = k.reshape(b, ctx_n, N_HEADS, HEAD_DIM)
        v = v.reshape(b, ctx_n, N_HEADS, HEAD_DIM)
        q = apply_axial_rope(q, pos_map)
        k = apply_axial_rope(k, ctx_pos_map)
        scale = 1.0 / np.sqrt(HEAD_DIM).astype(np.float32)
        logits = jnp.einsum('bqhd,bkhd->bhqk', q, k) * scale
        w = jax.nn.softmax(logits, axis=-1)
        attn = jnp.einsum('bhqk,bkhd->bqhd', w, v)
        attn = attn.reshape(b, n, N_HEADS * HEAD_DIM)
        return attn @ Wout + bout

    def _L3_ffn_ref(x, Wsh_up, Wsh_down, Wrt_up, Wrt_down, W_router):
        import jax, jax.numpy as jnp
        import numpy as np
        K_TOP = 2
        B, S, H = x.shape
        E_rt = Wrt_up.shape[0]
        xt = x.reshape(B * S, H)
        sh_mid = jax.nn.gelu(jnp.einsum('th,ehd->ted', xt, Wsh_up), approximate=False)
        shared_out = jnp.einsum('ted,edh->th', sh_mid, Wsh_down)
        probs = jax.nn.softmax(xt @ W_router, axis=-1)
        top_v, top_i = jax.lax.top_k(probs, K_TOP)
        gate = jnp.sum(jax.nn.one_hot(top_i, E_rt, dtype=xt.dtype) * top_v[..., None], axis=1)
        rt_mid = jax.nn.gelu(jnp.einsum('th,ehd->ted', xt, Wrt_up), approximate=False)
        routed_out = jnp.einsum('ted,edh->th', rt_mid * gate[:, :, None], Wrt_down)
        return (shared_out + routed_out).reshape(B, S, H)
    x = x + jnp.tanh(g_xattn[0]) * _L0_xattn_ref(_layernorm(x, axis=-1), ctx_1024, L0_xattn_Wq, L0_xattn_bq, L0_xattn_Wk, L0_xattn_bk, L0_xattn_Wv, L0_xattn_bv, L0_xattn_Wkv_dca, L0_xattn_bkv_dca, L0_xattn_qn_w, L0_xattn_qn_b, L0_xattn_kn_w, L0_xattn_kn_b, L0_xattn_kn_dca_w, L0_xattn_kn_dca_b, L0_xattn_Wo, L0_xattn_bo)
    x = x + jnp.tanh(g_ffn[0]) * _L0_ffn_ref(_layernorm(x, axis=-1), L0_ffn_up_weight, L0_ffn_down_weight, L0_ffn_up_scale, L0_ffn_down_scale, L0_ffn_output_scale)
    x = x + jnp.tanh(g_xattn[1]) * _L1_xattn_ref(_layernorm(x, axis=-1), ctx_1024, L1_xattn_Wq, L1_xattn_bq, L1_xattn_Wk, L1_xattn_bk)
    x = x + jnp.tanh(g_ffn[1]) * _L1_ffn_ref(_layernorm(x, axis=-1), L1_ffn_weight, L1_ffn_w_scale, L1_ffn_bias)
    x = x + jnp.tanh(g_xattn[2]) * _L2_xattn_ref(ctx_1024, _layernorm(x, axis=-1), L2_xattn_in_proj_w, L2_xattn_conv_w, L2_xattn_conv_b, L2_xattn_x_proj_w, L2_xattn_dt_proj_w, L2_xattn_dt_proj_b, L2_xattn_A_log, L2_xattn_D)
    x = x + jnp.tanh(g_ffn[2]) * _L2_ffn_ref(_layernorm(x, axis=-1), L2_ffn_gate_w, L2_ffn_w_gate, L2_ffn_w_up, L2_ffn_w_down)
    x = x + jnp.tanh(g_xattn[3]) * _L3_xattn_ref(_layernorm(x, axis=-1), ctx_1024, fside_BxSx2_0, fside_BxSx2_0, L3_xattn_Wq, L3_xattn_Wkv, L3_xattn_Wout, L3_xattn_bout)
    x = x + jnp.tanh(g_ffn[3]) * _L3_ffn_ref(_layernorm(x, axis=-1), L3_ffn_Wsh_up, L3_ffn_Wsh_down, L3_ffn_Wrt_up, L3_ffn_Wrt_down, L3_ffn_W_router)
    return x

_drawn_inputs = setup_inputs


def setup_inputs(seed=0):
    import zlib

    import numpy as np

    out = dict(_drawn_inputs(seed))
    spreads = {'L0_xattn_bq': (0.0, 0.1),
     'L0_xattn_bk': (0.0, 0.1),
     'L0_xattn_bv': (0.0, 0.1),
     'L0_xattn_bkv_dca': (0.0, 0.1),
     'L0_xattn_qn_w': (1.0, 0.2),
     'L0_xattn_qn_b': (0.0, 0.1),
     'L0_xattn_kn_w': (1.0, 0.2),
     'L0_xattn_kn_b': (0.0, 0.1),
     'L0_xattn_kn_dca_w': (1.0, 0.2),
     'L0_xattn_kn_dca_b': (0.0, 0.1),
     'L0_xattn_bo': (0.0, 0.1),
     'L0_ffn_up_scale': (1.0, 0.2),
     'L0_ffn_down_scale': (1.0, 0.2),
     'L1_xattn_bq': (0.0, 0.1),
     'L1_xattn_bk': (0.0, 0.1),
     'L2_xattn_conv_b': (0.0, 0.1),
     'L2_xattn_D': (1.0, 0.2),
     'L3_xattn_bout': (0.0, 0.1)}
    factors = {}
    for name, (base, spread) in spreads.items():
        noise = np.random.default_rng([zlib.crc32(name.encode()), seed]).standard_normal(out[name].shape)
        drawn = base * np.exp(spread * noise) if base else spread * noise
        out[name] = jnp.asarray(drawn.astype(out[name].dtype))
    for name, factor in factors.items():
        out[name] = (out[name] * factor).astype(out[name].dtype)
    return out
```

```python
from contextlib import ExitStack

import numpy as np

import concourse.bass as bass
from concourse import mybir

F32 = mybir.dt.float32
F16 = mybir.dt.float16
I8 = mybir.dt.int8
I32 = mybir.dt.int32
U32 = mybir.dt.uint32
ACT = mybir.ActivationFunctionType
ALU = mybir.AluOpType
AX = mybir.AxisListType

P = 128
B, S, D, C = 4, 512, 512, 256
T = B * S
NT = T // P
TPB = S // P
KD = D // P
KC = C // P

SY = 256.0
SC = 64.0
SW = 512.0


class Chain:

    def __init__(self, engine, sem, base=0):
        self.engine, self.sem, self.base, self.n = engine, sem, base, 0

    def link(self, instruction):
        self.n += 1
        instruction.then_inc(self.sem, 1)
        self.engine.wait_ge(self.sem, self.base + self.n)


class Env:

    def __init__(self, nc, stack, ins):
        self.nc, self.ins, self.stack, self.names = nc, ins, stack, 0
        self.sems, self.live = [], ExitStack()

    def sem(self, name):
        self.names += 1
        handle = self.live.enter_context(self.nc.semaphore(f"{name}_{self.names}"))
        self.sems.append(handle)
        return handle

    def recycle(self):
        sems = self.sems
        with self.nc.Block() as block:
            @block.gpsimd
            def _(pool):
                for s in sems:
                    pool.sem_clear(s)
        self.live.close()
        self.sems, self.live = [], ExitStack()

    def keep(self, name, shape, dt):
        return self.stack.enter_context(self.nc.sbuf_tensor(name, shape, dt))


def tiles_of(nc, ctx, tag):
    def sb(name, shape, dt=F32):
        return ctx.enter_context(nc.sbuf_tensor(f"{tag}_{name}", shape, dt))

    def ps(name, shape, dt=F32):
        return ctx.enter_context(nc.psum_tensor(f"{tag}_{name}", shape, dt))
    return sb, ps


def at(tile, t):
    return tile[:, bass.ds(t, 1), :].rearrange("p a d -> p (a d)")


def row_of(ap, n):
    return ap.rearrange("(a n) -> a n", a=1).to_broadcast([P, n])


def setup_block(nc, env):
    env.x = env.keep("x_res", [P, NT, D], F32)
    env.ctx_hi = env.keep("ctx_hi", [P, KC, T], F16)
    env.ctx_lo = env.keep("ctx_lo", [P, KC, T], F16)
    env.th = env.keep("tanh_gates", [P, 8], F32)
    env.id32 = env.keep("ident32", [P, P], F32)
    env.id16 = env.keep("ident16", [P, P], F16)
    env.eps5, env.eps6 = env.keep("eps5", [P, 1], F32), env.keep("eps6", [P, 1], F32)
    ins = env.ins
    with ExitStack() as ctx:
        sb, _ = tiles_of(nc, ctx, "su")
        ctx32 = sb("ctx32", [P, KC, T])
        graw = sb("graw", [P, 8])
        x_in, ctx_in, g_in = env.sem("x_in"), env.sem("ctx_in"), env.sem("gates_in")
        cleared, hi_done, done = env.sem("ident_cleared"), env.sem("ctx_hi_done"), env.sem("setup_done")
        block = ctx.enter_context(nc.Block())

        @block.sync
        def _(sp):
            sp.dma_start(ctx32[:], ins["ctx_t"].rearrange("(k p) t -> p k t", p=P)).then_inc(ctx_in, 16)
            sp.dma_start(graw[:, 0:4], row_of(ins["g_xattn"], 4)).then_inc(g_in, 16)
            sp.dma_start(graw[:, 4:8], row_of(ins["g_ffn"], 4)).then_inc(g_in, 16)
            sp.dma_start(env.x[:], ins["x"].rearrange("(t p) d -> p t d", p=P)).then_inc(x_in, 16)
            sp.wait_ge(x_in, 16)

        @block.gpsimd
        def _(pool):
            nc.gpsimd.memset(env.eps5[:], 1e-5).then_inc(done, 1)
            nc.gpsimd.memset(env.eps6[:], 1e-6).then_inc(done, 1)
            nc.gpsimd.memset(env.id32[:], 0.0).then_inc(cleared, 1)
            nc.gpsimd.memset(env.id16[:], 0.0).then_inc(cleared, 1)
            pool.wait_ge(cleared, 2)
            for m in (env.id32, env.id16):
                nc.gpsimd.affine_select(out=m[:], in_=m[:], compare_op=ALU.not_equal, fill=1.0, base=0,
                                        pattern=[[-1, P]], channel_multiplier=1).then_inc(done, 1)

        @block.scalar
        def _(act):
            act.wait_ge(g_in, 32)
            nc.scalar.activation(env.th[:], graw[:], ACT.Tanh).then_inc(done, 1)
            act.wait_ge(ctx_in, 16)
            nc.scalar.activation(env.ctx_hi[:], ctx32[:], ACT.Copy, scale=SC).then_inc(hi_done, 1)

        @block.vector
        def _(dve):
            dve.wait_ge(hi_done, 1)
            nc.vector.scalar_tensor_tensor(out=env.ctx_lo[:], in0=ctx32[:], scalar=SC, in1=env.ctx_hi[:],
                                           op0=ALU.mult, op1=ALU.subtract).then_inc(done, 1)
            dve.wait_ge(done, 6)


def norm_statistics(nc, dve, env, stats, agg, chain, ready):
    for t in range(NT):
        last = nc.vector.bn_stats(out=stats[:, t, :], in_=env.x[:, t, :])
    chain.link(last)
    for t in range(NT):
        last = nc.vector.bn_aggr(out=agg[:, t, :], in_=stats[:, t, :])
    last.then_inc(ready, 1)


def root(nc, out, var, eps, n):
    return nc.scalar.activation(out, var, ACT.Sqrt, bias=eps[0:n, :])


def norm_block(nc, env, y_hi, y_lo):
    with ExitStack() as ctx:
        env.count += 1
        sb, ps = tiles_of(nc, ctx, f"ln{env.count}")
        stats, agg, rstd = sb("stats", [P, NT, 6]), sb("agg", [P, NT, 2]), sb("rstd", [P, NT])
        y = sb("y", [P, 2, D])
        yt = [ps(f"yt{i}", [P, KD, P]) for i in range(2)]
        own, y_ready, t_ready = env.sem("ln_dve"), env.sem("y_ready"), env.sem("y_transposed")
        hi_ready, lo_ready = env.sem("y_hi_ready"), env.sem("y_lo_ready")
        root_done = env.sem("roots")
        var_ready = env.sem("variances")
        block = ctx.enter_context(nc.Block())

        @block.vector
        def _(dve):
            chain = Chain(dve, own)
            norm_statistics(nc, dve, env, stats, agg, chain, var_ready)
            dve.wait_ge(root_done, 1)
            chain.link(nc.vector.reciprocal(rstd[:], rstd[:]))

            def normalise(t, u):
                nc.vector.tensor_scalar(y[:, u, :], env.x[:, t, :], agg[:, t, 0:1],
                                        rstd[:, t:t + 1], ALU.subtract, ALU.mult).then_inc(y_ready, 1)

            def low_half(t, u):
                dve.wait_ge(hi_ready, t + 1)
                nc.vector.scalar_tensor_tensor(out=y_lo[:, :, t * P:(t + 1) * P], in0=yt[u][:], scalar=SY,
                                               in1=y_hi[:, :, t * P:(t + 1) * P], op0=ALU.mult,
                                               op1=ALU.subtract).then_inc(lo_ready, 1)
            for u in range(2):
                normalise(u, u)
            for t in range(0, NT - 2, 2):
                for u in range(2):
                    low_half(t + u, u)
                    normalise(t + u + 2, u)
            for u in range(2):
                low_half(NT - 2 + u, u)

        @block.tensor
        def _(pe):
            def transpose(t, u, reuse):
                pe.wait_ge(y_ready, t + 1)
                if reuse:
                    pe.wait_ge(lo_ready, t - 1)
                for k in range(KD):
                    last = nc.tensor.transpose(yt[u][:, k, :], y[:, u, k * P:(k + 1) * P], env.id32[:])
                last.then_inc(t_ready, 1)
            for u in range(2):
                transpose(u, u, False)
            for t in range(2, NT, 2):
                for u in range(2):
                    transpose(t + u, u, True)

        @block.scalar
        def _(act):
            act.wait_ge(var_ready, 1)
            root(nc, rstd[:], agg[:, :, 1], env.eps5, P).then_inc(root_done, 1)
            for t in range(0, NT, 2):
                for u in range(2):
                    act.wait_ge(t_ready, t + u + 1)
                    nc.scalar.activation(y_hi[:, :, (t + u) * P:(t + u + 1) * P], yt[u][:], ACT.Copy,
                                         scale=SY).then_inc(hi_ready, 1)


def router_block(nc, env, y_hi, y_lo, w_router, n_exp, shared, coef, th, down_scale, renorm):
    with ExitStack() as ctx:
        env.count += 1
        sb, ps = tiles_of(nc, ctx, f"rt{env.count}")
        w32, w_hi, w_lo = sb("w32", [P, KD, n_exp]), sb("wh", [P, KD, n_exp], F16), sb("wl", [P, KD, n_exp], F16)
        logit, prob = sb("logit", [P, NT, n_exp]), sb("prob", [P, NT, n_exp])
        red, inv = sb("red", [P, NT]), sb("inv", [P, NT])
        top, idx, idxf = sb("top", [P, NT, 8]), sb("idx", [P, NT, 8], U32), sb("idxf", [P, NT, 2])
        ramp, rampi = sb("ramp", [P, n_exp]), sb("rampi", [P, n_exp], I32)
        hot, hot2, tops = sb("hot", [P, NT, n_exp]), sb("hot2", [P, NT, n_exp]), sb("tops", [P, NT, 2])
        cs = sb("cs", [P, 1])
        pl = ps("logits", [P, NT, n_exp])
        w_in, hi_done, w_done = env.sem("router_in"), env.sem("router_hi"), env.sem("router_split")
        ramp_done, logit_done = env.sem("ramp"), env.sem("logits")
        shifted, exped, own = env.sem("logits_shifted"), env.sem("logits_exp"), env.sem("router_dve")
        block = ctx.enter_context(nc.Block())

        def over_e(v):
            return v.unsqueeze(2).to_broadcast([P, NT, n_exp])

        @block.sync
        def _(sp):
            sp.dma_start(w32[:], w_router.rearrange("(k p) e -> p k e", p=P)).then_inc(w_in, 16)

        @block.gpsimd
        def _(pool):
            nc.gpsimd.iota(rampi[:], pattern=[[1, n_exp]], base=0, channel_multiplier=0).then_inc(ramp_done, 1)

        @block.scalar
        def _(act):
            act.wait_ge(w_in, 16)
            nc.scalar.activation(w_hi[:], w32[:], ACT.Copy, scale=SW).then_inc(hi_done, 1)
            act.wait_ge(shifted, 1)
            nc.scalar.activation(prob[:], logit[:], ACT.Exp).then_inc(exped, 1)

        @block.tensor
        def _(pe):
            pe.wait_ge(w_done, 1)
            for t in range(NT):
                n = 0
                for yy, ww in ((y_hi, w_hi), (y_hi, w_lo), (y_lo, w_hi)):
                    for k in range(KD):
                        last = nc.tensor.matmul(pl[:, t, :], yy[:, k, t * P:(t + 1) * P], ww[:, k, :],
                                                start=(n == 0), stop=(n == 3 * KD - 1))
                        n += 1
            last.then_inc(logit_done, 1)

        @block.vector
        def _(dve):
            c = Chain(dve, own)
            dve.wait_ge(hi_done, 1)
            nc.vector.scalar_tensor_tensor(out=w_lo[:], in0=w32[:], scalar=SW, in1=w_hi[:], op0=ALU.mult,
                                           op1=ALU.subtract).then_inc(w_done, 1)
            dve.wait_ge(ramp_done, 1)
            c.link(nc.vector.tensor_copy(ramp[:], rampi[:]))
            c.link(nc.vector.tensor_scalar(cs[:], th, down_scale, None, ALU.mult))
            dve.wait_ge(logit_done, 1)
            c.link(nc.vector.tensor_scalar(logit[:], pl[:], 1.0 / (SY * SW), None, ALU.mult))
            c.link(nc.vector.tensor_reduce(red[:], logit[:], AX.X, ALU.max))
            nc.vector.tensor_tensor(logit[:], logit[:], over_e(red[:]), ALU.subtract).then_inc(shifted, 1)
            dve.wait_ge(exped, 1)
            c.link(nc.vector.tensor_reduce(red[:], prob[:], AX.X, ALU.add))
            c.link(nc.vector.reciprocal(inv[:], red[:]))
            c.link(nc.vector.tensor_tensor(prob[:], prob[:], over_e(inv[:]), ALU.mult))
            for t in range(NT):
                last = nc.vector.max(top[:, t, :], prob[:, t, :])
            c.link(last)
            for t in range(NT):
                last = nc.vector.max_index(idx[:, t, :], top[:, t, :], prob[:, t, :])
            c.link(last)
            c.link(nc.vector.tensor_copy(idxf[:], idx[:, :, 0:2]))
            if renorm:
                c.link(nc.vector.tensor_tensor(red[:], top[:, :, 0], top[:, :, 1], ALU.add))
                c.link(nc.vector.reciprocal(inv[:], red[:]))
                for j in range(2):
                    last = nc.vector.tensor_tensor(tops[:, :, j], top[:, :, j], inv[:], ALU.mult)
                    c.link(last)
            else:
                c.link(nc.vector.tensor_copy(tops[:], top[:, :, 0:2]))
            c.link(nc.vector.tensor_scalar(tops[:], tops[:], cs[:], None, ALU.mult))
            for j, h in enumerate((hot, hot2)):
                c.link(nc.vector.tensor_tensor(h[:], ramp[:].unsqueeze(1).to_broadcast([P, NT, n_exp]),
                                               over_e(idxf[:, :, j]), ALU.is_equal))
                c.link(nc.vector.tensor_tensor(h[:], h[:], over_e(tops[:, :, j]), ALU.mult))
            c.link(nc.vector.tensor_tensor(coef[:, :, shared:], hot[:], hot2[:], ALU.add))
            if shared:
                c.link(nc.vector.memset(coef[:, :, 0:shared], 1.0))
                c.link(nc.vector.tensor_scalar(coef[:, :, 0:shared], coef[:, :, 0:shared], cs[:], None, ALU.mult))


def experts_block(nc, env, y_hi, y_lo, w_up, w_down, kind, n_exp, inner, coef, finish):
    gated, binary = kind == "silu", kind == "sign"
    n_up = 2 if gated else 1
    chunks = [min(P, inner - i) for i in range(0, inner, P)]
    NC = len(chunks)
    parts = 1 if binary else 2
    smid = {"silu": 64.0, "gelu": 256.0, "sign": 4.0}[kind]
    s_up = 1.0 / SY if binary else 1.0 / (SY * SW)
    TB = T // 512
    with ExitStack() as ctx:
        env.count += 1
        sb, ps = tiles_of(nc, ctx, f"ex{env.count}")
        acc = sb("acc", [P, NT, D])
        up32, dn32 = sb("up32", [P, n_up, KD, inner]), sb("dn32", [P, NC, D])
        up16 = [[sb(f"up16_{w}{h}", [P, n_up, KD, inner], F16) for h in range(parts)] for w in range(2)]
        dn16 = [[sb(f"dn16_{w}{h}", [P, NC, D], F16) for h in range(parts)] for w in range(2)]
        mid = sb("mid", [P, 2, 512])
        sil = sb("sil", [P, 2, 512]) if gated else None
        mid_h, mid_l = sb("midh", [P, 2, NC, 512], F16), sb("midl", [P, 2, NC, 512], F16)
        if binary:
            ups = sb("ups", [P, n_exp * NC])
            ups_now = sb("ups_now", [P, 2, NC])
            dsr = sb("dsr", [P, D])
            osc = sb("osc", [P, 1])
        pu = [[ps(f"pu{i}{j}", [P, 512]) for j in range(n_up)] for i in range(2)]
        po = [ps(f"po{i}", [P, D]) for i in range(2)]
        w_in, w_read = env.sem("w_in"), env.sem("w_split")
        w_hi, scales_in, acc0 = env.sem("w_hi"), env.sem("scales_in"), env.sem("acc_cleared")
        up_done, mid_done, hi_done = env.sem("up_done"), env.sem("mid_done"), env.sem("mid_hi_done")
        sil_done, lo_done = env.sem("silu_done"), env.sem("mid_lo_done")
        dn_done, acc_done, own = env.sem("down_done"), env.sem("acc_done"), env.sem("expert_dve")
        block = ctx.enter_context(nc.Block())
        EPI = 2
        SPE = TB
        passes = [(0, 0), (1, 0)] if binary else [(0, 0), (1, 0), (0, 1)]
        n_dma = n_up + 1

        @block.sync
        def _(sp):
            if binary:
                sp.dma_start(ups[:], env.ins["up_scale_t"]).then_inc(scales_in, 16)
                sp.dma_start(dsr[:], row_of(env.ins["down_scale"], D)).then_inc(scales_in, 16)
                sp.dma_start(osc[:], row_of(env.ins["output_scale"], 1)).then_inc(scales_in, 16)

            def load(e, first):
                if not first:
                    sp.wait_ge(w_read, 2 * e)
                for j in range(n_up):
                    sp.dma_start(up32[:, j, :, :], w_up[j][bass.ds(e, 1), :, :].rearrange("e (k p) i -> p (e k) i", p=P)
                                 ).then_inc(w_in, 16)
                full = inner // P
                src = w_down[bass.ds(e, 1), 0:full * P, :].rearrange("e (c p) n -> p (e c) n", p=P)
                sp.dma_start(dn32[:, 0:full, :], src).then_inc(w_in, 16)
                if inner % P:
                    src = w_down[bass.ds(e, 1), full * P:inner, :].rearrange("e p n -> p (e n)")
                    sp.dma_start(dn32[0:inner % P, full, :], src).then_inc(w_in, 16)
            load(0, True)
            with sp.Fori(1, n_exp) as e:
                load(e, False)
        if inner % P:
            n_dma += 1

        def pieces(up, dn):
            full = inner // P
            out = [(up[:], 0), (dn[:, 0:full, :], 1)]
            if inner % P:
                out.append((dn[0:inner % P, full, :], 1))
            return [o for o, _ in out]

        @block.gpsimd
        def _(pool):
            nc.gpsimd.memset(acc[:], 0.0).then_inc(acc0, 1)

        @block.scalar
        def _(act):
            def split_hi(e, w, reuse):
                act.wait_ge(w_in, 16 * n_dma * (e + 1))
                if reuse:
                    act.wait_ge(dn_done, TPB * SPE * (e - 1))
                src, dst = pieces(up32, dn32), pieces(up16[w][0], dn16[w][0])
                for s, d in zip(src, dst):
                    if binary:
                        nc.scalar.activation(d, s, ACT.Sign).then_inc(w_hi, 1)
                    else:
                        nc.scalar.activation(d, s, ACT.Copy, scale=SW).then_inc(w_hi, 1)

            def chunk(e, w, tb, c, q, first):
                n = chunks[c]
                s = e * SPE + tb
                g = s * NC + c
                act.wait_ge(up_done, g + 1)
                if gated:
                    if not (first and tb == 0 and c < 2):
                        act.wait_ge(mid_done, g - 1)
                    nc.scalar.activation(sil[0:n, q, :], pu[q][0][0:n, :], ACT.Silu, scale=s_up).then_inc(sil_done, 1)
                    act.wait_ge(mid_done, g + 1)
                else:
                    if not (first and tb == 0 and c < 2):
                        act.wait_ge(lo_done, g - 1)
                    if binary:
                        ins = nc.scalar.activation(mid[0:n, q, :], pu[q][0][0:n, :], ACT.Relu,
                                                   scale=ups_now[0:n, w, c:c + 1])
                    else:
                        ins = nc.scalar.activation(mid[0:n, q, :], pu[q][0][0:n, :], ACT.Gelu, scale=s_up)
                    ins.then_inc(mid_done, 1)
                    act.wait_ge(mid_done, g + 1)
                if not (first and tb < 2):
                    act.wait_ge(dn_done, TPB * (s - 1))
                nc.scalar.activation(mid_h[0:n, tb % 2, c, :], mid[0:n, q, :], ACT.Copy,
                                     scale=smid).then_inc(hi_done, 1)

            def expert(e, w, first, ahead, reuse_next):
                if binary:
                    act.wait_ge(w_read, 2 * (e + 1))
                for tb in range(TB):
                    if tb == 1 and ahead:
                        split_hi(e + 1, 1 - w, reuse_next)
                    for c in range(NC):
                        chunk(e, w, tb, c, (tb * NC + c) % 2, first)
            split_hi(0, 0, False)
            expert(0, 0, True, True, False)
            expert(1, 1, False, True, True)
            with act.Fori(1, n_exp // EPI - 1) as i:
                e = i * EPI
                expert(e, 0, False, True, True)
                expert(e + 1, 1, False, True, True)
            expert(n_exp - 2, 0, False, True, True)
            expert(n_exp - 1, 1, False, False, True)

        @block.tensor
        def _(pe):
            def up(e, w, tb, first):
                s = e * SPE + tb
                for c, n in enumerate(chunks):
                    q = (tb * NC + c) % 2
                    g = s * NC + c
                    if not (first and tb == 0 and c < 2):
                        pe.wait_ge(mid_done, g - 1)
                    for j in range(n_up):
                        i = 0
                        for a, h in passes:
                            for k in range(KD):
                                last = nc.tensor.matmul(
                                    pu[q][j][0:n, :], up16[w][h][:, j, k, c * P:c * P + n],
                                    (y_hi, y_lo)[a][:, k, tb * 512:(tb + 1) * 512],
                                    start=(i == 0), stop=(i == len(passes) * KD - 1))
                                i += 1
                    last.then_inc(up_done, 1)

            def down(e, w, tb, first):
                s = e * SPE + tb
                pe.wait_ge(lo_done, NC * (s + 1))
                for j in range(TPB):
                    r = s * TPB + j
                    if not (first and tb == 0 and j < 2):
                        pe.wait_ge(acc_done, r - 1)
                    i = 0
                    for c, n in enumerate(chunks):
                        for a, h in passes:
                            last = nc.tensor.matmul(po[j % 2][:], (mid_h, mid_l)[a][0:n, tb % 2, c, j * P:(j + 1) * P],
                                                    dn16[w][h][0:n, c, :], start=(i == 0),
                                                    stop=(i == len(passes) * NC - 1))
                            i += 1
                    last.then_inc(dn_done, 1)

            def expert(e, w, first):
                pe.wait_ge(w_read, 2 * (e + 1))
                for tb in range(TB):
                    up(e, w, tb, first)
                    if tb:
                        down(e, w, tb - 1, first)
                down(e, w, TB - 1, first)
            expert(0, 0, True)
            expert(1, 1, False)
            with pe.Fori(1, n_exp // EPI) as i:
                e = i * EPI
                expert(e, 0, False)
                expert(e + 1, 1, False)

        @block.vector
        def _(dve):
            n_lo = len(pieces(up32, dn32))
            ch = Chain(dve, own)
            if binary:
                dve.wait_ge(scales_in, 48)
                ch.link(nc.vector.tensor_scalar(ups[:], ups[:], s_up, None, ALU.mult))
                ch.link(nc.vector.tensor_scalar(osc[:], osc[:], coef, None, ALU.mult))
                ch.link(nc.vector.tensor_scalar(dsr[:], dsr[:], osc[:], 1.0 / smid, ALU.mult, ALU.mult))

            def split_lo(e, w):
                dve.wait_ge(w_hi, n_lo * (e + 1))
                if binary:
                    nc.vector.tensor_scalar(ups_now[:, w, :], ups[:, bass.ds(e * NC, NC)], 1.0, None,
                                            ALU.mult).then_inc(w_read, 2)
                    return
                src, his = pieces(up32, dn32), pieces(up16[w][0], dn16[w][0])
                for n, (s, h, d) in enumerate(zip(src, his, pieces(up16[w][1], dn16[w][1]))):
                    last = nc.vector.scalar_tensor_tensor(out=d, in0=s, scalar=SW, in1=h, op0=ALU.mult,
                                                          op1=ALU.subtract)
                last.then_inc(w_read, 2)

            def chunk(e, tb, c):
                n = chunks[c]
                q = (tb * NC + c) % 2
                g = (e * SPE + tb) * NC + c
                if gated:
                    dve.wait_ge(sil_done, g + 1)
                    nc.vector.scalar_tensor_tensor(out=mid[0:n, q, :], in0=pu[q][1][0:n, :], scalar=s_up,
                                                   in1=sil[0:n, q, :], op0=ALU.mult, op1=ALU.mult
                                                   ).then_inc(mid_done, 1)
                dve.wait_ge(hi_done, g + 1)
                nc.vector.scalar_tensor_tensor(out=mid_l[0:n, tb % 2, c, :], in0=mid[0:n, q, :], scalar=smid,
                                               in1=mid_h[0:n, tb % 2, c, :], op0=ALU.mult,
                                               op1=ALU.subtract).then_inc(lo_done, 1)

            def add(e, tb):
                for j in range(TPB):
                    t = tb * TPB + j
                    r = (e * SPE + tb) * TPB + j
                    dve.wait_ge(dn_done, r + 1)
                    scale = 1.0 if binary else coef[:, t, bass.ds(e, 1)]
                    nc.vector.scalar_tensor_tensor(out=acc[:, t, :], in0=po[j % 2][:], scalar=scale,
                                                   in1=acc[:, t, :], op0=ALU.mult, op1=ALU.add
                                                   ).then_inc(acc_done, 1)

            def expert(e, w, ahead):
                for tb in range(TB):
                    for c in range(NC):
                        chunk(e, tb, c)
                    if tb == 1 and ahead:
                        split_lo(e + 1, 1 - w)
                    if tb:
                        add(e, tb - 1)
                add(e, TB - 1)
            split_lo(0, 0)
            dve.wait_ge(acc0, 1)
            with dve.Fori(0, n_exp // EPI - 1) as i:
                e = i * EPI
                expert(e, 0, True)
                expert(e + 1, 1, True)
            expert(n_exp - 2, 0, True)
            expert(n_exp - 1, 1, False)
            dve.wait_ge(acc_done, n_exp * NT)
            with dve.Fori(0, NT) as t:
                if binary:
                    nc.vector.tensor_tensor(at(acc, t), at(acc, t), dsr[:], ALU.mult).then_inc(own, 1)
            if binary:
                dve.wait_ge(own, 3 + NT)
            with dve.Fori(0, NT) as t:
                nc.vector.tensor_tensor(at(env.x, t), at(env.x, t), at(acc, t), ALU.add)


def layer_ffn(nc, env, index):
    ins = env.ins
    with ExitStack() as ctx:
        env.count += 1
        y_hi = ctx.enter_context(nc.sbuf_tensor(f"y_hi{env.count}", [P, KD, T], F16))
        y_lo = ctx.enter_context(nc.sbuf_tensor(f"y_lo{env.count}", [P, KD, T], F16))
        norm_block(nc, env, y_hi, y_lo)
        th = env.th[:, 4 + index:5 + index]
        if index == 0:
            experts_block(nc, env, y_hi, y_lo, [ins["up_weight_t"]], ins["down_weight_t"], "sign",
                          8, 256, th, None)
            return
        n_exp, shared = (8, 0) if index == 2 else (18, 2)
        coef = ctx.enter_context(nc.sbuf_tensor(f"coef{env.count}", [P, NT, n_exp], F32))
        smid = 64.0 if index == 2 else 256.0
        router = ins["gate_w_t"] if index == 2 else ins["W_router"]
        router_block(nc, env, y_hi, y_lo, router, n_exp - shared, shared, coef, th, 1.0 / (smid * SW), index == 2)
        if index == 2:
            experts_block(nc, env, y_hi, y_lo, [ins["w_gate"], ins["w_up"]], ins["w_down"], "silu",
                          8, 352, coef, None)
        else:
            experts_block(nc, env, y_hi, y_lo, [ins["exp_up"]], ins["exp_down"], "gelu", 18, 256, coef, None)


def split_weights_block(nc, env, jobs):
    with ExitStack() as ctx:
        env.count += 1
        sb, _ = tiles_of(nc, ctx, f"sw{env.count}")
        stage = sb("stage", [P, 2, KD, D])
        mean = sb("mean", [P, KD, D // 16])
        w_in = [env.sem("stage_in0"), env.sem("stage_in1")]
        ready, hi_done, lo_done, own = env.sem("w_centred"), env.sem("w_hi"), env.sem("w_lo"), env.sem("split_dve")
        block = ctx.enter_context(nc.Block())

        @block.sync
        def _(sp):
            for n, (w, hi, lo, _) in enumerate(jobs):
                if n >= 2:
                    sp.wait_ge(lo_done, n - 1)
                sp.dma_start(stage[:, n % 2, 0:hi.shape[1], :], w.rearrange("(k p) n -> p k n", p=P)
                             ).then_inc(w_in[n % 2], 16)

        @block.scalar
        def _(act):
            for n, (w, hi, lo, _) in enumerate(jobs):
                act.wait_ge(ready, n + 1)
                nc.scalar.activation(hi[:], stage[:, n % 2, 0:hi.shape[1], :], ACT.Copy,
                                     scale=SW).then_inc(hi_done, 1)

        @block.vector
        def _(dve):
            ch = Chain(dve, own)
            for n, (w, hi, lo, hd) in enumerate(jobs):
                kk = hi.shape[1]
                st = stage[:, n % 2, 0:kk, :]
                dve.wait_ge(w_in[n % 2], 16 * (n // 2 + 1))
                if hd:
                    nh = D // hd
                    for k in range(kk):
                        s4 = stage[:, n % 2, k, :].rearrange("p (h d) -> p h d", d=hd)
                        ch.link(nc.vector.tensor_reduce(mean[:, k, 0:nh], s4, AX.X, ALU.add))
                        ch.link(nc.vector.tensor_scalar(mean[:, k, 0:nh], mean[:, k, 0:nh], 1.0 / hd, None, ALU.mult))
                        ch.link(nc.vector.tensor_tensor(s4, s4, mean[:, k, 0:nh].unsqueeze(2).to_broadcast([P, nh, hd]),
                                                        ALU.subtract))
                dve.sem_inc(ready, 1)
                dve.wait_ge(hi_done, n + 1)
                nc.vector.scalar_tensor_tensor(out=lo[:], in0=st, scalar=SW, in1=hi[:], op0=ALU.mult,
                                               op1=ALU.subtract).then_inc(lo_done, 1)


def attention_block(nc, env, w, th, rope):
    H, HD = (32, 16) if rope else (16, 32)
    SK = 2048 // H
    VC = 1024 // H
    GH = P // VC
    NG, NP = H // GH, GH // 2
    DCA = 0 if rope else 16
    MAIN = S - DCA
    TAIL = P - DCA
    SQK, SM, SA = 64.0, 256.0, 64.0
    SCALE = float(HD) ** -0.5
    NPROJ = 3 * TPB + (0 if rope else 1)
    NCH = 2048 // P
    with ExitStack() as ctx:
        env.count += 1
        sb, ps = tiles_of(nc, ctx, f"at{env.count}")
        thc, bo = sb("thc", [P, 1]), sb("bo", [P, D])
        if rope:
            ang, cosr, sinr = sb("ang", [P, NT, 2]), sb("cosr", [P, NT, 8]), sb("sinr", [P, NT, 8])
            half_pi = sb("half_pi", [P, 1])
        else:
            bq, bk, bkt = sb("bq", [P, D]), sb("bk", [P, D]), sb("bkt", [P, D])
            bv, bvt, bvd = sb("bv", [P, D]), sb("bvt", [P, D]), sb("bvd", [P, D])
            qwb, kwb, kdwb = sb("qwb", [P, 2, HD]), sb("kwb", [P, 2, HD]), sb("kdwb", [P, 2, HD])
            bmean = sb("bmean", [P, H])
            mask = sb("mask", [P, 2])
        stats, agg, rstd = sb("stats", [P, NT, 6]), sb("agg", [P, NT, 2]), sb("rstd", [P, NT])
        y_h, y_l = sb("yh", [P, KD, P], F16), sb("yl", [P, KD, P], F16)
        c_h, c_l = sb("ch", [P, KC, S], F16), sb("cl", [P, KC, S], F16)
        if not rope:
            cm = [sb(f"cm{i}", [P, KC, P], F16) for i in range(2)]
            cd = [sb(f"cd{i}", [P, KC, P], F16) for i in range(2)]
        ss = sb("ss", [P, H])
        stq = sb("stq", [P, TPB, 2048], F16)
        stk = [sb(f"stk{i}", [P, 2048], F16) for i in range(1 if rope else 2)]
        QT = sb("QT", [P, NCH, S], F16)
        KT = sb("KT", [P, H, S], F16)
        V = sb("V", [P, TPB, H, VC])
        Vd = None if rope else sb("Vd", [P, H, VC])
        nmax = sb("nmax", [P, TPB, H, 1 if rope else 2])
        PTB = 3
        PT = sb("PT", [P, PTB, 2, S])
        y, sq, rot = PT[:, 0, 0, :], PT[:, 1, 0, :], PT[:, 1, 1, :]
        q2 = [PT[:, 0, 1, :], PT[:, 2, 0, :]]
        oT = sb("oT", [P, 1 if rope else 2, S])
        rec = sb("rec", [P, TPB, GH, 2])
        A, tmp = sb("A", [P, TPB, D]), (None if rope else sb("tmp", [P, TPB, GH, HD]))
        a16 = [PT[:, i, 0, :].bitcast(F16).rearrange("p (h k q) -> p h k q", h=2, q=P) for i in range(2)]
        psS = ps("S", [P, 4, 512])
        psB = psS[:, 2:4, :].bitcast(F16).rearrange("p b (c q) -> p (b c) q", q=P)
        psM = ps("M", [P, 2 if rope else 1, 512])
        psG = psM[:, 0, :].bitcast(F16).rearrange("p (c s) -> p c s", c=2)
        po = ps("o", [P, S])
        pd = None if rope else ps("od", [P, S])
        pt = ps("t", [P, 4, P])
        psN = [psM[:, 0, :], psM[:, 1, :] if rope else pt[:].rearrange("p j q -> p (j q)")]
        psP = [psS[:, 0, :], psS[:, 1, :], po[:]]

        sem = env.sem
        const_in, const_done, own = sem("const_in"), sem("const_done"), sem("attn_dve")
        var_ready, root_done, angles, trig = sem("variances"), sem("roots"), sem("angles"), sem("trig")
        zeroed, batch_in = sem("zeroed"), sem("batch_ctx")
        y_ready, yt_done, yh_done, yl_done = sem("y_ready"), sem("y_T"), sem("y_hi"), sem("y_lo")
        proj_done, proj_read = sem("proj_done"), sem("proj_read")
        c_done, ss_done, rt_done = sem("centred"), sem("sumsq"), sem("qk_roots")
        sq_done = sem("squares")
        low_begun = sem("qk_lo_begun")
        q_final, qh_done, st_ready, st_T, st_ev = sem("qk_final"), sem("qk_hi"), sem("stack"), sem("stack_T"), sem("stack_ev")
        s_done, max_done, m_ready = sem("scores"), sem("maxima"), sem("max_rows")
        sT_done, exp_done, pv_done = sem("scoresT"), sem("exp"), sem("pv")
        o_done, oT_done, ot_T, a_done = sem("group_out"), sem("group_ev"), sem("group_T"), sem("attn_norm")
        at_T, ah_done, al_done, wo_done, x_done = sem("attn_T"), sem("attn_hi"), sem("attn_lo"), sem("wo"), sem("x_done")
        block = ctx.enter_context(nc.Block())
        ins = env.ins
        units = [(g, kt, p) for g in range(NG) for kt in range(TPB) for p in range(NP)]
        NU, UPG = len(units), TPB * NP
        NM = H * TPB
        NMG = GH * TPB
        SPU = NM // NU
        AHEAD = NMG + 2 * SPU
        ROWS = UPG - 2
        NST = 8 + NG
        NOUT = 1 if rope else 2
        n_const = 1 + (1 if rope else 12)
        items = [(j, kind) for j in range(TPB) for kind in "qkv"]
        qk = [(j, kind) for j, kind in items if kind != "v"]

        def heads(tile):
            return tile.rearrange("p (h d) -> p h d", d=HD)

        def stack_of(j, kind):
            if kind == "q":
                return stq[:, j, :]
            return stk[0 if rope or j < TPB - 1 else 1][:]

        @block.sync
        def _(sp):
            sp.dma_start(bo[:], row_of(w["bo"], D)).then_inc(const_in, 16)
            if rope:
                sp.dma_start(ang[:], ins["fside"].rearrange("(t p) a -> p t a", p=P)).then_inc(const_in, 16)
            else:
                for tile, name in ((bq, "bq0"), (bk, "bk0"), (bkt, "bkd0"), (bv, "bv0"), (bvd, "bvd0"), (bvt, "bv0")):
                    sp.dma_start(tile[:], row_of(ins[name], D)).then_inc(const_in, 16)
                for tile, n in ((qwb, "qn"), (kwb, "kn"), (kdwb, "kd")):
                    sp.dma_start(tile[:, 0, :], row_of(ins[n + "_w"], HD)).then_inc(const_in, 16)
                    sp.dma_start(tile[:, 1, :], row_of(ins[n + "_b"], HD)).then_inc(const_in, 16)

        @block.gpsimd
        def _(pool):
            ch = Chain(pool, zeroed)
            nc.gpsimd.memset(stq[:], 0.0).then_inc(zeroed, 1)
            for s in stk:
                nc.gpsimd.memset(s[:], 0.0).then_inc(zeroed, 1)
            nc.gpsimd.memset(V[:], 0.0).then_inc(zeroed, 1)
            n = 2 + len(stk)
            if rope:
                nc.gpsimd.memset(KT[:], 0.0).then_inc(zeroed, 1)
                nc.gpsimd.memset(half_pi[:], float(np.pi / 2)).then_inc(zeroed, 1)
                pool.wait_ge(zeroed, n + 2)
                n += 2
                nc.gpsimd.memset(V[:, :, :, HD:HD + 1], 1.0).then_inc(zeroed, 1)
                nc.gpsimd.memset(stk[0][:].rearrange("p (h s) -> p h s", s=SK)[:, :, 3 * HD:3 * HD + 1],
                                 SM).then_inc(zeroed, 1)
                n += 2
            else:
                nc.gpsimd.memset(Vd[:], 0.0).then_inc(zeroed, 1)
                nc.gpsimd.memset(mask[:], 1.0).then_inc(zeroed, 1)
                for tile in cm + cd:
                    nc.gpsimd.memset(tile[:], 0.0).then_inc(zeroed, 1)
                n += 6
                pool.wait_ge(zeroed, n)
                nc.gpsimd.affine_select(out=mask[:, 0:1], in_=mask[:, 0:1], compare_op=ALU.is_ge, fill=0.0,
                                        base=TAIL - 1, pattern=[[0, 1]], channel_multiplier=-1).then_inc(zeroed, 1)
                nc.gpsimd.affine_select(out=mask[:, 1:2], in_=mask[:, 1:2], compare_op=ALU.is_ge, fill=0.0,
                                        base=-TAIL, pattern=[[0, 1]], channel_multiplier=1).then_inc(zeroed, 1)
                nc.gpsimd.memset(V[:, 0:TPB - 1, :, HD:HD + 1], 1.0).then_inc(zeroed, 1)
                sv = [s[:].rearrange("p (h s) -> p h s", s=SK) for s in stk]
                nc.gpsimd.memset(sv[0][:, :, 3 * HD:3 * HD + 1], SM).then_inc(zeroed, 1)
                n += 4
                pool.wait_ge(zeroed, n)
                one = mask[:, 0:1].unsqueeze(2).to_broadcast([P, H, 1])
                oned = mask[:, 1:2].unsqueeze(2).to_broadcast([P, H, 1])
                nc.gpsimd.tensor_copy(V[:, TPB - 1, :, HD:HD + 1], one).then_inc(zeroed, 1)
                nc.gpsimd.tensor_copy(Vd[:, :, HD:HD + 1], oned).then_inc(zeroed, 1)
                for i in range(2):
                    nc.gpsimd.tensor_scalar(sv[1][:, :, 3 * HD + i:3 * HD + i + 1], (one, oned)[i], SM, None,
                                            ALU.mult).then_inc(zeroed, 1)
                n += 4
            pool.wait_ge(zeroed, n)
            with pool.Fori(0, B) as b:
                nc.gpsimd.memset(stq[:].rearrange("p j (h s) -> p j h s", s=SK)[:, :, :, 3 * HD:3 * HD + NOUT],
                                 0.0).then_inc(batch_in, 1)
                for i, (src, dst) in enumerate(((env.ctx_hi, c_h), (env.ctx_lo, c_l))):
                    nc.gpsimd.tensor_copy(dst[:], src[:, :, bass.ds(b * S, S)]).then_inc(batch_in, 1)
                    if not rope:
                        nc.gpsimd.tensor_copy(cm[i][:, :, 0:TAIL], src[:, :, bass.ds(b * S + S - P, TAIL)]
                                              ).then_inc(batch_in, 1)
                        nc.gpsimd.tensor_copy(cd[i][:, :, TAIL:P], src[:, :, bass.ds(b * S + MAIN, DCA)]
                                              ).then_inc(batch_in, 1)
                for m in range(2 * TPB):
                    j, kind = divmod(m, 2)
                    pool.wait_ge(qh_done, (b * 8 + m + 1) * 2)
                    pool.sem_inc(low_begun, 1)
                    dst = stack_of(j, "kq"[kind]).rearrange("p (h s) -> p h s", s=SK)
                    lo = 2 * HD if kind else HD
                    nc.gpsimd.tensor_tensor(dst[:, :, lo:lo + HD], heads(q2[kind]), dst[:, :, 0:HD],
                                            ALU.subtract).then_inc(st_ready, 1)
                pool.wait_ge(st_T, (b + 1) * NST)
        n_zero = 2 + len(stk) + (4 if rope else 14)
        n_ctx = 1 + (2 if rope else 6)

        @block.tensor
        def _(pe):
            pe.wait_ge(zeroed, n_zero)
            with pe.Fori(0, B) as b:
                def project(out, acts, weights):
                    total = sum(3 * wh.shape[1] for (_, _), (wh, _) in zip(acts, weights))
                    n = 0
                    for (ah, al), (wh, wl) in zip(acts, weights):
                        for aa, ww in ((ah, wh), (al, wh), (ah, wl)):
                            for k in range(wh.shape[1]):
                                last = nc.tensor.matmul(out, aa(k), ww[:, k, :], start=(n == 0), stop=(n == total - 1))
                                n += 1
                    return last

                def projection(j, kind):
                    n = 3 * j + "kvq".index(kind)
                    if n >= 3:
                        pe.wait_ge(proj_read, b * NPROJ + n - 2)
                    out = psP[n % 3]
                    whole = (lambda k: c_h[:, k, j * P:(j + 1) * P], lambda k: c_l[:, k, j * P:(j + 1) * P])
                    main = (lambda k: cm[0][:, k, :], lambda k: cm[1][:, k, :])
                    dca = (lambda k: cd[0][:, k, :], lambda k: cd[1][:, k, :])
                    if kind == "q":
                        pe.wait_ge(yl_done, b * TPB + j + 1)
                        last = project(out, [(lambda k: y_h[:, k, :], lambda k: y_l[:, k, :])], [w["q"]])
                    elif rope or j < TPB - 1:
                        last = project(out, [whole], [w[kind]])
                    elif kind == "k":
                        last = project(out, [main, dca], [w["k"], w["kd"]])
                    else:
                        last = project(out, [main], [w["v"]])
                    last.then_inc(proj_done, 1)

                def stack_transposes(m):
                    j, kind = divmod(m, 2)
                    pe.wait_ge(st_ready, b * 8 + m + 1)
                    if m:
                        pe.wait_ge(st_ev, b * NST + m)
                    for c in range(NCH):
                        last = nc.tensor.transpose(psB[:, c, :], stack_of(j, "kq"[kind])[:, c * P:(c + 1) * P],
                                                   env.id16[:])
                    last.then_inc(st_T, 1)

                def y_transposes(j):
                    pe.wait_ge(y_ready, b * TPB + j + 1)
                    for k in range(KD):
                        last = nc.tensor.transpose(pt[:, k, :], y[:, k * P:(k + 1) * P], env.id32[:])
                    last.then_inc(yt_done, 1)

                y_transposes(0)
                pe.wait_ge(batch_in, (b + 1) * n_ctx)
                projection(0, "k")
                projection(0, "v")
                for j in range(TPB):
                    projection(j, "q")
                    if j + 1 < TPB:
                        y_transposes(j + 1)
                        projection(j + 1, "k")
                        projection(j + 1, "v")
                    if j:
                        stack_transposes(2 * j - 1)
                    stack_transposes(2 * j)
                if not rope:
                    pe.wait_ge(proj_read, b * NPROJ + 10)
                    project(psS[:, 0, :], [(lambda k: cd[0][:, k, :], lambda k: cd[1][:, k, :])],
                            [w["vd"]]).then_inc(proj_done, 1)
                stack_transposes(2 * TPB - 1)

                def scores(n):
                    g, i, j = n // NMG, n // TPB % GH, n % TPB
                    if n >= 2:
                        pe.wait_ge(max_done, b * NM + n - 1)
                    h = g * GH + i
                    nc.tensor.matmul(psN[n % 2], QT[:, h if SK == P else h // 2, j * P:(j + 1) * P],
                                     KT[:, h, :], start=True, stop=True).then_inc(s_done, 1)

                def maxima_rows(g, issued):
                    pe.wait_ge(m_ready, b * NG + g + 1)
                    pe.wait_ge(max_done, b * NM + issued)
                    for j in range(TPB):
                        for c in range(2):
                            last = nc.tensor.transpose(psG[:, c, j * P:(j + 1) * P],
                                                       stq[:, j, (2 * g + c) * P:(2 * g + c + 1) * P], env.id16[:])
                    last.then_inc(st_T, 1)

                def scores_t(n):
                    g, kt, p = units[n]
                    if kt == 0 and p == 0:
                        pe.wait_ge(st_ev, b * NST + 8 + g + 1)
                    if n >= 2:
                        pe.wait_ge(exp_done, b * NU + n - 1)
                    for i in range(2):
                        h = g * GH + 2 * p + i
                        last = nc.tensor.matmul(psS[:, 2 * (n % 2) + i, :], KT[:, h, kt * P:(kt + 1) * P],
                                                QT[:, h if SK == P else h // 2, :], start=True, stop=True)
                    last.then_inc(sT_done, 1)

                def group_transposes(g, i, issued):
                    if not rope:
                        pe.wait_ge(max_done, b * NM + issued)
                    if i == 0:
                        pe.wait_ge(oT_done, b * NG + g + 1)
                    r = g * NOUT + i
                    if r:
                        pe.wait_ge(a_done, b * NG * NOUT + r)
                    for j in range(TPB):
                        last = nc.tensor.transpose(pt[:, j, :], oT[:, i, j * P:(j + 1) * P], env.id32[:])
                    last.then_inc(ot_T, 1)

                def values(n):
                    g, kt, p = units[n]
                    if kt == 0 and p == 0 and g:
                        pe.wait_ge(oT_done, b * NG + g)
                    pe.wait_ge(exp_done, b * NU + n + 1)
                    for i in range(2):
                        r = 2 * p + i
                        h = g * GH + r
                        last = nc.tensor.matmul(po[r * VC:(r + 1) * VC, :], V[:, kt, h, :],
                                                PT[:, n % PTB, i, :], start=(kt == 0), stop=(kt == TPB - 1))
                    if not rope and kt == TPB - 1:
                        for i in range(2):
                            last = nc.tensor.matmul(pd[i * VC:(i + 1) * VC, :], Vd[:, g * GH + i, :],
                                                    PT[:, n % PTB, i, :], start=True, stop=True)
                    last.then_inc(pv_done, 1)

                pe.wait_ge(st_ev, b * NST + 8)
                pe.wait_ge(proj_read, (b + 1) * NPROJ)
                for n in range(AHEAD):
                    scores(n)
                maxima_rows(0, AHEAD)
                scores_t(0)
                for n in range(NU):
                    g, u = divmod(n, UPG)
                    if n + 1 < NU:
                        scores_t(n + 1)
                    issued = min(NM, AHEAD + n * SPU)
                    more = range(issued, min(NM, issued + SPU))
                    if u == ROWS and g + 1 < NG:
                        maxima_rows(g + 1, issued)
                        values(n)
                        if more:
                            pe.wait_ge(st_ev, b * NST + 8 + g + 2)
                    if g and u >= 2 and not rope and more:
                        pe.wait_ge(a_done, (b * NG + g - 1) * NOUT + u - 1)
                    for i in more:
                        scores(i)
                    if not (u == ROWS and g + 1 < NG):
                        values(n)
                    if g and u == 1:
                        group_transposes(g - 1, 0, issued + len(more))
                    if g and u == 2 and not rope:
                        group_transposes(g - 1, 1, issued + len(more))
                for i in range(NOUT):
                    group_transposes(NG - 1, i, NM)
                def attention_transposes(j):
                    if j >= 2:
                        pe.wait_ge(al_done, b * TPB + j - 1)
                    out = (pt, psM[:, 0, :].rearrange("p (k q) -> p k q", q=P))[j % 2]
                    for k in range(KD):
                        last = nc.tensor.transpose(out[:, k, :], A[:, j, k * P:(k + 1) * P], env.id32[:])
                    last.then_inc(at_T, 1)
                pe.wait_ge(a_done, (b + 1) * NG * NOUT)
                attention_transposes(0)
                for j in range(TPB):
                    if j + 1 < TPB:
                        attention_transposes(j + 1)
                    pe.wait_ge(al_done, b * TPB + j + 1)
                    if j >= 2:
                        pe.wait_ge(x_done, b * TPB + j - 1)
                    a = a16[j % 2]
                    project(psS[:, j % 2, :], [(lambda k: a[:, 0, k, :], lambda k: a[:, 1, k, :])],
                            [w["o"]]).then_inc(wo_done, 1)
                pe.wait_ge(x_done, (b + 1) * TPB)

        @block.scalar
        def _(act):
            act.wait_ge(var_ready, 1)
            root(nc, rstd[:], agg[:, :, 1], env.eps5, P).then_inc(root_done, 1)
            if rope:
                act.wait_ge(angles, 1)
                act.wait_ge(zeroed, n_zero)
                nc.scalar.activation(sinr[:], sinr[:], ACT.Sin).then_inc(trig, 1)
                nc.scalar.activation(cosr[:], cosr[:], ACT.Sin).then_inc(trig, 1)
            act.wait_ge(zeroed, n_zero)
            with act.Fori(0, B) as b:
                def evacuate(m):
                    j, kind = divmod(m, 2)
                    act.wait_ge(st_T, b * NST + m + 1)
                    if kind:
                        nc.scalar.activation(QT[:, :, j * P:(j + 1) * P], psB, ACT.Copy).then_inc(st_ev, 1)
                    elif SK == P:
                        nc.scalar.activation(KT[:, :, j * P:(j + 1) * P], psB, ACT.Copy).then_inc(st_ev, 1)
                    else:
                        kv = KT[:].rearrange("p (c two) s -> p c two s", two=2)
                        nc.scalar.activation(kv[0:64, :, 0, j * P:(j + 1) * P], psB[0:64], ACT.Copy)
                        nc.scalar.activation(kv[64:P, :, 1, j * P:(j + 1) * P], psB[64:P], ACT.Copy).then_inc(st_ev, 1)

                def group_rows(g):
                    act.wait_ge(st_T, b * NST + 8 + g + 1)
                    nc.scalar.activation(QT[:, 2 * g:2 * g + 2, :], psG, ACT.Copy).then_inc(st_ev, 1)

                def y_high(j):
                    act.wait_ge(yt_done, b * TPB + j + 1)
                    if j:
                        act.wait_ge(proj_done, b * NPROJ + 3 * j)
                    nc.scalar.activation(y_h[:], pt[:], ACT.Copy, scale=SY).then_inc(yh_done, 1)

                y_high(0)
                for j in range(TPB):
                    for i, kind in enumerate("kq"):
                        n = 2 * j + i
                        if not rope:
                            act.wait_ge(c_done, b * 8 + n + 1)
                            nc.scalar.activation(sq, q2[i], ACT.Square).then_inc(sq_done, 1)
                            act.wait_ge(ss_done, b * 8 + n + 1)
                            nc.scalar.activation(ss[:], ss[:], ACT.Sqrt, bias=env.eps6[:, :],
                                                 scale=1.0 / HD).then_inc(rt_done, 1)
                        if n:
                            evacuate(n - 1)
                        act.wait_ge(q_final, b * 8 + n + 1)
                        dst = stack_of(j, kind).rearrange("p (h s) -> p h s", s=SK)
                        nc.scalar.activation(dst[:, :, 0:HD], heads(q2[i]), ACT.Copy).then_inc(qh_done, 1)
                        second = 2 * HD if kind == "k" else HD
                        nc.scalar.activation(dst[:, :, second:second + HD], heads(q2[i]), ACT.Copy
                                             ).then_inc(qh_done, 1)
                        if kind == "k" and j + 1 < TPB:
                            y_high(j + 1)
                evacuate(2 * TPB - 1)
                group_rows(0)
                for n in range(NU):
                    g, u = divmod(n, UPG)
                    act.wait_ge(sT_done, b * NU + n + 1)
                    if n >= PTB:
                        act.wait_ge(pv_done, b * NU + n - PTB + 1)
                    nc.scalar.activation(PT[:, n % PTB, :, :], psS[:, 2 * (n % 2):2 * (n % 2) + 2, :], ACT.Exp,
                                         scale=SCALE / (SQK * SQK)).then_inc(exp_done, 1)
                    if u == ROWS and g + 1 < NG:
                        group_rows(g + 1)
                    if u == UPG - 1:
                        act.wait_ge(pv_done, b * NU + n + 1)
                        if g:
                            act.wait_ge(ot_T, (b * NG + g) * NOUT)
                        if rope:
                            nc.scalar.activation(oT[:, 0, :], po[:], ACT.Copy).then_inc(oT_done, 1)
                        else:
                            nc.scalar.activation(oT[:, 0, :], po[:], ACT.Copy)
                            nc.scalar.activation(oT[:, 1, :], pd[:], ACT.Copy).then_inc(oT_done, 1)
                for j in range(TPB):
                    act.wait_ge(at_T, b * TPB + j + 1)
                    if j >= 2:
                        act.wait_ge(wo_done, b * TPB + j - 1)
                    src = (pt, psM[:, 0, :].rearrange("p (k q) -> p k q", q=P))[j % 2]
                    nc.scalar.activation(a16[j % 2][:, 0, :, :], src[:, :, :], ACT.Copy, scale=SA).then_inc(ah_done, 1)
                act.wait_ge(x_done, (b + 1) * TPB)

        @block.vector
        def _(dve):
            ch = Chain(dve, own)
            norm_statistics(nc, dve, env, stats, agg, ch, var_ready)
            dve.wait_ge(const_in, 16 * n_const if not rope else 32)
            if rope:
                for a in range(2):
                    for f in range(4):
                        ch.link(nc.vector.tensor_scalar(sinr[:, :, 4 * a + f], ang[:, :, a],
                                                        float(np.float32(10000.0) ** np.float32(-f / 4)), None, ALU.mult))
                two_pi = float(2 * np.pi)
                big = 12582912.0
                ch.link(nc.vector.tensor_scalar(cosr[:], sinr[:], float(np.pi / 2), None, ALU.add))
                for r in (sinr, cosr):
                    k = sq[:, 0:NT * 8].rearrange("p (t e) -> p t e", e=8)
                    ch.link(nc.vector.tensor_scalar(k, r[:], 1.0 / two_pi, None, ALU.mult))
                    ch.link(nc.vector.tensor_scalar(k, k, big, None, ALU.add))
                    ch.link(nc.vector.tensor_scalar(k, k, -big, None, ALU.add))
                    ch.link(nc.vector.scalar_tensor_tensor(out=r[:], in0=k, scalar=-two_pi, in1=r[:], op0=ALU.mult,
                                                           op1=ALU.add))
                    ch.link(nc.vector.tensor_scalar(r[:], r[:], float(np.float32(3.1415925)), float(np.float32(-3.1415925)),
                                                    ALU.min, ALU.max))
                dve.sem_inc(angles, 1)
            else:
                dve.wait_ge(zeroed, n_zero)
                for tile in (bq, bk, bkt):
                    t3 = heads(tile[:])
                    ch.link(nc.vector.tensor_reduce(bmean[:], t3, AX.X, ALU.add))
                    ch.link(nc.vector.tensor_scalar(bmean[:], bmean[:], 1.0 / HD, None, ALU.mult))
                    ch.link(nc.vector.tensor_tensor(t3, t3, bmean[:].unsqueeze(2).to_broadcast([P, H, HD]), ALU.subtract))
                for tile in (qwb, kwb, kdwb):
                    ch.link(nc.vector.tensor_scalar(tile[:], tile[:], SQK, None, ALU.mult))
                ch.link(nc.vector.tensor_scalar(bkt[:], bkt[:], mask[:, 1:2], None, ALU.mult))
                ch.link(nc.vector.scalar_tensor_tensor(out=bkt[:], in0=bk[:], scalar=mask[:, 0:1], in1=bkt[:],
                                                       op0=ALU.mult, op1=ALU.add))
                ch.link(nc.vector.tensor_scalar(kdwb[:], kdwb[:], mask[:, 1:2], None, ALU.mult))
                ch.link(nc.vector.scalar_tensor_tensor(out=kdwb[:], in0=kwb[:], scalar=mask[:, 0:1], in1=kdwb[:],
                                                       op0=ALU.mult, op1=ALU.add))
                ch.link(nc.vector.tensor_scalar(bvt[:], bvt[:], mask[:, 0:1], None, ALU.mult))
                ch.link(nc.vector.tensor_scalar(bvd[:], bvd[:], mask[:, 1:2], None, ALU.mult))
            ch.link(nc.vector.tensor_scalar(thc[:], th, 1.0 / (SA * SW), None, ALU.mult))
            ch.link(nc.vector.tensor_scalar(bo[:], bo[:], th, None, ALU.mult))
            dve.wait_ge(root_done, 1)
            ch.link(nc.vector.reciprocal(rstd[:], rstd[:]))
            if rope:
                dve.wait_ge(trig, 2)
            dve.wait_ge(zeroed, n_zero)
            before = ch.n
            per = 8 * 3 + NG + TPB if rope else 8 * 4 + NG * 3 + TPB
            with dve.Fori(0, B) as b:
                c = Chain(dve, own, before + b * per)

                def projected(j, kind):
                    n = 3 * j + "kvq".index(kind)
                    dve.wait_ge(proj_done, b * NPROJ + n + 1)
                    out = psP[n % 3]
                    s = 1.0 / ((SY if kind == "q" else SC) * SW)
                    if kind == "v":
                        dst = V[:, j, :, 0:HD]
                        if rope:
                            nc.vector.tensor_scalar(dst, heads(out), s, None, ALU.mult).then_inc(proj_read, 1)
                        else:
                            bias = bv if j < TPB - 1 else bvt
                            nc.vector.scalar_tensor_tensor(out=dst, in0=heads(out), scalar=s, in1=heads(bias[:]),
                                                           op0=ALU.mult, op1=ALU.add).then_inc(proj_read, 1)
                        return
                    m = 2 * j + "kq".index(kind)
                    q32 = q2[m % 2]
                    if m >= 2:
                        dve.wait_ge(st_ready, b * 8 + m - 1)
                    if rope:
                        ins_ = nc.vector.tensor_scalar(q32, out, s * SQK, None, ALU.mult)
                        ins_.then_inc(proj_read, 1)
                        dve.wait_ge(proj_read, b * NPROJ + n + 1)
                        v = q32.rearrange("p (h a two f) -> p (h a) two f", a=2, two=2, f=4)
                        o = rot.rearrange("p (h a two f) -> p (h a) two f", a=2, two=2, f=4)
                        o2 = sq.rearrange("p (h a two f) -> p (h a) two f", a=2, two=2, f=4)

                        def trig_of(tile):
                            t = tile[:, bass.ds(b * TPB + j, 1), :].rearrange("p a (x f) -> p (a x) f", f=4)
                            return t.unsqueeze(1).to_broadcast([P, H, 2, 4])

                        def four(ap):
                            return ap.rearrange("p (h a) f -> p h a f", a=2)
                        for i in range(2):
                            nc.vector.tensor_tensor(four(o[:, :, i, :]), four(v[:, :, i, :]), trig_of(cosr), ALU.mult)
                            last = nc.vector.tensor_tensor(four(o2[:, :, i, :]), four(v[:, :, 1 - i, :]), trig_of(sinr),
                                                           ALU.mult)
                        c.link(last)
                        c.link(nc.vector.tensor_tensor(v[:, :, 0, :], o[:, :, 0, :], o2[:, :, 0, :], ALU.subtract))
                        c.link(nc.vector.tensor_tensor(v[:, :, 1, :], o[:, :, 1, :], o2[:, :, 1, :], ALU.add))
                    else:
                        bias = bq if kind == "q" else (bk if j < TPB - 1 else bkt)
                        wb = qwb if kind == "q" else (kwb if j < TPB - 1 else kdwb)
                        nc.vector.scalar_tensor_tensor(out=q32, in0=out, scalar=s, in1=bias[:], op0=ALU.mult,
                                                       op1=ALU.add).then_inc(proj_read, 1)
                        dve.wait_ge(proj_read, b * NPROJ + n + 1)
                        dve.sem_inc(c_done, 1)
                        dve.wait_ge(sq_done, b * 8 + m + 1)
                        nc.vector.tensor_reduce(ss[:], heads(sq), AX.X, ALU.add).then_inc(ss_done, 1)
                        dve.wait_ge(rt_done, b * 8 + m + 1)
                        c.link(nc.vector.reciprocal(ss[:], ss[:]))
                        q3 = heads(q32)
                        c.link(nc.vector.tensor_tensor(q3, q3, ss[:].unsqueeze(2).to_broadcast([P, H, HD]), ALU.mult))
                        for i, op in ((0, ALU.mult), (1, ALU.add)):
                            c.link(nc.vector.tensor_tensor(q3, q3, wb[:, i:i + 1, :].to_broadcast([P, H, HD]), op))
                    dve.sem_inc(q_final, 1)

                def normalise(j):
                    t = b * TPB + j
                    if j:
                        dve.wait_ge(yt_done, b * TPB + j)
                    nc.vector.tensor_scalar(y, at(env.x, t), agg[:, bass.ds(t, 1), 0], rstd[:, bass.ds(t, 1)],
                                            ALU.subtract, ALU.mult).then_inc(y_ready, 1)

                def maximum(n):
                    g, i, j = n // NMG, n // TPB % GH, n % TPB
                    h = g * GH + i
                    dve.wait_ge(s_done, b * NM + n + 1)
                    sc = psN[n % 2]
                    last = nc.vector.tensor_reduce(nmax[:, j, h:h + 1, 0], sc[:, 0:MAIN], AX.X, ALU.max)
                    if not rope:
                        last = nc.vector.tensor_reduce(nmax[:, j, h:h + 1, 1], sc[:, MAIN:S], AX.X, ALU.max)
                    last.then_inc(max_done, 1)

                def maxima_rows(g):
                    dve.wait_ge(max_done, b * NM + (g + 1) * NMG)
                    rows = stq[:].rearrange("p j (h s) -> p j h s", s=SK)
                    for i in range(NOUT):
                        last = nc.vector.tensor_scalar(rows[:, :, g * GH:(g + 1) * GH, 3 * HD + i],
                                                       nmax[:, :, g * GH:(g + 1) * GH, i], -1.0 / SM, None, ALU.mult)
                    last.then_inc(m_ready, 1)

                def group_output(g, i):
                    dve.wait_ge(ot_T, (b * NG + g) * NOUT + i + 1)
                    av = A[:, :, g * GH * HD:(g + 1) * GH * HD].rearrange("p j (h d) -> p j h d", d=HD)
                    v = pt[:].rearrange("p j (h c) -> p j h c", c=VC)
                    c.link(nc.vector.reciprocal(rec[:, :, :, i], v[:, :, :, HD]))
                    spread = rec[:, :, :, i:i + 1].to_broadcast([P, TPB, GH, HD])
                    out = av if i == 0 else tmp[:]
                    product = nc.vector.tensor_tensor(out, v[:, :, :, 0:HD], spread, ALU.mult)
                    if i == 0:
                        product.then_inc(a_done, 1)
                        return
                    c.link(product)
                    nc.vector.tensor_tensor(av, av, tmp[:], ALU.add).then_inc(a_done, 1)

                normalise(0)
                for j in range(TPB):
                    dve.wait_ge(yh_done, b * TPB + j + 1)
                    nc.vector.scalar_tensor_tensor(out=y_l[:], in0=pt[:], scalar=SY, in1=y_h[:], op0=ALU.mult,
                                                   op1=ALU.subtract).then_inc(yl_done, 1)
                    projected(j, "k")
                    projected(j, "v")
                    if j + 1 < TPB:
                        normalise(j + 1)
                    projected(j, "q")
                if not rope:
                    dve.wait_ge(proj_done, (b + 1) * NPROJ)
                    nc.vector.scalar_tensor_tensor(out=Vd[:, :, 0:HD], in0=heads(psS[:, 0, :]),
                                                   scalar=1.0 / (SC * SW), in1=heads(bvd[:]), op0=ALU.mult,
                                                   op1=ALU.add).then_inc(proj_read, 1)
                for n in range(AHEAD):
                    if n == NMG:
                        maxima_rows(0)
                    maximum(n)
                for n in range(NU):
                    g, u = divmod(n, UPG)
                    if u == ROWS and g + 1 < NG:
                        maxima_rows(g + 1)
                    issued = AHEAD + n * SPU
                    for i in range(issued, min(NM, issued + SPU)):
                        maximum(i)
                    if g and u == 1:
                        group_output(g - 1, 0)
                    if g and u == 2 and not rope:
                        group_output(g - 1, 1)
                for i in range(NOUT):
                    group_output(NG - 1, i)

                def attention_low(j):
                    dve.wait_ge(ah_done, b * TPB + j + 1)
                    src = (pt, psM[:, 0, :].rearrange("p (k q) -> p k q", q=P))[j % 2]
                    nc.vector.scalar_tensor_tensor(out=a16[j % 2][:, 1, :, :], in0=src[:, :, :], scalar=SA,
                                                   in1=a16[j % 2][:, 0, :, :], op0=ALU.mult,
                                                   op1=ALU.subtract).then_inc(al_done, 1)
                attention_low(0)
                for j in range(TPB):
                    if j + 1 < TPB:
                        attention_low(j + 1)
                    t = b * TPB + j
                    dve.wait_ge(wo_done, b * TPB + j + 1)
                    c.link(nc.vector.scalar_tensor_tensor(out=at(env.x, t), in0=psS[:, j % 2, :], scalar=thc[:],
                                                          in1=at(env.x, t), op0=ALU.mult, op1=ALU.add))
                    nc.vector.tensor_tensor(at(env.x, t), at(env.x, t), bo[:], ALU.add).then_inc(x_done, 1)
                assert c.n == per
                dve.wait_ge(x_done, (b + 1) * TPB)


def layer_attention(nc, env, index):
    ins = env.ins
    with ExitStack() as ctx:
        env.count += 1

        def pair(name, kk):
            return tuple(ctx.enter_context(nc.sbuf_tensor(f"{name}_{h}{env.count}", [P, kk, D], F16)) for h in "hl")
        if index == 0:
            names = [("q", "Wq0", KD, 32), ("k", "Wk0", KC, 32), ("kd", "Wkd0", KC, 32), ("v", "Wv0", KC, 0),
                     ("vd", "Wvd0", KC, 0), ("o", "Wo0", KD, 0)]
        else:
            names = [("q", "Wq3", KD, 0), ("k", "Wk3", KC, 0), ("v", "Wv3", KC, 0), ("o", "Wo3", KD, 0)]
        w = {key: pair(key, kk) for key, _, kk, _ in names}
        split_weights_block(nc, env, [(ins[n], *w[key], hd) for key, n, _, hd in names])
        w["bo"] = ins["bo0" if index == 0 else "bo3"]
        attention_block(nc, env, w, env.th[:, index:index + 1], index == 3)


def layer_xattn0(nc, env):
    layer_attention(nc, env, 0)


def layer_xattn3(nc, env):
    layer_attention(nc, env, 3)


def layer_xattn1(nc, env):
    ins = env.ins
    SQ, SAT = 64.0, 4096.0
    with ExitStack() as ctx:
        env.count += 1
        sb, ps = tiles_of(nc, ctx, f"x1{env.count}")
        y_hi, y_lo = sb("y_hi", [P, KD, T], F16), sb("y_lo", [P, KD, T], F16)
        norm_block(nc, env, y_hi, y_lo)
        w32, w_h, w_l = sb("w32", [P, 2, KC, P]), sb("wh", [P, 2, KC, P], F16), sb("wl", [P, 2, KC, P], F16)
        bias, thc = sb("bias", [P, 2]), sb("thc", [P, 1])
        yb = [sb(f"yb{i}", [P, KD, S], F16) for i in range(2)]
        cb = [sb(f"cb{i}", [P, KC, S], F16) for i in range(2)]
        qk, qk_h, qk_l = sb("qk", [P, 2, S]), sb("qkh", [P, 2, S], F16), sb("qkl", [P, 2, S], F16)
        nm, tot, prob = sb("nm", [P, 2]), sb("tot", [P, 2]), sb("prob", [P, 2, S])
        at_h, at_l = sb("ath", [P, TPB, S], F16), sb("atl", [P, TPB, S], F16)
        pq, pe_, pt, po = ps("q", [P, 2, S]), ps("e", [P, 2, S]), ps("t", [P, 2, 4, P]), ps("o", [P, 2, S])
        sem = env.sem
        w_in, w_hi, w_done, copied, own = sem("w_in"), sem("w_hi"), sem("w_done"), sem("batch_copy"), sem("x1_dve")
        q_done, q_ev, qh_done, ql_done = sem("q_done"), sem("q_ev"), sem("q_hi"), sem("q_lo")
        e_done, m_done, p_done, n_done = sem("energy"), sem("rowmax"), sem("exp"), sem("normed")
        t_done, th_done, tl_done, o_done, x_done = sem("att_T"), sem("att_hi"), sem("att_lo"), sem("out"), sem("x_done")
        block = ctx.enter_context(nc.Block())

        @block.sync
        def _(sp):
            for i, n in enumerate(("Wq1", "Wk1")):
                sp.dma_start(w32[:, i, :, :], ins[n].rearrange("(k p) d -> p k d", p=P)).then_inc(w_in, 16)
            for i, n in enumerate(("bq1", "bk1")):
                sp.dma_start(bias[:, i:i + 1], ins[n]).then_inc(w_in, 16)

        @block.gpsimd
        def _(pool):
            with pool.Fori(0, B) as b:
                for src, dst in ((env.ctx_hi, cb[0]), (env.ctx_lo, cb[1]), (y_hi, yb[0]), (y_lo, yb[1])):
                    nc.gpsimd.tensor_copy(dst[:], src[:, :, bass.ds(b * S, S)]).then_inc(copied, 1)
                pool.wait_ge(x_done, (b + 1) * TPB)

        @block.tensor
        def _(pe):
            pe.wait_ge(w_done, 1)
            with pe.Fori(0, B) as b:
                pe.wait_ge(copied, b * 4 + 2)
                for i in range(2):
                    n = 0
                    for wt, c in ((w_h, cb[0]), (w_h, cb[1]), (w_l, cb[0])):
                        for k in range(KC):
                            last = nc.tensor.matmul(pq[:, i, :], wt[:, i, k, :], c[:, k, :], start=(n == 0),
                                                    stop=(n == 3 * KC - 1))
                            n += 1
                last.then_inc(q_done, 1)
                pe.wait_ge(ql_done, b + 1)
                pe.wait_ge(copied, (b + 1) * 4)

                def energy(j):
                    if j >= 2:
                        pe.wait_ge(p_done, b * TPB + j - 1)
                    for n, (q, k) in enumerate(((qk_h, qk_h), (qk_l, qk_h), (qk_h, qk_l))):
                        last = nc.tensor.matmul(pe_[:, j % 2, :], q[:, 0, j * P:(j + 1) * P], k[:, 1, :],
                                                start=(n == 0), stop=(n == 2))
                    last.then_inc(e_done, 1)
                energy(0)
                for j in range(TPB):
                    if j + 1 < TPB:
                        energy(j + 1)
                    pe.wait_ge(n_done, b * TPB + j + 1)
                    if j >= 2:
                        pe.wait_ge(tl_done, b * TPB + j - 1)
                    for k in range(4):
                        last = nc.tensor.transpose(pt[:, j % 2, k, :], prob[:, j % 2, k * P:(k + 1) * P], env.id32[:])
                    last.then_inc(t_done, 1)
                pe.wait_ge(tl_done, (b + 1) * TPB)
                for j in range(TPB):
                    if j >= 2:
                        pe.wait_ge(x_done, b * TPB + j - 1)
                    n = 0
                    for y, a in ((yb[0], at_h), (yb[1], at_h), (yb[0], at_l)):
                        for k in range(KD):
                            last = nc.tensor.matmul(po[:, j % 2, :], y[:, k, j * P:(j + 1) * P], a[:, k, :],
                                                    start=(n == 0), stop=(n == 3 * KD - 1))
                            n += 1
                    last.then_inc(o_done, 1)
                pe.wait_ge(x_done, (b + 1) * TPB)

        @block.scalar
        def _(act):
            act.wait_ge(w_in, 64)
            nc.scalar.activation(w_h[:], w32[:], ACT.Copy, scale=SW).then_inc(w_hi, 1)
            with act.Fori(0, B) as b:
                act.wait_ge(q_done, b + 1)
                for i in range(2):
                    last = nc.scalar.activation(qk[:, i, :], pq[:, i, :], ACT.Identity, bias=bias[:, i:i + 1],
                                                scale=1.0 / (SC * SW))
                last.then_inc(q_ev, 1)
                act.wait_ge(q_ev, b + 1)
                nc.scalar.activation(qk_h[:], qk[:], ACT.Copy, scale=SQ).then_inc(qh_done, 1)

                def exponentials(j):
                    act.wait_ge(m_done, b * TPB + j + 1)
                    if j >= 2:
                        act.wait_ge(t_done, b * TPB + j - 1)
                    nc.scalar.activation(prob[:, j % 2, :], pe_[:, j % 2, :], ACT.Exp, bias=nm[:, j % 2:j % 2 + 1],
                                         scale=1.0 / (SQ * SQ), accum_out=tot[:, j % 2:j % 2 + 1]).then_inc(p_done, 1)

                def high(j):
                    act.wait_ge(t_done, b * TPB + j + 1)
                    nc.scalar.activation(at_h[:, :, j * P:(j + 1) * P], pt[:, j % 2, :, :], ACT.Copy,
                                         scale=SAT).then_inc(th_done, 1)
                exponentials(0)
                for j in range(1, TPB):
                    exponentials(j)
                    high(j - 1)
                high(TPB - 1)
                act.wait_ge(x_done, (b + 1) * TPB)

        @block.vector
        def _(dve):
            ch = Chain(dve, own)
            dve.wait_ge(w_hi, 1)
            nc.vector.scalar_tensor_tensor(out=w_l[:], in0=w32[:], scalar=SW, in1=w_h[:], op0=ALU.mult,
                                           op1=ALU.subtract).then_inc(w_done, 1)
            ch.link(nc.vector.tensor_scalar(thc[:], env.th[:, 1:2], 1.0 / (SY * SAT), None, ALU.mult))
            base, per = ch.n, 2 * TPB
            with dve.Fori(0, B) as b:
                c = Chain(dve, own, base + b * per)
                dve.wait_ge(qh_done, b + 1)
                nc.vector.scalar_tensor_tensor(out=qk_l[:], in0=qk[:], scalar=SQ, in1=qk_h[:], op0=ALU.mult,
                                               op1=ALU.subtract).then_inc(ql_done, 1)

                def maximum(j):
                    dve.wait_ge(e_done, b * TPB + j + 1)
                    c.link(nc.vector.tensor_reduce(nm[:, j % 2:j % 2 + 1], pe_[:, j % 2, :], AX.X, ALU.max))
                    nc.vector.tensor_scalar(nm[:, j % 2:j % 2 + 1], nm[:, j % 2:j % 2 + 1], -1.0 / (SQ * SQ), None,
                                            ALU.mult).then_inc(m_done, 1)

                def low(j):
                    dve.wait_ge(th_done, b * TPB + j + 1)
                    nc.vector.scalar_tensor_tensor(out=at_l[:, :, j * P:(j + 1) * P], in0=pt[:, j % 2, :, :], scalar=SAT,
                                                   in1=at_h[:, :, j * P:(j + 1) * P], op0=ALU.mult,
                                                   op1=ALU.subtract).then_inc(tl_done, 1)
                maximum(0)
                for j in range(TPB):
                    if j + 1 < TPB:
                        if j:
                            dve.wait_ge(p_done, b * TPB + j)
                        maximum(j + 1)
                    dve.wait_ge(p_done, b * TPB + j + 1)
                    c.link(nc.vector.reciprocal(tot[:, j % 2:j % 2 + 1], tot[:, j % 2:j % 2 + 1]))
                    nc.vector.tensor_scalar(prob[:, j % 2, :], prob[:, j % 2, :], tot[:, j % 2:j % 2 + 1], None,
                                            ALU.mult).then_inc(n_done, 1)
                    if j:
                        low(j - 1)
                low(TPB - 1)
                for j in range(TPB):
                    dve.wait_ge(o_done, b * TPB + j + 1)
                    xt = at(env.x, b * TPB + j)
                    nc.vector.scalar_tensor_tensor(out=xt, in0=po[:, j % 2, :], scalar=thc[:], in1=xt, op0=ALU.mult,
                                                   op1=ALU.add).then_inc(x_done, 1)
                assert c.n == per
                dve.wait_ge(x_done, (b + 1) * TPB)


def layer_ffn1(nc, env):
    ins = env.ins
    BIG = 12582912.0
    with ExitStack() as ctx:
        env.count += 1
        sb, ps = tiles_of(nc, ctx, f"f1{env.count}")
        w8, w16 = sb("w8", [P, KD, D // 4], I32), sb("w16", [P, KD, D], F16)
        ws, bias = sb("ws", [P, D]), sb("bias", [P, D])
        stats, agg, rstd = sb("stats", [P, NT, 6]), sb("agg", [P, NT, 2]), sb("rstd", [P, NT])
        y, q = sb("y", [P, 2, D]), sb("q", [P, 2, D], F16)
        qT = sb("qT", [P, 2, KD, P], F16)
        sc, inv, least = sb("sc", [P, 2]), sb("inv", [P, 2]), sb("least", [P, 2])
        o32, o16 = sb("o32", [P, 2, D]), sb("o16", [P, 2, D], F16)
        pt = [ps(f"t{i}", [P, KD, P], F16) for i in range(2)]
        po = [ps(f"o{i}", [P, D]) for i in range(2)]
        sem = env.sem
        w_in, c_in, w_done, own = sem("w_in"), sem("consts_in"), sem("w_done"), sem("f1_dve")
        var_ready, root_done = sem("variances"), sem("roots")
        q_ready, t_done, t_ev, o_done, o_read = sem("q_ready"), sem("q_T"), sem("q_T_ev"), sem("out"), sem("out_read")
        scaled, biased = sem("scaled"), sem("biased")
        block = ctx.enter_context(nc.Block())

        @block.sync
        def _(sp):
            sp.dma_start(w8[:], ins["weight1"].rearrange("(k p) n -> p k n", p=P)).then_inc(w_in, 16)
            sp.dma_start(ws[:], row_of(ins["w_scale1"], D)).then_inc(c_in, 16)
            sp.dma_start(bias[:], row_of(ins["bias1"], D)).then_inc(c_in, 16)

        @block.gpsimd
        def _(pool):
            pool.wait_ge(c_in, 32)
            for t in range(NT):
                u = t % 2
                pool.wait_ge(scaled, t + 1)
                nc.gpsimd.tensor_tensor(o16[:, u, :], o32[:, u, :], bias[:], ALU.add).then_inc(biased, 1)

        @block.scalar
        def _(act):
            act.wait_ge(w_in, 16)
            nc.scalar.activation(w16[:], w8[:].bitcast(I8), ACT.Copy).then_inc(w_done, 1)
            act.wait_ge(var_ready, 1)
            root(nc, rstd[:], agg[:, :, 1], env.eps5, P).then_inc(root_done, 1)
            for t in range(NT):
                act.wait_ge(t_done, t + 1)
                nc.scalar.activation(qT[:, t % 2, :, :], pt[t % 2][:], ACT.Copy).then_inc(t_ev, 1)

        @block.tensor
        def _(pe):
            pe.wait_ge(w_done, 1)

            def product(t):
                u = t % 2
                pe.wait_ge(t_ev, t + 1)
                if t >= 2:
                    pe.wait_ge(scaled, t - 1)
                for k in range(KD):
                    last = nc.tensor.matmul(po[u][:], qT[:, u, k, :], w16[:, k, :], start=(k == 0), stop=(k == KD - 1))
                last.then_inc(o_done, 1)
            for t in range(NT):
                u = t % 2
                pe.wait_ge(q_ready, t + 1)
                if t >= 2:
                    pe.wait_ge(t_ev, t - 1)
                for k in range(KD):
                    last = nc.tensor.transpose(pt[u][:, k, :], q[:, u, k * P:(k + 1) * P], env.id16[:])
                last.then_inc(t_done, 1)
                if t:
                    product(t - 1)
            product(NT - 1)

        @block.vector
        def _(dve):
            c = Chain(dve, own)
            norm_statistics(nc, dve, env, stats, agg, c, var_ready)
            dve.wait_ge(root_done, 1)
            c.link(nc.vector.reciprocal(rstd[:], rstd[:]))
            dve.wait_ge(c_in, 32)

            def output(t):
                u = t % 2
                dve.wait_ge(o_done, t + 1)
                if t >= 2:
                    dve.wait_ge(biased, t - 1)
                nc.vector.scalar_tensor_tensor(out=o32[:, u, :], in0=po[u][:], scalar=sc[:, u:u + 1], in1=ws[:],
                                               op0=ALU.mult, op1=ALU.mult).then_inc(scaled, 1)

            def residual(t):
                u = t % 2
                dve.wait_ge(biased, t + 1)
                nc.vector.scalar_tensor_tensor(out=env.x[:, t, :], in0=o16[:, u, :], scalar=env.th[:, 5:6],
                                               in1=env.x[:, t, :], op0=ALU.mult, op1=ALU.add)
            for t in range(NT):
                u = t % 2
                c.link(nc.vector.tensor_scalar(y[:, u, :], env.x[:, t, :], agg[:, t, 0:1], rstd[:, t:t + 1],
                                               ALU.subtract, ALU.mult))
                if t >= 2:
                    output(t - 2)
                nc.vector.tensor_reduce(least[:, u:u + 1], y[:, u, :], AX.X, ALU.min)
                c.link(nc.vector.tensor_reduce(inv[:, u:u + 1], y[:, u, :], AX.X, ALU.max))
                c.link(nc.vector.scalar_tensor_tensor(out=inv[:, u:u + 1], in0=least[:, u:u + 1], scalar=-1.0,
                                                      in1=inv[:, u:u + 1], op0=ALU.mult, op1=ALU.max))
                if t >= 2:
                    dve.wait_ge(scaled, t - 1)
                c.link(nc.vector.tensor_scalar(sc[:, u:u + 1], inv[:, u:u + 1], 1e-7, 1.0 / 127.0, ALU.max, ALU.mult))
                c.link(nc.vector.reciprocal(inv[:, u:u + 1], sc[:, u:u + 1]))
                c.link(nc.vector.tensor_scalar(y[:, u, :], y[:, u, :], inv[:, u:u + 1], BIG, ALU.mult, ALU.add))
                if t >= 2:
                    dve.wait_ge(t_done, t - 1)
                nc.vector.tensor_scalar(q[:, u, :], y[:, u, :], -BIG, 127.0, ALU.add, ALU.min).then_inc(q_ready, 1)
                if t >= 3:
                    residual(t - 3)
            output(NT - 2)
            residual(NT - 3)
            output(NT - 1)
            residual(NT - 2)
            residual(NT - 1)


LOG1P = (0.33333319832513, 0.2000383545232939, 0.14116977575002837, 0.1343377665106373)


def ssm_prepare_block(nc, env, u, delta, du, bc, SB):
    ins = env.ins
    TAPS, R, NS = 4, 16, 16
    XD = R + 2 * NS
    c1, c2, c3, c4 = LOG1P
    with ExitStack() as ctx:
        env.count += 1
        sb, ps = tiles_of(nc, ctx, f"sp{env.count}")
        w32, cw = sb("w32", [P, KC, D]), sb("cw", [P, TAPS, D])
        wt = sb("wt", [P, KC, D])
        w_h, w_l = sb("wh", [P, TAPS, KC, D], F16), sb("wl", [P, TAPS, KC, D], F16)
        cb, dtb, dd = sb("cb", [P, KD]), sb("dtb", [P, KD]), sb("dd", [P, KD])
        xp, dtw = sb("xp", [P, KD, XD]), sb("dtw", [R, D])
        xd = sb("xd", [XD, S])
        t1, t2 = sb("t1", [P, 2, S]), sb("t2", [P, 2, S])
        pu = [ps(f"u{i}", [P, S]) for i in range(2)]
        px = ps("x", [P, S])
        pd = ps("d", [P, KD, S])
        sem = env.sem
        c_in, w_ready, w_hi, w_done = sem("ssm_in"), sem("tap"), sem("tap_hi"), sem("tap_lo")
        zero, u_mm, u_ev, x_mm, x_ev, bch, bcl = (sem(n) for n in ("bc_zero", "u_mm", "u_ev", "x_mm", "x_ev", "bc_hi", "bc_lo"))
        d_mm, own, abs_in, z_done, s_done, q_done, du_done = (sem(n) for n in (
            "dt_mm", "sp_dve", "dt_raw", "exp_abs", "s_ready", "q_ready", "du_done"))
        block = ctx.enter_context(nc.Block())

        @block.sync
        def _(sp):
            sp.dma_start(w32[:], ins["in_proj"].rearrange("(k p) e -> p k e", p=P)).then_inc(c_in, 16)
            sp.dma_start(cw[:], row_of(ins["conv_w_t"], TAPS * D).rearrange("p (j e) -> p j e", e=D)).then_inc(c_in, 16)
            for tile, n in ((cb, "conv_b_t"), (dtb, "dt_b_t"), (dd, "D_t"), (dtw, "dt_w")):
                sp.dma_start(tile[:], ins[n]).then_inc(c_in, 16)
            sp.dma_start(xp[:], ins["x_proj"].rearrange("(k p) r -> p k r", p=P)).then_inc(c_in, 16)

        @block.gpsimd
        def _(pool):
            nc.gpsimd.memset(bc[:], 0.0).then_inc(zero, 1)
            pool.wait_ge(c_in, 112)
            for b in range(B):
                for h in range(2):
                    pool.wait_ge(du_done, 2 * b + h + 1)
                    for c in (2 * h, 2 * h + 1):
                        nc.gpsimd.tensor_scalar(u[:, 4 * b + c, :], u[:, 4 * b + c, :], dd[:, c:c + 1], None, ALU.mult)

        @block.tensor
        def _(pe):
            pe.wait_ge(w_done, TAPS)
            for b in range(B):
                for c in range(KD):
                    m = b * KD + c
                    if m >= 2:
                        pe.wait_ge(u_ev, m - 1)
                    n = 0
                    for j in range(TAPS - 1, -1, -1):
                        shift = TAPS - 1 - j
                        for ww, cc in ((w_h, env.ctx_hi), (w_h, env.ctx_lo), (w_l, env.ctx_hi)):
                            for k in range(KC):
                                last = nc.tensor.matmul(pu[m % 2][:, shift:S], ww[:, j, k, c * P:(c + 1) * P],
                                                        cc[:, k, b * S:(b + 1) * S - shift], start=(n == 0),
                                                        stop=(n == TAPS * 3 * KC - 1))
                                n += 1
                    last.then_inc(u_mm, 1)
                pe.wait_ge(u_ev, (b + 1) * KD)
                if b:
                    pe.wait_ge(bcl, b)
                for k in range(KD):
                    last = nc.tensor.matmul(px[0:XD, :], xp[:, k, :], u[:, b * KD + k, :], start=(k == 0), stop=(k == KD - 1))
                last.then_inc(x_mm, 1)
                pe.wait_ge(x_ev, b + 1)
                if b:
                    pe.wait_ge(abs_in, 2 * b)
                for c in range(KD):
                    last = nc.tensor.matmul(pd[:, c, :], dtw[:, c * P:(c + 1) * P], xd[0:R, :], start=True, stop=True)
                last.then_inc(d_mm, 1)

        @block.scalar
        def _(act):
            for j in range(TAPS):
                act.wait_ge(w_ready, j + 1)
                nc.scalar.activation(w_h[:, j, :, :], wt[:], ACT.Copy, scale=SW).then_inc(w_hi, 1)
            act.wait_ge(c_in, 112)
            act.wait_ge(zero, 1)

            def steps(b):
                for h in range(2):
                    act.wait_ge(abs_in, 2 * b + h + 1)
                    sl = slice(4 * b + 2 * h, 4 * b + 2 * h + 2)
                    nc.scalar.activation(du[:, sl, :], delta[:, sl, :], ACT.Abs).then_inc(z_done, 1)
                    act.wait_ge(z_done, 2 * (2 * b + h) + 1)
                    nc.scalar.activation(du[:, sl, :], du[:, sl, :], ACT.Exp, scale=-1.0).then_inc(z_done, 1)
                    act.wait_ge(s_done, 2 * b + h + 1)
                    nc.scalar.activation(t2[:], t1[:], ACT.Square, scale=0.5).then_inc(q_done, 1)
            for b in range(B):
                for c in range(KD):
                    m = b * KD + c
                    act.wait_ge(u_mm, m + 1)
                    nc.scalar.activation(u[:, m, :], pu[m % 2][:], ACT.Silu, bias=cb[:, c:c + 1],
                                         scale=1.0 / (SC * SW)).then_inc(u_ev, 1)
                act.wait_ge(x_mm, b + 1)
                if b:
                    act.wait_ge(d_mm, b)
                nc.scalar.activation(xd[:], px[0:XD, :], ACT.Copy).then_inc(x_ev, 1)
                nc.scalar.activation(bc[0:XD, b, :], px[0:XD, :], ACT.Copy, scale=SB).then_inc(bch, 1)
                steps(b)

        @block.vector
        def _(dve):
            ch = Chain(dve, own)
            dve.wait_ge(c_in, 112)
            for j in range(TAPS):
                if j:
                    dve.wait_ge(w_done, j)
                nc.vector.tensor_tensor(wt[:], w32[:], cw[:, j:j + 1, :].to_broadcast([P, KC, D]), ALU.mult
                                        ).then_inc(w_ready, 1)
                dve.wait_ge(w_hi, j + 1)
                nc.vector.scalar_tensor_tensor(out=w_l[:, j, :, :], in0=wt[:], scalar=SW, in1=w_h[:, j, :, :],
                                               op0=ALU.mult, op1=ALU.subtract).then_inc(w_done, 1)
            for b in range(B):
                dve.wait_ge(bch, b + 1)
                nc.vector.scalar_tensor_tensor(out=bc[64:64 + XD, b, :], in0=px[0:XD, :], scalar=SB, in1=bc[0:XD, b, :],
                                               op0=ALU.mult, op1=ALU.subtract).then_inc(bcl, 1)
                dve.wait_ge(d_mm, b + 1)
                for c in range(KD):
                    last = nc.vector.tensor_scalar(delta[:, 4 * b + c, :], pd[:, c, :], dtb[:, c:c + 1], None, ALU.add)
                    if c % 2:
                        last.then_inc(abs_in, 1)
                for h in range(2):
                    i = 2 * b + h
                    sl = slice(4 * b + 2 * h, 4 * b + 2 * h + 2)
                    z, t = du[:, sl, :], delta[:, sl, :]
                    dve.wait_ge(z_done, 2 * i + 2)
                    ch.link(nc.vector.tensor_scalar(t1[:], z, 2.0, None, ALU.add))
                    ch.link(nc.vector.reciprocal(t1[:], t1[:]))
                    nc.vector.scalar_tensor_tensor(out=t1[:], in0=z, scalar=2.0, in1=t1[:], op0=ALU.mult, op1=ALU.mult
                                                   ).then_inc(s_done, 1)
                    dve.wait_ge(q_done, i + 1)
                    ch.link(nc.vector.tensor_scalar(z, t2[:], c4, None, ALU.mult))
                    for cc in (c3, c2, c1):
                        ch.link(nc.vector.scalar_tensor_tensor(out=z, in0=z, scalar=cc, in1=t2[:], op0=ALU.add,
                                                               op1=ALU.mult))
                    ch.link(nc.vector.scalar_tensor_tensor(out=z, in0=z, scalar=1.0, in1=t1[:], op0=ALU.add, op1=ALU.mult))
                    ch.link(nc.vector.scalar_tensor_tensor(out=t, in0=t, scalar=0.0, in1=z, op0=ALU.max, op1=ALU.add))
                    nc.vector.scalar_tensor_tensor(out=z, in0=t, scalar=1.0 / SB, in1=u[:, sl, :], op0=ALU.mult,
                                                   op1=ALU.mult).then_inc(du_done, 1)


def ssm_scan_block(nc, env, u, delta, du, bc, SB):
    NS, R = 16, 16
    NU = NS * KD
    RA, RH, RC = 4, 3, 3
    with ExitStack() as ctx:
        env.count += 1
        sb, ps = tiles_of(nc, ctx, f"sc{env.count}")
        A = sb("A", [P, KD, NS])
        sel = sb("sel", [P, 2 * NS, P], F16)
        stats, agg, rstd = sb("stats", [P, NT, 6]), sb("agg", [P, NT, 2]), sb("rstd", [P, NT])
        dl = sb("dl", [P, KD, S])
        g = sb("g", [P, KD, D])
        dA, dB = sb("dA", [P, RA, S]), sb("dB", [P, 2, S])
        h, hc, cs = sb("h", [P, RH, S]), sb("hc", [P, RC, S]), sb("cs", [P, 2, S])
        bcb = sb("bcb", [P, S], F16)
        yt = sb("yt", [P, 2, S])
        py = ps("y", [P, KD, S])
        pb = [ps(f"b{i}", [P, S]) for i in range(2)]
        pc = [ps(f"c{i}", [P, S]) for i in range(2)]
        sem = env.sem
        a_in, a_done, sel_done, own = sem("A_in"), sem("A_exp"), sem("selectors"), sem("scan_dve")
        var_ready, root_done, copied = sem("variances"), sem("roots"), sem("batch_copy")
        z_done, g_done, b_mm, c_mm, c_ev = (sem(n) for n in ("z", "silu_z", "B_rows", "C_rows", "C_ev"))
        dA_done, dB_done, h_done, hc_done, y_mm = (sem(n) for n in ("decay", "input", "state", "stateC", "y_mm"))
        y_ev, yg_done, yt_done, x_done = (sem(n) for n in ("y_ev", "y_gated", "y_T", "x_done"))
        block = ctx.enter_context(nc.Block())

        @block.sync
        def _(sp):
            sp.dma_start(A[:], env.ins["A_log_t"].rearrange("(c p) n -> p c n", p=P)).then_inc(a_in, 16)

        @block.gpsimd
        def _(pool):
            nc.gpsimd.memset(sel[:], 0.0).then_inc(sel_done, 1)
            pool.wait_ge(sel_done, 1)
            for i, off in enumerate((R, 64 + R)):
                nc.gpsimd.affine_select(out=sel[:], in_=sel[:], compare_op=ALU.not_equal, fill=1.0, base=-off,
                                        pattern=[[-1, 2 * NS], [0, P]], channel_multiplier=1).then_inc(sel_done, 1)
                pool.wait_ge(sel_done, i + 2)
            with pool.Fori(0, B) as b:
                nc.gpsimd.tensor_copy(bcb[:], bc[:, bass.ds(b, 1), :].rearrange("p a s -> p (a s)")).then_inc(copied, 1)
                nc.gpsimd.tensor_copy(dl[:], delta[:, bass.ds(b * KD, KD), :]).then_inc(copied, 1)

                for n in range(NS):
                    for c in range(KD):
                        m = n * KD + c
                        if c == 0:
                            pool.wait_ge(c_ev, b * NS + n + 1)
                        pool.wait_ge(h_done, b * NU + m + 1)
                        if m >= RC:
                            pool.wait_ge(y_mm, b * NU + m - RC + 1)
                        nc.gpsimd.tensor_tensor(hc[:, m % RC, :], h[:, m % RH, :], cs[:, n % 2, :], ALU.mult
                                                ).then_inc(hc_done, 1)
                for c in range(KD):
                    pool.wait_ge(y_ev, b * KD + c + 1)
                    nc.gpsimd.tensor_tensor(yt[:, c % 2, :], yt[:, c % 2, :], g[:, c, :], ALU.mult).then_inc(yg_done, 1)
                pool.wait_ge(x_done, (b + 1) * KD)

        @block.tensor
        def _(pe):
            pe.wait_ge(sel_done, 3)
            with pe.Fori(0, B) as b:
                def rows(n):
                    if n >= 2:
                        pe.wait_ge(dB_done, b * NU + (n - 1) * KD)
                        pe.wait_ge(c_ev, b * NS + n - 1)
                    nc.tensor.matmul(pb[n % 2][:], sel[:, n, :], bcb[:], start=True, stop=True).then_inc(b_mm, 1)
                    nc.tensor.matmul(pc[n % 2][:], sel[:, NS + n, :], bcb[:], start=True, stop=True).then_inc(c_mm, 1)
                pe.wait_ge(copied, b * 2 + 1)
                rows(0)
                for n in range(NS):
                    if n + 1 < NS:
                        rows(n + 1)
                    for c in range(KD):
                        m = n * KD + c
                        pe.wait_ge(hc_done, b * NU + m + 1)
                        nc.tensor.matmul(py[:, c, :], env.id32[:], hc[:, m % RC, :], start=(n == 0),
                                         stop=(n == NS - 1)).then_inc(y_mm, 1)
                for c in range(KD):
                    pe.wait_ge(yg_done, b * KD + c + 1)
                    if c >= 2:
                        pe.wait_ge(x_done, b * KD + c - 1)
                    out = pb[c % 2][:].rearrange("p (t e) -> p t e", e=P)
                    for t in range(TPB):
                        last = nc.tensor.transpose(out[:, t, :], yt[:, c % 2, t * P:(t + 1) * P], env.id32[:])
                    last.then_inc(yt_done, 1)
                pe.wait_ge(x_done, (b + 1) * KD)

        @block.scalar
        def _(act):
            act.wait_ge(var_ready, 1)
            root(nc, rstd[:], agg[:, :, 1], env.eps5, P).then_inc(root_done, 1)
            act.wait_ge(a_in, 16)
            nc.scalar.activation(A[:], A[:], ACT.Exp).then_inc(a_done, 1)
            act.wait_ge(a_done, 2)
            with act.Fori(0, B) as b:
                act.wait_ge(z_done, b + 1)
                nc.scalar.activation(g[:], g[:], ACT.Silu).then_inc(g_done, 1)
                act.wait_ge(copied, (b + 1) * 2)
                for n in range(NS):
                    act.wait_ge(c_mm, b * NS + n + 1)
                    if n >= 2:
                        act.wait_ge(hc_done, b * NU + (n - 1) * KD)
                    nc.scalar.activation(cs[:, n % 2, :], pc[n % 2][:], ACT.Copy, scale=1.0 / SB).then_inc(c_ev, 1)
                    for c in range(KD):
                        m = n * KD + c
                        if m >= RA:
                            act.wait_ge(h_done, b * NU + m - RA + 1)
                        nc.scalar.activation(dA[:, m % RA, :], dl[:, c, :], ACT.Exp, scale=A[:, c, n:n + 1]
                                             ).then_inc(dA_done, 1)
                act.wait_ge(x_done, (b + 1) * KD)

        def update(dve, b, c):
            dve.wait_ge(yt_done, b * KD + c + 1)
            dve.wait_ge(g_done, b + 1)
            xv = env.x[:, bass.ds(b * TPB, TPB), c * P:(c + 1) * P]
            nc.vector.scalar_tensor_tensor(out=xv, in0=pb[c % 2][:].rearrange("p (t e) -> p t e", e=P),
                                           scalar=env.th[:, 2:3], in1=xv, op0=ALU.mult, op1=ALU.add
                                           ).then_inc(x_done, 1)

        @block.vector
        def _(dve):
            ch = Chain(dve, own)
            norm_statistics(nc, dve, env, stats, agg, ch, var_ready)
            dve.wait_ge(a_done, 1)
            nc.vector.tensor_scalar(A[:], A[:], -1.0, None, ALU.mult).then_inc(a_done, 1)
            dve.wait_ge(root_done, 1)
            ch.link(nc.vector.reciprocal(rstd[:], rstd[:]))
            with dve.Fori(0, B) as b:
                for c in range(KD):
                    t = b * KD + c
                    last = nc.vector.tensor_scalar(g[:, c, :], at(env.x, t), agg[:, bass.ds(t, 1), 0], rstd[:, bass.ds(t, 1)],
                                                   ALU.subtract, ALU.mult)
                last.then_inc(z_done, 1)

                def inputs(m):
                    n, c = divmod(m, KD)
                    if c == 0:
                        dve.wait_ge(b_mm, b * NS + n + 1)
                    nc.vector.tensor_tensor(dB[:, m % 2, :], at(du, b * KD + c), pb[n % 2][:], ALU.mult
                                            ).then_inc(dB_done, 1)

                def scan(m):
                    dve.wait_ge(dB_done, b * NU + m + 1)
                    dve.wait_ge(dA_done, b * NU + m + 1)
                    if m >= RH:
                        dve.wait_ge(hc_done, b * NU + m - RH + 1)
                    nc.vector.tensor_tensor_scan(h[:, m % RH, :], dA[:, m % RA, :], dB[:, m % 2, :], 0.0, ALU.mult,
                                                 ALU.add).then_inc(h_done, 1)
                inputs(0)
                for m in range(NU):
                    if m + 1 < NU:
                        if m:
                            dve.wait_ge(h_done, b * NU + m)
                        inputs(m + 1)
                    scan(m)
                for c in range(KD):
                    dve.wait_ge(y_mm, b * NU + NU - KD + c + 1)
                    if c >= 2:
                        dve.wait_ge(yt_done, b * KD + c - 1)
                    nc.vector.tensor_tensor(yt[:, c % 2, :], py[:, c, :], at(u, b * KD + c), ALU.add).then_inc(y_ev, 1)
                    if c:
                        update(dve, b, c - 1)
                update(dve, b, KD - 1)
                dve.wait_ge(x_done, (b + 1) * KD)


def layer_xattn2(nc, env):
    SB = 64.0
    with ExitStack() as ctx:
        env.count += 1
        sb, _ = tiles_of(nc, ctx, f"ss{env.count}")
        u, delta, du = sb("u", [P, B * KD, S]), sb("delta", [P, B * KD, S]), sb("du", [P, B * KD, S])
        bc = sb("bc", [P, B, S], F16)
        ssm_prepare_block(nc, env, u, delta, du, bc, SB)
        ssm_scan_block(nc, env, u, delta, du, bc, SB)


def store_block(nc, env, out):
    with ExitStack() as ctx:
        stored = env.sem("out_stored")
        block = ctx.enter_context(nc.Block())

        @block.sync
        def _(sp):
            sp.dma_start(out.rearrange("(t p) d -> p t d", p=P), env.x[:]).then_inc(stored, 16)
            sp.wait_ge(stored, 16)


LAYERS = ("xattn0", "ffn0", "xattn1", "ffn1", "xattn2", "ffn2", "xattn3", "ffn3")


def build_program(nc, ins, out, layers=LAYERS):
    with ExitStack() as stack:
        env = Env(nc, stack, ins)
        env.count = 0
        nc.disable_value_cache = True
        setup_block(nc, env)
        for name in layers:
            {"xattn0": layer_xattn0, "ffn0": lambda n, e: layer_ffn(n, e, 0), "xattn1": layer_xattn1,
             "ffn1": layer_ffn1, "xattn2": layer_xattn2, "ffn2": lambda n, e: layer_ffn(n, e, 2),
             "xattn3": layer_xattn3, "ffn3": lambda n, e: layer_ffn(n, e, 3)}[name](nc, env)
            env.recycle()
        store_block(nc, env, out)


def laid_out(v):
    a = {k: np.asarray(x) for k, x in v.items()}
    t = np.ascontiguousarray
    HS = 256
    rope = np.arange(16).reshape(2, 4, 2).transpose(0, 2, 1).reshape(-1)
    perm = (np.arange(32)[:, None] * 16 + rope[None, :]).reshape(-1)
    kv = np.concatenate([a["L0_xattn_Wk"], a["L0_xattn_Wv"]], axis=1).reshape(C, 16, 2, 32)
    bkv = np.concatenate([a["L0_xattn_bk"], a["L0_xattn_bv"]]).reshape(16, 2, 32)
    return {
        "x": a["x"].reshape(T, D),
        "ctx_t": t(a["ctx_1024"].reshape(T, C).T),
        "g_xattn": a["g_xattn"], "g_ffn": a["g_ffn"],
        "up_weight_t": t(a["L0_ffn_up_weight"].reshape(-1, HS, D).transpose(0, 2, 1)),
        "down_weight_t": t(a["L0_ffn_down_weight"].reshape(D, -1, HS).transpose(1, 2, 0)),
        "up_scale_t": t(a["L0_ffn_up_scale"].reshape(-1, P).T),
        "down_scale": a["L0_ffn_down_scale"], "output_scale": a["L0_ffn_output_scale"],
        "gate_w_t": t(a["L2_ffn_gate_w"].T), "w_gate": a["L2_ffn_w_gate"], "w_up": a["L2_ffn_w_up"],
        "w_down": a["L2_ffn_w_down"],
        "W_router": a["L3_ffn_W_router"],
        "exp_up": np.concatenate([a["L3_ffn_Wsh_up"], a["L3_ffn_Wrt_up"]]),
        "exp_down": np.concatenate([a["L3_ffn_Wsh_down"], a["L3_ffn_Wrt_down"]]),
        "Wq0": a["L0_xattn_Wq"], "bq0": a["L0_xattn_bq"], "Wk0": t(kv[:, :, 0]).reshape(C, D), "bk0": t(bkv[:, 0]).reshape(D),
        "Wv0": t(kv[:, :, 1]).reshape(C, D), "bv0": t(bkv[:, 1]).reshape(D),
        "Wkd0": t(a["L0_xattn_Wkv_dca"][:, :D]), "Wvd0": t(a["L0_xattn_Wkv_dca"][:, D:]),
        "bkd0": t(a["L0_xattn_bkv_dca"][:D]), "bvd0": t(a["L0_xattn_bkv_dca"][D:]),
        "qn_w": a["L0_xattn_qn_w"], "qn_b": a["L0_xattn_qn_b"], "kn_w": a["L0_xattn_kn_w"],
        "kn_b": a["L0_xattn_kn_b"], "kd_w": a["L0_xattn_kn_dca_w"], "kd_b": a["L0_xattn_kn_dca_b"],
        "Wo0": a["L0_xattn_Wo"], "bo0": a["L0_xattn_bo"],
        "Wq1": t(a["L1_xattn_Wq"].T), "bq1": a["L1_xattn_bq"].reshape(P, 1), "Wk1": t(a["L1_xattn_Wk"].T),
        "bk1": a["L1_xattn_bk"].reshape(P, 1),
        "weight1": t(a["L1_ffn_weight"].T).view(np.int32),
        "w_scale1": t(a["L1_ffn_w_scale"][:, 0]), "bias1": a["L1_ffn_bias"],
        "in_proj": t(a["L2_xattn_in_proj_w"].T), "conv_w_t": t(a["L2_xattn_conv_w"].T).reshape(-1),
        "conv_b_t": t(a["L2_xattn_conv_b"].reshape(-1, P).T),
        "x_proj": t(a["L2_xattn_x_proj_w"].T), "dt_w": t(a["L2_xattn_dt_proj_w"].T),
        "dt_b_t": t(a["L2_xattn_dt_proj_b"].reshape(-1, P).T), "A_log_t": a["L2_xattn_A_log"],
        "D_t": t(a["L2_xattn_D"].reshape(-1, P).T),
        "fside": a["fside_BxSx2_0"].reshape(T, 2),
        "Wq3": t(a["L3_xattn_Wq"][:, perm]), "Wk3": t(a["L3_xattn_Wkv"][:, :D][:, perm]),
        "Wv3": t(a["L3_xattn_Wkv"][:, D:]), "Wo3": a["L3_xattn_Wout"], "bo3": a["L3_xattn_bout"],
    }


def kernel(**inputs):
    import concourse.bacc as bacc
    from concourse.bass_utils import run_bass_kernel_spmd

    nc = bacc.Bacc("TRN2", target_bir_lowering=False, num_devices=1)
    arrays, ins = {}, {}
    for name, a in laid_out(inputs).items():
        arrays[f"in_{name}"] = a
        ins[name] = nc.dram_tensor(f"in_{name}", a.shape, mybir.dt.from_np(a.dtype), kind="ExternalInput").ap()
    out = nc.dram_tensor("out_x", (T, D), F32, kind="ExternalOutput").ap()
    build_program(nc, ins, out)
    r = run_bass_kernel_spmd(nc, [arrays], core_ids=[0])
    return r.results[0]["out_x"].reshape(B, S, D)
```

```python
from contextlib import ExitStack

import numpy as np

import concourse.bass as bass
from concourse import mybir

F32 = mybir.dt.float32
F16 = mybir.dt.float16
I8 = mybir.dt.int8
I32 = mybir.dt.int32
U32 = mybir.dt.uint32
ACT = mybir.ActivationFunctionType
ALU = mybir.AluOpType
AX = mybir.AxisListType

P = 128
B, S, D, C = 4, 512, 512, 256
T = B * S
NT = T // P
TPB = S // P
KD = D // P
KC = C // P

SY = 256.0
SC = 64.0
SW = 512.0


class Chain:

    def __init__(self, engine, sem, base=0):
        self.engine, self.sem, self.base, self.n = engine, sem, base, 0

    def link(self, instruction):
        self.n += 1
        instruction.then_inc(self.sem, 1)
        self.engine.wait_ge(self.sem, self.base + self.n)


class Env:

    def __init__(self, nc, stack, ins):
        self.nc, self.ins, self.stack, self.names = nc, ins, stack, 0
        self.sems, self.live = [], ExitStack()

    def sem(self, name):
        self.names += 1
        handle = self.live.enter_context(self.nc.semaphore(f"{name}_{self.names}"))
        self.sems.append(handle)
        return handle

    def dma_sem(self, name):
        self.names += 1
        return self.stack.enter_context(self.nc.semaphore(f"{name}_{self.names}"))

    def recycle(self):
        sems = self.sems
        with self.nc.Block() as block:
            @block.gpsimd
            def _(pool):
                for s in sems:
                    pool.sem_clear(s)
        self.live.close()
        self.sems, self.live = [], ExitStack()

    def keep(self, name, shape, dt):
        return self.stack.enter_context(self.nc.sbuf_tensor(name, shape, dt))


def tiles_of(nc, ctx, tag):
    def sb(name, shape, dt=F32):
        return ctx.enter_context(nc.sbuf_tensor(f"{tag}_{name}", shape, dt))

    def ps(name, shape, dt=F32):
        return ctx.enter_context(nc.psum_tensor(f"{tag}_{name}", shape, dt))
    return sb, ps


def at(tile, t):
    return tile[:, bass.ds(t, 1), :].rearrange("p a d -> p (a d)")


def row_of(ap, n):
    return ap.rearrange("(a n) -> a n", a=1).to_broadcast([P, n])


def setup_block(nc, env):
    env.x = env.keep("x_res", [P, NT, D], F32)
    env.ctx_hi = env.keep("ctx_hi", [P, KC, T], F16)
    env.ctx_lo = env.keep("ctx_lo", [P, KC, T], F16)
    env.th = env.keep("tanh_gates", [P, 8], F32)
    env.id32 = env.keep("ident32", [P, P], F32)
    env.id16 = env.keep("ident16", [P, P], F16)
    env.eps5, env.eps6 = env.keep("eps5", [P, 1], F32), env.keep("eps6", [P, 1], F32)
    ins = env.ins
    with ExitStack() as ctx:
        sb, _ = tiles_of(nc, ctx, "su")
        ctx32 = sb("ctx32", [P, KC, T])
        graw = sb("graw", [P, 8])
        x_in, ctx_in, g_in = env.sem("x_in"), env.sem("ctx_in"), env.sem("gates_in")
        cleared, hi_done, done = env.sem("ident_cleared"), env.sem("ctx_hi_done"), env.sem("setup_done")
        block = ctx.enter_context(nc.Block())

        @block.sync
        def _(sp):
            sp.dma_start(ctx32[:], ins["ctx_t"].rearrange("(k p) t -> p k t", p=P)).then_inc(ctx_in, 16)
            sp.dma_start(graw[:, 0:4], row_of(ins["g_xattn"], 4)).then_inc(g_in, 16)
            sp.dma_start(graw[:, 4:8], row_of(ins["g_ffn"], 4)).then_inc(g_in, 16)
            sp.dma_start(env.x[:], ins["x"].rearrange("(t p) d -> p t d", p=P)).then_inc(x_in, 16)
            sp.wait_ge(x_in, 16)

        @block.gpsimd
        def _(pool):
            nc.gpsimd.memset(env.eps5[:], 1e-5).then_inc(done, 1)
            nc.gpsimd.memset(env.eps6[:], 1e-6).then_inc(done, 1)
            nc.gpsimd.memset(env.id32[:], 0.0).then_inc(cleared, 1)
            nc.gpsimd.memset(env.id16[:], 0.0).then_inc(cleared, 1)
            pool.wait_ge(cleared, 2)
            for m in (env.id32, env.id16):
                nc.gpsimd.affine_select(out=m[:], in_=m[:], compare_op=ALU.not_equal, fill=1.0, base=0,
                                        pattern=[[-1, P]], channel_multiplier=1).then_inc(done, 1)

        @block.scalar
        def _(act):
            act.wait_ge(g_in, 32)
            nc.scalar.activation(env.th[:], graw[:], ACT.Tanh).then_inc(done, 1)
            act.wait_ge(ctx_in, 16)
            nc.scalar.activation(env.ctx_hi[:], ctx32[:], ACT.Copy, scale=SC).then_inc(hi_done, 1)

        @block.vector
        def _(dve):
            dve.wait_ge(hi_done, 1)
            nc.vector.scalar_tensor_tensor(out=env.ctx_lo[:], in0=ctx32[:], scalar=SC, in1=env.ctx_hi[:],
                                           op0=ALU.mult, op1=ALU.subtract).then_inc(done, 1)
            dve.wait_ge(done, 6)


def norm_statistics(nc, dve, env, stats, agg, chain, ready):
    for t in range(NT):
        last = nc.vector.bn_stats(out=stats[:, t, :], in_=env.x[:, t, :])
    chain.link(last)
    for t in range(NT):
        last = nc.vector.bn_aggr(out=agg[:, t, :], in_=stats[:, t, :])
    last.then_inc(ready, 1)


def root(nc, out, var, eps, n):
    return nc.scalar.activation(out, var, ACT.Sqrt, bias=eps[0:n, :])


def norm_block(nc, env, y_hi, y_lo, rows=None):
    NY = 4
    with ExitStack() as ctx:
        env.count += 1
        sb, ps = tiles_of(nc, ctx, f"ln{env.count}")
        stats, agg, rstd = sb("stats", [P, NT, 6]), sb("agg", [P, NT, 2]), sb("rstd", [P, NT])
        y = sb("y", [P, NY, D])
        yt = [ps(f"yt{i}", [P, KD, P]) for i in range(2)]
        own, y_ready, t_ready = env.sem("ln_dve"), env.sem("y_ready"), env.sem("y_transposed")
        hi_ready, lo_ready = env.sem("y_hi_ready"), env.sem("y_lo_ready")
        root_done = env.sem("roots")
        var_ready, row_out = env.sem("variances"), [env.sem(f"y_rows_out{i}") for i in range(NY)]
        block = ctx.enter_context(nc.Block())

        @block.sync
        def _(sp):
            if rows is not None:
                for t in range(NT):
                    sp.wait_ge(y_ready, t + 1)
                    sp.dma_start(rows[t * P:(t + 1) * P, :], y[:, t % NY, :]).then_inc(row_out[t % NY], 16)
                for i in range(NY):
                    sp.wait_ge(row_out[i], 16 * NT // NY)

        @block.vector
        def _(dve):
            chain = Chain(dve, own)
            norm_statistics(nc, dve, env, stats, agg, chain, var_ready)
            dve.wait_ge(root_done, 1)
            chain.link(nc.vector.reciprocal(rstd[:], rstd[:]))

            def normalise(t, u):
                if rows is not None and t >= NY:
                    dve.wait_ge(row_out[t % NY], 16 * (t // NY))
                nc.vector.tensor_scalar(y[:, t % NY, :], env.x[:, t, :], agg[:, t, 0:1],
                                        rstd[:, t:t + 1], ALU.subtract, ALU.mult).then_inc(y_ready, 1)

            def low_half(t, u):
                dve.wait_ge(hi_ready, t + 1)
                nc.vector.scalar_tensor_tensor(out=y_lo[:, :, t * P:(t + 1) * P], in0=yt[u][:], scalar=SY,
                                               in1=y_hi[:, :, t * P:(t + 1) * P], op0=ALU.mult,
                                               op1=ALU.subtract).then_inc(lo_ready, 1)
            for u in range(2):
                normalise(u, u)
            for t in range(0, NT - 2, 2):
                for u in range(2):
                    low_half(t + u, u)
                    normalise(t + u + 2, u)
            for u in range(2):
                low_half(NT - 2 + u, u)

        @block.tensor
        def _(pe):
            def transpose(t, u, reuse):
                pe.wait_ge(y_ready, t + 1)
                if reuse:
                    pe.wait_ge(lo_ready, t - 1)
                for k in range(KD):
                    last = nc.tensor.transpose(yt[u][:, k, :], y[:, t % NY, k * P:(k + 1) * P], env.id32[:])
                last.then_inc(t_ready, 1)
            for u in range(2):
                transpose(u, u, False)
            for t in range(2, NT, 2):
                for u in range(2):
                    transpose(t + u, u, True)

        @block.scalar
        def _(act):
            act.wait_ge(var_ready, 1)
            root(nc, rstd[:], agg[:, :, 1], env.eps5, P).then_inc(root_done, 1)
            for t in range(0, NT, 2):
                for u in range(2):
                    act.wait_ge(t_ready, t + u + 1)
                    nc.scalar.activation(y_hi[:, :, (t + u) * P:(t + u + 1) * P], yt[u][:], ACT.Copy,
                                         scale=SY).then_inc(hi_ready, 1)


SLOTS = 256
ROUND = 12582912.0


def router_block(nc, env, y_hi, y_lo, w_router, n_exp, coef, routing, th, down_scale, renorm, shared):
    gates, slot, step_expert, step_token = routing
    NS = step_expert.shape[1]
    with ExitStack() as ctx:
        env.count += 1
        sb, ps = tiles_of(nc, ctx, f"rt{env.count}")
        sem = env.sem
        w32, w_hi, w_lo = sb("w32", [P, KD, n_exp]), sb("wh", [P, KD, n_exp], F16), sb("wl", [P, KD, n_exp], F16)
        logit, prob = sb("logit", [P, NT, n_exp]), sb("prob", [P, NT, n_exp])
        red, inv = sb("red", [P, NT]), sb("inv", [P, NT])
        top, idx, idxf = sb("top", [P, NT, 8]), sb("idx", [P, NT, 8], U32), sb("idxf", [P, NT, 2])
        ramp, rampi = sb("ramp", [P, n_exp]), sb("rampi", [P, n_exp], I32)
        hot, hot2, tops = sb("hot", [P, NT, n_exp]), sb("hot2", [P, NT, n_exp]), sb("tops", [P, NT, 2])
        cs = sb("cs", [P, 1])
        both, tri, ones = sb("both", [P, NT, n_exp], F16), sb("tri", [P, P], F16), sb("ones", [P, P], F16)
        before, where = sb("before", [P, NT, n_exp]), sb("where", [P, NT, n_exp])
        need, base = sb("need", [P, n_exp]), sb("base", [P, n_exp + 1])
        slotf, tile = sb("slotf", [P, NT, 2]), sb("tile", [P, NT, 2])
        stepi, stepf, owner = sb("stepi", [P, NS], I32), sb("stepf", [P, NS]), sb("owner", [P, NS])
        token, ramp_p = sb("token", [P, NT], I32), sb("ramp_p", [P, P], I32)
        tokenf, ramp_pf = sb("tokenf", [P, NT]), sb("ramp_pf", [P, P])
        hot_p = sb("hot_p", [P, NT * 2, P], F16)
        hot_h = sb("hot_h", [P, NT * 2, 2 * NS], F16)
        p_rank, p_total = ps("rank", [P, NT, n_exp]), ps("total", [P, NT, n_exp])
        p_token = ps("slot_token", [P, 2 * NS])
        tri_clear, tri_done, hot_ready, counted = sem("tri_clear"), sem("tri"), sem("one_hots"), sem("counted")
        placed, inverted = sem("places"), sem("inverted")
        pl = ps("logits", [P, NT, n_exp])
        w_in, hi_done, w_done = env.sem("router_in"), env.sem("router_hi"), env.sem("router_split")
        ramp_done, logit_done = env.sem("ramp"), env.sem("logits")
        shifted, exped, own = env.sem("logits_shifted"), env.sem("logits_exp"), env.sem("router_dve")
        block = ctx.enter_context(nc.Block())

        def over_e(v):
            return v.unsqueeze(2).to_broadcast([P, NT, n_exp])

        @block.sync
        def _(sp):
            sp.dma_start(w32[:], w_router.rearrange("(k p) e -> p k e", p=P)).then_inc(w_in, 16)

        @block.gpsimd
        def _(pool):
            nc.gpsimd.iota(rampi[:], pattern=[[1, n_exp]], base=0, channel_multiplier=0).then_inc(ramp_done, 1)
            nc.gpsimd.iota(stepi[:], pattern=[[1, NS]], base=0, channel_multiplier=0).then_inc(ramp_done, 1)
            nc.gpsimd.iota(token[:], pattern=[[P, NT]], base=0, channel_multiplier=1).then_inc(ramp_done, 1)
            nc.gpsimd.iota(ramp_p[:], pattern=[[1, P]], base=0, channel_multiplier=0).then_inc(ramp_done, 1)
            nc.gpsimd.memset(ones[:], 1.0).then_inc(tri_done, 1)
            nc.gpsimd.memset(tri[:], 1.0).then_inc(tri_clear, 1)
            pool.wait_ge(tri_clear, 1)
            nc.gpsimd.affine_select(out=tri[:], in_=tri[:], compare_op=ALU.is_ge, fill=0.0, base=-1,
                                    pattern=[[1, P]], channel_multiplier=-1).then_inc(tri_done, 1)

        @block.scalar
        def _(act):
            act.wait_ge(w_in, 16)
            nc.scalar.activation(w_hi[:], w32[:], ACT.Copy, scale=SW).then_inc(hi_done, 1)
            act.wait_ge(shifted, 1)
            nc.scalar.activation(prob[:], logit[:], ACT.Exp).then_inc(exped, 1)

        @block.tensor
        def _(pe):
            pe.wait_ge(w_done, 1)
            for t in range(NT):
                n = 0
                for yy, ww in ((y_hi, w_hi), (y_hi, w_lo), (y_lo, w_hi)):
                    for k in range(KD):
                        last = nc.tensor.matmul(pl[:, t, :], yy[:, k, t * P:(t + 1) * P], ww[:, k, :],
                                                start=(n == 0), stop=(n == 3 * KD - 1))
                        n += 1
            last.then_inc(logit_done, 1)
            pe.wait_ge(tri_done, 2)
            pe.wait_ge(hot_ready, 1)
            for out, m in ((p_rank, tri), (p_total, ones)):
                nc.tensor.matmul(out[:], m[:], both[:], start=True, stop=True).then_inc(counted, 1)
            pe.wait_ge(placed, 1)
            for n in range(2 * NT):
                last = nc.tensor.matmul(p_token[:], hot_p[:, n, :], hot_h[:, n, :], start=(n == 0), stop=(n == 2 * NT - 1))
            last.then_inc(inverted, 1)

        @block.vector
        def _(dve):
            c = Chain(dve, own)
            dve.wait_ge(hi_done, 1)
            nc.vector.scalar_tensor_tensor(out=w_lo[:], in0=w32[:], scalar=SW, in1=w_hi[:], op0=ALU.mult,
                                           op1=ALU.subtract).then_inc(w_done, 1)
            dve.wait_ge(ramp_done, 4)
            c.link(nc.vector.tensor_copy(ramp[:], rampi[:]))
            c.link(nc.vector.tensor_scalar(cs[:], th, down_scale, None, ALU.mult))
            c.link(nc.vector.memset(coef[:], 1.0))
            dve.wait_ge(logit_done, 1)
            c.link(nc.vector.tensor_scalar(logit[:], pl[:], 1.0 / (SY * SW), None, ALU.mult))
            c.link(nc.vector.tensor_reduce(red[:], logit[:], AX.X, ALU.max))
            nc.vector.tensor_tensor(logit[:], logit[:], over_e(red[:]), ALU.subtract).then_inc(shifted, 1)
            dve.wait_ge(exped, 1)
            c.link(nc.vector.tensor_reduce(red[:], prob[:], AX.X, ALU.add))
            c.link(nc.vector.reciprocal(inv[:], red[:]))
            c.link(nc.vector.tensor_tensor(prob[:], prob[:], over_e(inv[:]), ALU.mult))
            for t in range(NT):
                last = nc.vector.max(top[:, t, :], prob[:, t, :])
            c.link(last)
            for t in range(NT):
                last = nc.vector.max_index(idx[:, t, :], top[:, t, :], prob[:, t, :])
            c.link(last)
            c.link(nc.vector.tensor_copy(idxf[:], idx[:, :, 0:2]))
            if renorm:
                c.link(nc.vector.tensor_tensor(red[:], top[:, :, 0], top[:, :, 1], ALU.add))
                c.link(nc.vector.reciprocal(inv[:], red[:]))
                for j in range(2):
                    last = nc.vector.tensor_tensor(tops[:, :, j], top[:, :, j], inv[:], ALU.mult)
                    c.link(last)
            else:
                c.link(nc.vector.tensor_copy(tops[:], top[:, :, 0:2]))
            c.link(nc.vector.tensor_scalar(gates[:], tops[:], cs[:], None, ALU.mult))
            for j, h in enumerate((hot, hot2)):
                c.link(nc.vector.tensor_tensor(h[:], ramp[:].unsqueeze(1).to_broadcast([P, NT, n_exp]),
                                               over_e(idxf[:, :, j]), ALU.is_equal))
            nc.vector.tensor_tensor(both[:], hot[:], hot2[:], ALU.add).then_inc(hot_ready, 1)
            c.link(nc.vector.tensor_scalar(coef[:], coef[:], cs[:], None, ALU.mult))
            c.link(nc.vector.tensor_copy(stepf[:], stepi[:]))
            dve.wait_ge(counted, 2)
            c.link(nc.vector.memset(before[:, 0, :], 0.0))
            for t in range(1, NT):
                c.link(nc.vector.tensor_tensor(before[:, t, :], before[:, t - 1, :], p_total[:, t - 1, :], ALU.add))
            c.link(nc.vector.tensor_tensor(need[:], before[:, NT - 1, :], p_total[:, NT - 1, :], ALU.add))
            c.link(nc.vector.tensor_scalar(need[:], need[:], 1.0 / SLOTS, (SLOTS - 1) / 2 / SLOTS, ALU.mult, ALU.add))
            c.link(nc.vector.tensor_scalar(need[:], need[:], ROUND, None, ALU.add))
            c.link(nc.vector.tensor_scalar(need[:], need[:], -ROUND, None, ALU.add))
            c.link(nc.vector.memset(base[:, 0:1], 0.0))
            for e in range(n_exp):
                c.link(nc.vector.tensor_tensor(base[:, e + 1:e + 2], base[:, e:e + 1], need[:, e:e + 1], ALU.add))
            c.link(nc.vector.tensor_tensor(where[:], before[:], p_rank[:], ALU.add))
            c.link(nc.vector.scalar_tensor_tensor(out=where[:], in0=base[:, 0:n_exp].unsqueeze(1).to_broadcast(
                [P, NT, n_exp]), scalar=float(SLOTS), in1=where[:], op0=ALU.mult, op1=ALU.add))
            for j, h in enumerate((hot, hot2)):
                c.link(nc.vector.tensor_tensor(h[:], h[:], where[:], ALU.mult))
                c.link(nc.vector.tensor_reduce(slotf[:, :, j], h[:], AX.X, ALU.add))
            c.link(nc.vector.tensor_copy(slot[:], slotf[:]))
            for i in (tokenf, token), (ramp_pf, ramp_p):
                c.link(nc.vector.tensor_copy(i[0][:], i[1][:]))
            c.link(nc.vector.tensor_scalar(tile[:], slotf[:], 1.0 / P, -(P - 1) / 2 / P, ALU.mult, ALU.add))
            c.link(nc.vector.tensor_scalar(tile[:], tile[:], ROUND, None, ALU.add))
            c.link(nc.vector.tensor_scalar(tile[:], tile[:], -ROUND, None, ALU.add))
            c.link(nc.vector.scalar_tensor_tensor(out=slotf[:], in0=tile[:], scalar=-float(P), in1=slotf[:],
                                                  op0=ALU.mult, op1=ALU.add))

            def spread(v, n):
                return v.rearrange("p t j -> p (t j)").unsqueeze(2).to_broadcast([P, 2 * NT, n])
            c.link(nc.vector.tensor_tensor(hot_p[:], ramp_pf[:].unsqueeze(1).to_broadcast([P, 2 * NT, P]),
                                           spread(slotf[:], P), ALU.is_equal))
            c.link(nc.vector.tensor_tensor(hot_h[:], ramp_pf[:, 0:2 * NS].unsqueeze(1).to_broadcast(
                [P, 2 * NT, 2 * NS]), spread(tile[:], 2 * NS), ALU.is_equal))
            h4 = hot_h[:].rearrange("p (t j) h -> p t (j h)", j=2)
            nc.vector.tensor_tensor(h4, h4, tokenf[:].unsqueeze(2).to_broadcast([P, NT, 4 * NS]), ALU.mult
                                    ).then_inc(placed, 1)
            c.link(nc.vector.memset(owner[:], 0.0))
            for e in range(1, n_exp + 1):
                c.link(nc.vector.scalar_tensor_tensor(out=owner[:], in0=stepf[:], scalar=base[:, e:e + 1], in1=owner[:],
                                                      op0=ALU.is_ge, op1=ALU.add))
            c.link(nc.vector.tensor_scalar(owner[:], owner[:], float(n_exp - 1), float(shared), ALU.min, ALU.add))
            c.link(nc.vector.tensor_copy(step_expert[:], owner[:]))
            dve.wait_ge(inverted, 1)
            c.link(nc.vector.tensor_copy(step_token[:], p_token[:]))


def experts_block(nc, env, y_hi, y_lo, w_up, w_down, kind, n_exp, inner, coef):
    gated, binary = kind == "silu", kind == "sign"
    n_up = 2 if gated else 1
    chunks = [min(P, inner - i) for i in range(0, inner, P)]
    NC = len(chunks)
    parts = 1 if binary else 2
    smid = {"silu": 64.0, "gelu": 256.0, "sign": 4.0}[kind]
    s_up = 1.0 / SY if binary else 1.0 / (SY * SW)
    TB = T // 512
    with ExitStack() as ctx:
        env.count += 1
        sb, ps = tiles_of(nc, ctx, f"ex{env.count}")
        acc = sb("acc", [P, NT, D])
        up32, dn32 = sb("up32", [P, n_up, KD, inner]), sb("dn32", [P, NC, D])
        up16 = [[sb(f"up16_{w}{h}", [P, n_up, KD, inner], F16) for h in range(parts)] for w in range(2)]
        dn16 = [[sb(f"dn16_{w}{h}", [P, NC, D], F16) for h in range(parts)] for w in range(2)]
        mid = sb("mid", [P, 2, 512])
        sil = sb("sil", [P, 2, 512]) if gated else None
        mid_h, mid_l = sb("midh", [P, 2, NC, 512], F16), sb("midl", [P, 2, NC, 512], F16)
        if binary:
            ups = sb("ups", [P, n_exp * NC])
            ups_now = sb("ups_now", [P, 2, NC])
            dsr = sb("dsr", [P, D])
            osc = sb("osc", [P, 1])
        pu = [[ps(f"pu{i}{j}", [P, 512]) for j in range(n_up)] for i in range(2)]
        po = [ps(f"po{i}", [P, D]) for i in range(TPB)]
        w_in, w_read = env.sem("w_in"), env.sem("w_split")
        w_hi, scales_in, acc0 = env.sem("w_hi"), env.sem("scales_in"), env.sem("acc_cleared")
        up_done, mid_done, hi_done = env.sem("up_done"), env.sem("mid_done"), env.sem("mid_hi_done")
        sil_done, lo_done = env.sem("silu_done"), env.sem("mid_lo_done")
        dn_done, acc_done, own = env.sem("down_done"), env.sem("acc_done"), env.sem("expert_dve")
        block = ctx.enter_context(nc.Block())
        EPI = 2
        SPE = TB
        passes = [(0, 0), (1, 0)] if binary else [(0, 0), (1, 0), (0, 1)]
        n_dma = n_up + 1

        @block.sync
        def _(sp):
            if binary:
                sp.dma_start(ups[:], env.ins["up_scale_t"]).then_inc(scales_in, 16)
                sp.dma_start(dsr[:], row_of(env.ins["down_scale"], D)).then_inc(scales_in, 16)
                sp.dma_start(osc[:], row_of(env.ins["output_scale"], 1)).then_inc(scales_in, 16)

            def load(e, first):
                if not first:
                    sp.wait_ge(w_read, 2 * e)
                for j in range(n_up):
                    sp.dma_start(up32[:, j, :, :], w_up[j][bass.ds(e, 1), :, :].rearrange("e (k p) i -> p (e k) i", p=P)
                                 ).then_inc(w_in, 16)
                full = inner // P
                src = w_down[bass.ds(e, 1), 0:full * P, :].rearrange("e (c p) n -> p (e c) n", p=P)
                sp.dma_start(dn32[:, 0:full, :], src).then_inc(w_in, 16)
                if inner % P:
                    src = w_down[bass.ds(e, 1), full * P:inner, :].rearrange("e p n -> p (e n)")
                    sp.dma_start(dn32[0:inner % P, full, :], src).then_inc(w_in, 16)
            load(0, True)
            if n_exp == 2:
                load(1, False)
            else:
                with sp.Fori(1, n_exp) as e:
                    load(e, False)
        if inner % P:
            n_dma += 1

        def pieces(up, dn):
            full = inner // P
            out = [(up[:], 0), (dn[:, 0:full, :], 1)]
            if inner % P:
                out.append((dn[0:inner % P, full, :], 1))
            return [o for o, _ in out]

        @block.gpsimd
        def _(pool):
            nc.gpsimd.memset(acc[:], 0.0).then_inc(acc0, 1)

        @block.scalar
        def _(act):
            def split_hi(e, w, reuse):
                act.wait_ge(w_in, 16 * n_dma * (e + 1))
                if reuse:
                    act.wait_ge(dn_done, TPB * SPE * (e - 1))
                src, dst = pieces(up32, dn32), pieces(up16[w][0], dn16[w][0])
                for s, d in zip(src, dst):
                    if binary:
                        nc.scalar.activation(d, s, ACT.Sign).then_inc(w_hi, 1)
                    else:
                        nc.scalar.activation(d, s, ACT.Copy, scale=SW).then_inc(w_hi, 1)

            def chunk(e, w, tb, c, q, first):
                n = chunks[c]
                s = e * SPE + tb
                g = s * NC + c
                act.wait_ge(up_done, g + 1)
                if gated:
                    if not (first and tb == 0 and c < 2):
                        act.wait_ge(mid_done, g - 1)
                    nc.scalar.activation(sil[0:n, q, :], pu[q][0][0:n, :], ACT.Silu, scale=s_up).then_inc(sil_done, 1)
                    act.wait_ge(mid_done, g + 1)
                else:
                    if not (first and tb == 0 and c < 2):
                        act.wait_ge(lo_done, g - 1)
                    if binary:
                        ins = nc.scalar.activation(mid[0:n, q, :], pu[q][0][0:n, :], ACT.Relu,
                                                   scale=ups_now[0:n, w, c:c + 1])
                    else:
                        ins = nc.scalar.activation(mid[0:n, q, :], pu[q][0][0:n, :], ACT.Gelu, scale=s_up)
                    ins.then_inc(mid_done, 1)
                    act.wait_ge(mid_done, g + 1)
                if not (first and tb < 2):
                    act.wait_ge(dn_done, TPB * (s - 1))
                nc.scalar.activation(mid_h[0:n, tb % 2, c, :], mid[0:n, q, :], ACT.Copy,
                                     scale=smid).then_inc(hi_done, 1)

            def expert(e, w, first, ahead, reuse_next):
                if binary:
                    act.wait_ge(w_read, 2 * (e + 1))
                for tb in range(TB):
                    if tb == 1 and ahead:
                        split_hi(e + 1, 1 - w, reuse_next)
                    for c in range(NC):
                        chunk(e, w, tb, c, (tb * NC + c) % 2, first)
            split_hi(0, 0, False)
            expert(0, 0, True, True, False)
            expert(1, 1, False, n_exp > 2, True)
            if n_exp > 2:
                with act.Fori(1, n_exp // EPI - 1) as i:
                    e = i * EPI
                    expert(e, 0, False, True, True)
                    expert(e + 1, 1, False, True, True)
                expert(n_exp - 2, 0, False, True, True)
                expert(n_exp - 1, 1, False, False, True)

        @block.tensor
        def _(pe):
            def up(e, w, tb, first):
                s = e * SPE + tb
                for c, n in enumerate(chunks):
                    q = (tb * NC + c) % 2
                    g = s * NC + c
                    if not (first and tb == 0 and c < 2):
                        pe.wait_ge(mid_done, g - 1)
                    for j in range(n_up):
                        i = 0
                        for a, h in passes:
                            for k in range(KD):
                                last = nc.tensor.matmul(
                                    pu[q][j][0:n, :], up16[w][h][:, j, k, c * P:c * P + n],
                                    (y_hi, y_lo)[a][:, k, tb * 512:(tb + 1) * 512],
                                    start=(i == 0), stop=(i == len(passes) * KD - 1))
                                i += 1
                    last.then_inc(up_done, 1)

            def down(e, w, tb, first):
                s = e * SPE + tb
                pe.wait_ge(lo_done, NC * (s + 1))
                for j in range(TPB):
                    r = s * TPB + j
                    if not (first and tb == 0):
                        pe.wait_ge(acc_done, r - TPB + 1)
                    i = 0
                    for c, n in enumerate(chunks):
                        for a, h in passes:
                            last = nc.tensor.matmul(po[j][:], (mid_h, mid_l)[a][0:n, tb % 2, c, j * P:(j + 1) * P],
                                                    dn16[w][h][0:n, c, :], start=(i == 0),
                                                    stop=(i == len(passes) * NC - 1))
                            i += 1
                    last.then_inc(dn_done, 1)

            def expert(e, w, first):
                pe.wait_ge(w_read, 2 * (e + 1))
                for tb in range(TB):
                    up(e, w, tb, first)
                    if tb:
                        down(e, w, tb - 1, first)
                down(e, w, TB - 1, first)
            expert(0, 0, True)
            expert(1, 1, False)
            if n_exp > 2:
                with pe.Fori(1, n_exp // EPI) as i:
                    e = i * EPI
                    expert(e, 0, False)
                    expert(e + 1, 1, False)

        @block.vector
        def _(dve):
            n_lo = len(pieces(up32, dn32))
            ch = Chain(dve, own)
            if binary:
                dve.wait_ge(scales_in, 48)
                ch.link(nc.vector.tensor_scalar(ups[:], ups[:], s_up, None, ALU.mult))
                ch.link(nc.vector.tensor_scalar(osc[:], osc[:], coef, None, ALU.mult))
                ch.link(nc.vector.tensor_scalar(dsr[:], dsr[:], osc[:], 1.0 / smid, ALU.mult, ALU.mult))

            def split_lo(e, w):
                dve.wait_ge(w_hi, n_lo * (e + 1))
                if binary:
                    nc.vector.tensor_scalar(ups_now[:, w, :], ups[:, bass.ds(e * NC, NC)], 1.0, None,
                                            ALU.mult).then_inc(w_read, 2)
                    return
                src, his = pieces(up32, dn32), pieces(up16[w][0], dn16[w][0])
                for n, (s, h, d) in enumerate(zip(src, his, pieces(up16[w][1], dn16[w][1]))):
                    last = nc.vector.scalar_tensor_tensor(out=d, in0=s, scalar=SW, in1=h, op0=ALU.mult,
                                                          op1=ALU.subtract)
                last.then_inc(w_read, 2)

            def chunk(e, tb, c):
                n = chunks[c]
                q = (tb * NC + c) % 2
                g = (e * SPE + tb) * NC + c
                if gated:
                    dve.wait_ge(sil_done, g + 1)
                    nc.vector.scalar_tensor_tensor(out=mid[0:n, q, :], in0=pu[q][1][0:n, :], scalar=s_up,
                                                   in1=sil[0:n, q, :], op0=ALU.mult, op1=ALU.mult
                                                   ).then_inc(mid_done, 1)
                dve.wait_ge(hi_done, g + 1)
                nc.vector.scalar_tensor_tensor(out=mid_l[0:n, tb % 2, c, :], in0=mid[0:n, q, :], scalar=smid,
                                               in1=mid_h[0:n, tb % 2, c, :], op0=ALU.mult,
                                               op1=ALU.subtract).then_inc(lo_done, 1)

            def add(e, tb, final):
                for j in range(TPB):
                    t = tb * TPB + j
                    r = (e * SPE + tb) * TPB + j
                    dve.wait_ge(dn_done, r + 1)
                    scale = 1.0 if binary else coef[:, t, bass.ds(e, 1)]
                    nc.vector.scalar_tensor_tensor(out=acc[:, t, :], in0=po[j][:], scalar=scale,
                                                   in1=acc[:, t, :], op0=ALU.mult, op1=ALU.add
                                                   ).then_inc(acc_done, 1)
                    if final:
                        dve.wait_ge(acc_done, r + 1)
                        if binary:
                            ch.link(nc.vector.tensor_tensor(acc[:, t, :], acc[:, t, :], dsr[:], ALU.mult))
                        nc.vector.tensor_tensor(env.x[:, t, :], env.x[:, t, :], acc[:, t, :], ALU.add)

            def expert(e, w, ahead):
                final = not ahead
                for tb in range(TB):
                    for c in range(NC):
                        chunk(e, tb, c)
                    if tb == 1 and ahead:
                        split_lo(e + 1, 1 - w)
                    if tb:
                        add(e, tb - 1, final)
                add(e, TB - 1, final)
            split_lo(0, 0)
            dve.wait_ge(acc0, 1)
            if n_exp > 2:
                with dve.Fori(0, n_exp // EPI - 1) as i:
                    e = i * EPI
                    expert(e, 0, True)
                    expert(e + 1, 1, True)
            expert(n_exp - 2, 0, True)
            expert(n_exp - 1, 1, False)


def routed_block(nc, env, rows, slots_out, w_up, w_down, kind, inner, routing):
    gates, slot, step_expert, step_token = routing
    NS = step_expert.shape[1]
    gated = kind == "silu"
    n_up = 2 if gated else 1
    chunks = [min(P, inner - i) for i in range(0, inner, P)]
    NC, full, rest = len(chunks), inner // P, inner % P
    n_dn = 2 if rest else 1
    smid = {"silu": 64.0, "gelu": 256.0}[kind]
    s_up = 1.0 / (SY * SW)
    HS = SLOTS // P
    passes = [(0, 0), (1, 0), (0, 1)]
    CT = HS
    with ExitStack() as ctx:
        env.count += 1
        sb, ps = tiles_of(nc, ctx, f"mo{env.count}")
        up32, dn32 = sb("up32", [P, 2, n_up, KD, inner]), sb("dn32", [P, 2, NC, D])
        up16 = [sb(f"up16{h}", [P, 2, n_up, KD, inner], F16) for h in "hl"]
        dn16 = [sb(f"dn16{h}", [P, 2, NC, D], F16) for h in "hl"]
        cur, g = sb("cur", [P, 2, HS], I32), sb("g", [P, 2, HS, D])
        y16 = [sb(f"y16{h}", [P, 2, KD, SLOTS], F16) for h in "hl"]
        mid = sb("mid", [P, 2, SLOTS])
        sil = sb("sil", [P, 2, SLOTS]) if gated else None
        mid16 = [sb(f"mid16{h}", [P, 2, NC, SLOTS], F16) for h in "hl"]
        o32 = sb("o32", [P, 2, HS, D])
        cur_slot = sb("cur_slot", [P, 2, CT, 2], I32)
        back = [t[:].rearrange("p w h d -> p (w h) d").rearrange("p (j u) d -> p j u d", j=2) for t in (g, o32)]
        pT = ps("yT", [P, KD, SLOTS])
        pu = [ps(f"pu{i}", [P, n_up, SLOTS]) for i in range(2)]
        po = [ps(f"po{i}", [P, D]) for i in range(HS)]
        sem = env.sem
        up_in, dn_in = ([sem(f"{n}{i}") for i in range(2)] for n in ("up_in", "dn_in"))
        g_in, back_in = ([env.dma_sem(f"{n}{i}") for i in range(2)] for n in ("rows_in", "results_in"))
        up_hi, up_ready, dn_hi, dn_ready = sem("up_hi"), sem("up_split"), sem("dn_hi"), sem("dn_split")
        cur_done, g_go, g_T, yh_done, yl_done = sem("cur"), sem("gather_go"), sem("rows_T"), sem("y_hi"), sem("y_lo")
        up_done, sil_done, mid_done, hi_done, lo_done = (sem("up_done"), sem("silu"), sem("mid"), sem("mid_hi"),
                                                         sem("mid_lo"))
        dn_done, o_done, stored, all_stored = sem("down_done"), sem("out_done"), [sem("out0"), sem("out1")], sem("stored")
        slot_done, added = sem("slot_cur"), sem("x_added")
        add_own, load_go = sem("add_dve"), sem("load_go")
        block = ctx.enter_context(nc.Block())

        def run_steps(engine, step):
            for s in range(2):
                step(s, s, s < 1, s < 2, False)
            with engine.Fori(1, NS // 2 - 1) as i:
                step(i * 2, 0, False, False, False)
                step(i * 2 + 1, 1, False, False, False)
            for s in (NS - 2, NS - 1):
                step(s, s % 2, False, False, s == NS - 1)

        def turns(s, w):
            return s + (2 - w)

        def down_pieces(t, w):
            return [t[:, w, 0:full, :]] + ([t[0:rest, w, full, :]] if rest else [])

        @block.sync
        def _(sp):
            def load(s, w, reuse):
                if reuse:
                    sp.wait_ge(up_ready, n_up * (s - 1))
                    sp.sem_inc(load_go, 1)
                    sp.wait_ge(dn_ready, n_dn * (s - 1))
                    sp.sem_inc(load_go, 1)
                e = sp.value_load(step_expert[0:1, bass.ds(s, 1)], min_val=0, max_val=w_down.shape[0] - 1)
                for j in range(n_up):
                    sp.dma_start(up32[:, w, j, :, :], w_up[j][bass.ds(e, 1), :, :].rearrange("e (k p) i -> p (e k) i", p=P)
                                 ).then_inc(up_in[w], 16)
                sp.dma_start(dn32[:, w, 0:full, :],
                             w_down[bass.ds(e, 1), 0:full * P, :].rearrange("e (c p) n -> p (e c) n", p=P)
                             ).then_inc(dn_in[w], 16)
                if rest:
                    sp.dma_start(dn32[0:rest, w, full, :],
                                 w_down[bass.ds(e, 1), full * P:inner, :].rearrange("e p n -> p (e n)")
                                 ).then_inc(dn_in[w], 16)

            def step(s, w, first, early, last):
                if not (isinstance(s, int) and s + 2 >= NS):
                    load(s + 2, w, True)
                if not first:
                    store(s - 1, 1 - w)

            def store(s, w):
                sp.wait_ge(o_done, HS * (s + 1))
                sp.sem_inc(load_go, 1)
                sp.dma_start(slots_out[bass.ds(s * SLOTS, SLOTS), :].rearrange("(h p) d -> p h d", p=P),
                             o32[:, w, :, :]).then_inc(stored[w], 16)
            for w in range(2):
                sp.sem_inc(stored[w], 16)
            load(0, 0, False)
            load(1, 1, False)
            run_steps(sp, step)
            store(NS - 1, 1)
            sp.wait_ge(stored[0], 16 * (NS // 2 + 1))
            sp.wait_ge(stored[1], 16 * (NS // 2 + 1))
            sp.sem_inc(all_stored, 1)

        @block.gpsimd
        def _(pool):
            def gather(s, w, reuse):
                if reuse:
                    pool.wait_ge(g_T, s - 1)
                    pool.sem_inc(g_go, 1)
                nc.gpsimd.tensor_copy(cur[:, w, :], step_token[:, bass.ds(s * HS, HS)]).then_inc(cur_done, 1)
                pool.wait_ge(cur_done, s + 1)
                pool.sem_inc(g_go, 1)
                for h in range(HS):
                    pool.indirect_dma_start(g[:, w, h, :], None, rows, bass.IndirectOffsetOnAxis(cur[:, w, h:h + 1], 0)
                                            ).then_inc(g_in[w], 16)

            def step(s, w, first, early, last):
                if not last:
                    gather(s + 1, 1 - w, not first)
            gather(0, 0, False)
            run_steps(pool, step)
            pool.wait_ge(all_stored, 1)

            def fetch(i, v, reuse):
                if reuse:
                    pool.wait_ge(added, (2 * i + v - 1) * CT)
                    pool.sem_inc(g_go, 1)
                nc.gpsimd.tensor_copy(cur_slot[:, v, :, :], slot[:, bass.ds((2 * i + v) * CT, CT), :]
                                      ).then_inc(slot_done, 1)
                pool.wait_ge(slot_done, 2 * i + v + 1)
                pool.sem_inc(g_go, 1)
                for u in range(CT):
                    for j in range(2):
                        pool.indirect_dma_start(back[v][:, j, u, :], None, slots_out,
                                                bass.IndirectOffsetOnAxis(cur_slot[:, v, u, j:j + 1], 0)
                                                ).then_inc(back_in[v], 16)
            for v in range(2):
                fetch(0, v, False)
            with pool.Fori(1, NT // (2 * CT)) as i:
                for v in range(2):
                    fetch(i, v, True)

        @block.tensor
        def _(pe):
            def transposes(s, w, reuse):
                pe.wait_ge(g_in[w], 16 * turns(s, w))
                if reuse:
                    pe.wait_ge(yl_done, s)
                for h in range(HS):
                    for k in range(KD):
                        last = nc.tensor.transpose(pT[:, k, h * P:(h + 1) * P], g[:, w, h, k * P:(k + 1) * P], env.id32[:])
                last.then_inc(g_T, 1)

            def up(s, w, first):
                pe.wait_ge(yl_done, s + 1)
                pe.wait_ge(up_ready, n_up * (s + 1))
                for c, n in enumerate(chunks):
                    q = (w * NC + c) % 2
                    gc = s * NC + c
                    if not (first and c < 2):
                        pe.wait_ge(mid_done, gc - 1)
                    for j in range(n_up):
                        i = 0
                        for a, h in passes:
                            for k in range(KD):
                                last = nc.tensor.matmul(pu[q][0:n, j, :], up16[h][:, w, j, k, c * P:c * P + n],
                                                        y16[a][:, w, k, :], start=(i == 0),
                                                        stop=(i == len(passes) * KD - 1))
                                i += 1
                    last.then_inc(up_done, 1)

            def down(s, w, first):
                pe.wait_ge(dn_ready, n_dn * (s + 1))
                pe.wait_ge(lo_done, NC * (s + 1))
                for h in range(HS):
                    if not first:
                        pe.wait_ge(o_done, HS * (s - 1) + h + 1)
                    i = 0
                    for c, n in enumerate(chunks):
                        for a, b in passes:
                            last = nc.tensor.matmul(po[h][:], mid16[a][0:n, w, c, h * P:(h + 1) * P],
                                                    dn16[b][0:n, w, c, :], start=(i == 0),
                                                    stop=(i == len(passes) * NC - 1))
                            i += 1
                    last.then_inc(dn_done, 1)

            def step(s, w, first, early, last):
                if not last:
                    transposes(s + 1, 1 - w, True)
                up(s, w, first)
                if not first:
                    down(s - 1, 1 - w, early)
            transposes(0, 0, False)
            run_steps(pe, step)
            down(NS - 1, 1, False)

        @block.scalar
        def _(act):
            def y_high(s, w, reuse):
                act.wait_ge(g_T, s + 1)
                if reuse:
                    act.wait_ge(up_done, NC * (s - 1))
                nc.scalar.activation(y16[0][:, w, :, :], pT[:], ACT.Copy,
                                     scale=SY).then_inc(yh_done, 1)

            def up_high(s, w, j, reuse):
                act.wait_ge(up_in[w], 8 * n_up * turns(s, w))
                if reuse:
                    act.wait_ge(up_done, NC * (s - 1))
                nc.scalar.activation(up16[0][:, w, j, :, :], up32[:, w, j, :, :], ACT.Copy, scale=SW).then_inc(up_hi, 1)

            def down_high(s, w, reuse):
                act.wait_ge(dn_in[w], 8 * n_dn * turns(s, w))
                if reuse:
                    act.wait_ge(dn_done, HS * (s - 1))
                for a, b in zip(down_pieces(dn16[0], w), down_pieces(dn32, w)):
                    nc.scalar.activation(a, b, ACT.Copy, scale=SW).then_inc(dn_hi, 1)

            def chunk(s, w, c, first, early):
                n, q, gc = chunks[c], (w * NC + c) % 2, s * NC + c
                act.wait_ge(up_done, gc + 1)
                if not (first and c < 2):
                    act.wait_ge(lo_done, gc - 1)
                if gated:
                    nc.scalar.activation(sil[0:n, q, :], pu[q][0:n, 0, :], ACT.Silu, scale=s_up).then_inc(sil_done, 1)
                else:
                    nc.scalar.activation(mid[0:n, q, :], pu[q][0:n, 0, :], ACT.Gelu, scale=s_up).then_inc(mid_done, 1)
                act.wait_ge(mid_done, gc + 1)
                if not early:
                    act.wait_ge(dn_done, HS * (s - 1))
                nc.scalar.activation(mid16[0][0:n, w, c, :], mid[0:n, q, :], ACT.Copy, scale=smid).then_inc(hi_done, 1)

            def results(s, w):
                act.wait_ge(stored[w], 8 * turns(s, w))
                for h in range(HS):
                    act.wait_ge(dn_done, HS * s + h + 1)
                    nc.scalar.activation(o32[:, w, h, :], po[h][:], ACT.Copy).then_inc(o_done, 1)

            def step(s, w, first, early, last):
                if not last:
                    y_high(s + 1, 1 - w, not first)
                for c in range(NC):
                    chunk(s, w, c, first, early)
                    if not last and c < n_up:
                        up_high(s + 1, 1 - w, c, not first)
                if not first:
                    results(s - 1, 1 - w)
                if not last:
                    down_high(s + 1, 1 - w, not first)
            y_high(0, 0, False)
            for j in range(n_up):
                up_high(0, 0, j, False)
            down_high(0, 0, False)
            run_steps(act, step)
            results(NS - 1, 1)

        @block.vector
        def _(dve):
            def y_low(s, w):
                dve.wait_ge(yh_done, s + 1)
                nc.vector.scalar_tensor_tensor(out=y16[1][:, w, :, :], in0=pT[:],
                                               scalar=SY, in1=y16[0][:, w, :, :], op0=ALU.mult, op1=ALU.subtract).then_inc(yl_done, 1)

            def up_low(s, w, j):
                dve.wait_ge(up_hi, n_up * s + j + 1)
                nc.vector.scalar_tensor_tensor(out=up16[1][:, w, j, :, :], in0=up32[:, w, j, :, :], scalar=SW,
                                               in1=up16[0][:, w, j, :, :], op0=ALU.mult, op1=ALU.subtract
                                               ).then_inc(up_ready, 1)

            def down_low(s, w):
                for i, (a, b, c) in enumerate(zip(*(down_pieces(t, w) for t in (dn16[1], dn32, dn16[0])))):
                    dve.wait_ge(dn_hi, n_dn * s + i + 1)
                    nc.vector.scalar_tensor_tensor(out=a, in0=b, scalar=SW, in1=c, op0=ALU.mult,
                                                   op1=ALU.subtract).then_inc(dn_ready, 1)

            def chunk(s, w, c):
                n, q, gc = chunks[c], (w * NC + c) % 2, s * NC + c
                if gated:
                    dve.wait_ge(sil_done, gc + 1)
                    nc.vector.scalar_tensor_tensor(out=mid[0:n, q, :], in0=pu[q][0:n, 1, :], scalar=s_up,
                                                   in1=sil[0:n, q, :], op0=ALU.mult, op1=ALU.mult).then_inc(mid_done, 1)
                dve.wait_ge(hi_done, gc + 1)
                nc.vector.scalar_tensor_tensor(out=mid16[1][0:n, w, c, :], in0=mid[0:n, q, :], scalar=smid,
                                               in1=mid16[0][0:n, w, c, :], op0=ALU.mult, op1=ALU.subtract
                                               ).then_inc(lo_done, 1)

            def step(s, w, first, early, last):
                if not last:
                    y_low(s + 1, 1 - w)
                for c in range(NC):
                    chunk(s, w, c)
                    if not last and c < n_up:
                        up_low(s + 1, 1 - w, c)
                if not last:
                    down_low(s + 1, 1 - w)
            y_low(0, 0)
            for j in range(n_up):
                up_low(0, 0, j)
            down_low(0, 0)
            run_steps(dve, step)
            with dve.Fori(0, NT // (2 * CT)) as i:
                for v in range(2):
                    dve.wait_ge(back_in[v], (i + 1) * (16 * 2 * CT))
                    for n in range(3):
                        for u in range(CT):
                            t = (2 * i + v) * CT + u
                            a, b = back[v][:, 0, u, :], back[v][:, 1, u, :]
                            if n == 0:
                                nc.vector.tensor_scalar(a, a, gates[:, bass.ds(t, 1), 0], None, ALU.mult
                                                        ).then_inc(add_own, 1)
                                continue
                            dve.wait_ge(add_own, (2 * i + v) * (2 * CT) + (n - 1) * CT + u + 1)
                            if n == 1:
                                nc.vector.scalar_tensor_tensor(out=a, in0=b, scalar=gates[:, bass.ds(t, 1), 1], in1=a,
                                                               op0=ALU.mult, op1=ALU.add).then_inc(add_own, 1)
                            else:
                                nc.vector.tensor_tensor(at(env.x, t), at(env.x, t), a, ALU.add).then_inc(added, 1)


def layer_ffn(nc, env, index):
    ins = env.ins
    with ExitStack() as ctx:
        env.count += 1
        y_hi = ctx.enter_context(nc.sbuf_tensor(f"y_hi{env.count}", [P, KD, T], F16))
        y_lo = ctx.enter_context(nc.sbuf_tensor(f"y_lo{env.count}", [P, KD, T], F16))
        rows = None
        if index:
            rows = nc.dram_tensor(f"normalised{index}", (T, D), F32, kind="Internal").ap()
        norm_block(nc, env, y_hi, y_lo, rows)
        th = env.th[:, 4 + index:5 + index]
        if index == 0:
            experts_block(nc, env, y_hi, y_lo, [ins["up_weight_t"]], ins["down_weight_t"], "sign",
                          8, 256, th)
            return
        n_exp, shared = (8, 0) if index == 2 else (16, 2)
        NS = 2 * T // SLOTS + n_exp
        smid = 64.0 if index == 2 else 256.0

        def keep(name, shape, dt):
            return ctx.enter_context(nc.sbuf_tensor(f"{name}{env.count}", shape, dt))
        coef = keep("coef", [P, NT, max(shared, 1)], F32)
        routing = (keep("gates", [P, NT, 2], F32), keep("slot", [P, NT, 2], I32), keep("step_expert", [P, NS], I32),
                   keep("step_token", [P, 2 * NS], I32))
        slots_out = nc.dram_tensor(f"slot_results{index}", (NS * SLOTS, D), F32, kind="Internal").ap()
        router = ins["gate_w_t"] if index == 2 else ins["W_router"]
        router_block(nc, env, y_hi, y_lo, router, n_exp, coef, routing, th, 1.0 / (smid * SW), index == 2, shared)
        if index == 2:
            routed_block(nc, env, rows, slots_out, [ins["w_gate"], ins["w_up"]], ins["w_down"], "silu", 352, routing)
        else:
            experts_block(nc, env, y_hi, y_lo, [ins["exp_up"]], ins["exp_down"], "gelu", shared, 256, coef)
            routed_block(nc, env, rows, slots_out, [ins["exp_up"]], ins["exp_down"], "gelu", 256, routing)


def split_weights_block(nc, env, jobs, clear):
    with ExitStack() as ctx:
        env.count += 1
        sb, _ = tiles_of(nc, ctx, f"sw{env.count}")
        stage = sb("stage", [P, 2, KD, D])
        mean = sb("mean", [P, KD, D // 16])
        w_in = [env.sem("stage_in0"), env.sem("stage_in1")]
        cleared = env.sem("cleared")
        ready, hi_done, lo_done, own = env.sem("w_centred"), env.sem("w_hi"), env.sem("w_lo"), env.sem("split_dve")
        block = ctx.enter_context(nc.Block())

        @block.sync
        def _(sp):
            for n, (w, hi, lo, _) in enumerate(jobs):
                if n >= 2:
                    sp.wait_ge(lo_done, n - 1)
                sp.dma_start(stage[:, n % 2, 0:hi.shape[1], :], w.rearrange("(k p) n -> p k n", p=P)
                             ).then_inc(w_in[n % 2], 16)

        @block.gpsimd
        def _(pool):
            for tile in clear[1:]:
                nc.gpsimd.memset(tile[:], 0.0).then_inc(cleared, 1)
            pool.wait_ge(cleared, len(clear))

        @block.scalar
        def _(act):
            for n, (w, hi, lo, _) in enumerate(jobs):
                act.wait_ge(ready, n + 1)
                nc.scalar.activation(hi[:], stage[:, n % 2, 0:hi.shape[1], :], ACT.Copy,
                                     scale=SW).then_inc(hi_done, 1)

        @block.vector
        def _(dve):
            ch = Chain(dve, own)
            nc.vector.memset(clear[0][:], 0.0).then_inc(cleared, 1)
            for n, (w, hi, lo, hd) in enumerate(jobs):
                kk = hi.shape[1]
                st = stage[:, n % 2, 0:kk, :]
                dve.wait_ge(w_in[n % 2], 16 * (n // 2 + 1))
                if hd:
                    nh = D // hd
                    for k in range(kk):
                        s4 = stage[:, n % 2, k, :].rearrange("p (h d) -> p h d", d=hd)
                        ch.link(nc.vector.tensor_reduce(mean[:, k, 0:nh], s4, AX.X, ALU.add))
                        ch.link(nc.vector.tensor_scalar(mean[:, k, 0:nh], mean[:, k, 0:nh], 1.0 / hd, None, ALU.mult))
                        ch.link(nc.vector.tensor_tensor(s4, s4, mean[:, k, 0:nh].unsqueeze(2).to_broadcast([P, nh, hd]),
                                                        ALU.subtract))
                dve.sem_inc(ready, 1)
                dve.wait_ge(hi_done, n + 1)
                nc.vector.scalar_tensor_tensor(out=lo[:], in0=st, scalar=SW, in1=hi[:], op0=ALU.mult,
                                               op1=ALU.subtract).then_inc(lo_done, 1)


def attention_block(nc, env, w, th, rope):
    H, HD = (32, 16) if rope else (16, 32)
    SK = 2048 // H
    VC = 1024 // H
    GH = P // VC
    NG, NP = H // GH, GH // 2
    DCA = 0 if rope else 16
    MAIN = S - DCA
    TAIL = P - DCA
    SQK, SM, SA = 64.0, 256.0, 64.0
    SCALE = float(HD) ** -0.5
    NPROJ = 3 * TPB + (0 if rope else 1)
    NCH = 2048 // P
    with ExitStack() as ctx:
        env.count += 1
        sb, ps = tiles_of(nc, ctx, f"at{env.count}")
        thc, bo = sb("thc", [P, 1]), sb("bo", [P, D])
        if rope:
            ang, cosr, sinr = sb("ang", [P, NT, 2]), sb("cosr", [P, NT, 8]), sb("sinr", [P, NT, 8])
        else:
            bq, bk, bkt = sb("bq", [P, D]), sb("bk", [P, D]), sb("bkt", [P, D])
            bv, bvt, bvd = sb("bv", [P, D]), sb("bvt", [P, D]), sb("bvd", [P, D])
            qwb, kwb, kdwb = sb("qwb", [P, 2, HD]), sb("kwb", [P, 2, HD]), sb("kdwb", [P, 2, HD])
            bmean = sb("bmean", [P, H])
            mask = sb("mask", [P, 2])
        stats, agg, rstd = sb("stats", [P, NT, 6]), sb("agg", [P, NT, 2]), sb("rstd", [P, NT])
        y_h, y_l = sb("yh", [P, KD, P], F16), sb("yl", [P, KD, P], F16)
        c_h, c_l = sb("ch", [P, KC, S], F16), sb("cl", [P, KC, S], F16)
        if not rope:
            cm = [sb(f"cm{i}", [P, KC, P], F16) for i in range(2)]
            cd = [sb(f"cd{i}", [P, KC, P], F16) for i in range(2)]
        ss = sb("ss", [P, H])
        stq, stk, KT, V = w["stq"], w["stk"], w["KT"], w["V"]
        QT = sb("QT", [P, NCH, S], F16)
        Vd = w.get("Vd")
        nmax = sb("nmax", [P, TPB, H, 1 if rope else 2])
        PTB = 3
        PT = sb("PT", [P, PTB, 2, S])
        y, sq, rot = PT[:, 0, 0, :], PT[:, 1, 0, :], PT[:, 1, 1, :]
        q2 = [PT[:, 0, 1, :], PT[:, 2, 0, :]]
        oT = sb("oT", [P, 1 if rope else 2, S])
        rec = sb("rec", [P, TPB, GH, 2])
        A, tmp = sb("A", [P, TPB, D]), (None if rope else sb("tmp", [P, TPB, GH, HD]))
        a16 = [PT[:, i, 0, :].bitcast(F16).rearrange("p (h k q) -> p h k q", h=2, q=P) for i in range(2)]
        psS = ps("S", [P, 4, 512])
        psB = psS[:, 2:4, :].bitcast(F16).rearrange("p b (c q) -> p (b c) q", q=P)
        psM = ps("M", [P, 2 if rope else 1, 512])
        po = ps("o", [P, S])
        pd = None if rope else ps("od", [P, S])
        pt = ps("t", [P, 4, P])
        psN = [psM[:, 0, :], psM[:, 1, :] if rope else pt[:].rearrange("p j q -> p (j q)")]
        psT = pt if rope else pd[:].rearrange("p (j q) -> p j q", q=P)
        psG = (pt[:].rearrange("p j q -> p (j q)") if rope else psM[:, 0, :]
               ).bitcast(F16).rearrange("p (c s) -> p c s", c=2)
        psP = [psS[:, 0, :], psS[:, 1, :], po[:]]

        sem = env.sem
        const_in, const_done, own = sem("const_in"), sem("const_done"), sem("attn_dve")
        var_ready, root_done, angles, trig = sem("variances"), sem("roots"), sem("angles"), sem("trig")
        zeroed, batch_in = sem("zeroed"), sem("batch_ctx")
        y_ready, yt_done, yh_done, yl_done = sem("y_ready"), sem("y_T"), sem("y_hi"), sem("y_lo")
        proj_done, proj_read = sem("proj_done"), sem("proj_read")
        c_done, ss_done, rt_done = sem("centred"), sem("sumsq"), sem("qk_roots")
        sq_done = sem("squares")
        low_begun = sem("qk_lo_begun")
        q_final, qh_done, st_ready, st_T, st_ev = sem("qk_final"), sem("qk_hi"), sem("stack"), sem("stack_T"), sem("stack_ev")
        s_done, max_done, m_ready = sem("scores"), sem("maxima"), sem("max_rows")
        sT_done, exp_done, pv_done = sem("scoresT"), sem("exp"), sem("pv")
        o_done, oT_done, ot_T, a_done = sem("group_out"), sem("group_ev"), sem("group_T"), sem("attn_norm")
        at_T, ah_done, al_done, wo_done, x_done = sem("attn_T"), sem("attn_hi"), sem("attn_lo"), sem("wo"), sem("x_done")
        block = ctx.enter_context(nc.Block())
        ins = env.ins
        units = [(g, kt, p) for g in range(NG) for kt in range(TPB) for p in range(NP)]
        NU, UPG = len(units), TPB * NP
        NM = H * TPB
        NMG = GH * TPB
        SPU = NM // NU
        ROWS = UPG - (4 if rope else 3)
        AHEAD = NMG + (UPG - ROWS) * SPU
        NST = 8 + NG
        NOUT = 1 if rope else 2
        n_const = 1 + (1 if rope else 12)
        items = [(j, kind) for j in range(TPB) for kind in "qkv"]
        qk = [(j, kind) for j, kind in items if kind != "v"]

        def heads(tile):
            return tile.rearrange("p (h d) -> p h d", d=HD)

        def stack_of(j, kind):
            if kind == "q":
                return stq[:, j, :]
            return stk[0 if rope or j < TPB - 1 else 1][:]

        @block.sync
        def _(sp):
            sp.dma_start(bo[:], row_of(w["bo"], D)).then_inc(const_in, 16)
            if rope:
                sp.dma_start(ang[:], ins["fside"].rearrange("(t p) a -> p t a", p=P)).then_inc(const_in, 16)
            else:
                for tile, name in ((bq, "bq0"), (bk, "bk0"), (bkt, "bkd0"), (bv, "bv0"), (bvd, "bvd0"), (bvt, "bv0")):
                    sp.dma_start(tile[:], row_of(ins[name], D)).then_inc(const_in, 16)
                for tile, n in ((qwb, "qn"), (kwb, "kn"), (kdwb, "kd")):
                    sp.dma_start(tile[:, 0, :], row_of(ins[n + "_w"], HD)).then_inc(const_in, 16)
                    sp.dma_start(tile[:, 1, :], row_of(ins[n + "_b"], HD)).then_inc(const_in, 16)

        @block.gpsimd
        def _(pool):
            ch = Chain(pool, zeroed)
            n = 0
            if rope:
                nc.gpsimd.memset(V[:, :, :, HD:HD + 1], 1.0).then_inc(zeroed, 1)
                nc.gpsimd.memset(stk[0][:].rearrange("p (h s) -> p h s", s=SK)[:, :, 3 * HD:3 * HD + 1],
                                 SM).then_inc(zeroed, 1)
                n += 2
            else:
                nc.gpsimd.memset(mask[:], 1.0).then_inc(zeroed, 1)
                for tile in cm + cd:
                    nc.gpsimd.memset(tile[:], 0.0).then_inc(zeroed, 1)
                n += 5
                pool.wait_ge(zeroed, n)
                nc.gpsimd.affine_select(out=mask[:, 0:1], in_=mask[:, 0:1], compare_op=ALU.is_ge, fill=0.0,
                                        base=TAIL - 1, pattern=[[0, 1]], channel_multiplier=-1).then_inc(zeroed, 1)
                nc.gpsimd.affine_select(out=mask[:, 1:2], in_=mask[:, 1:2], compare_op=ALU.is_ge, fill=0.0,
                                        base=-TAIL, pattern=[[0, 1]], channel_multiplier=1).then_inc(zeroed, 1)
                nc.gpsimd.memset(V[:, 0:TPB - 1, :, HD:HD + 1], 1.0).then_inc(zeroed, 1)
                sv = [s[:].rearrange("p (h s) -> p h s", s=SK) for s in stk]
                nc.gpsimd.memset(sv[0][:, :, 3 * HD:3 * HD + 1], SM).then_inc(zeroed, 1)
                n += 4
                pool.wait_ge(zeroed, n)
                one = mask[:, 0:1].unsqueeze(2).to_broadcast([P, H, 1])
                oned = mask[:, 1:2].unsqueeze(2).to_broadcast([P, H, 1])
                nc.gpsimd.tensor_copy(V[:, TPB - 1, :, HD:HD + 1], one).then_inc(zeroed, 1)
                nc.gpsimd.tensor_copy(Vd[:, :, HD:HD + 1], oned).then_inc(zeroed, 1)
                for i in range(2):
                    nc.gpsimd.tensor_scalar(sv[1][:, :, 3 * HD + i:3 * HD + i + 1], (one, oned)[i], SM, None,
                                            ALU.mult).then_inc(zeroed, 1)
                n += 4
            pool.wait_ge(zeroed, n)
            with pool.Fori(0, B) as b:
                nc.gpsimd.memset(stq[:].rearrange("p j (h s) -> p j h s", s=SK)[:, :, :, 3 * HD:3 * HD + NOUT],
                                 0.0).then_inc(batch_in, 1)
                for i, (src, dst) in enumerate(((env.ctx_hi, c_h), (env.ctx_lo, c_l))):
                    nc.gpsimd.tensor_copy(dst[:], src[:, :, bass.ds(b * S, S)]).then_inc(batch_in, 1)
                    if not rope:
                        nc.gpsimd.tensor_copy(cm[i][:, :, 0:TAIL], src[:, :, bass.ds(b * S + S - P, TAIL)]
                                              ).then_inc(batch_in, 1)
                        nc.gpsimd.tensor_copy(cd[i][:, :, TAIL:P], src[:, :, bass.ds(b * S + MAIN, DCA)]
                                              ).then_inc(batch_in, 1)
                for m in range(2 * TPB):
                    j, kind = divmod(m, 2)
                    pool.wait_ge(qh_done, (b * 8 + m + 1) * 2)
                    pool.sem_inc(low_begun, 1)
                    dst = stack_of(j, "kq"[kind]).rearrange("p (h s) -> p h s", s=SK)
                    lo = 2 * HD if kind else HD
                    nc.gpsimd.tensor_tensor(dst[:, :, lo:lo + HD], heads(q2[kind]), dst[:, :, 0:HD],
                                            ALU.subtract).then_inc(st_ready, 1)
                pool.wait_ge(st_T, (b + 1) * NST)
        n_zero = 2 if rope else 13
        n_ctx = 1 + (2 if rope else 6)

        @block.tensor
        def _(pe):
            pe.wait_ge(zeroed, n_zero)
            with pe.Fori(0, B) as b:
                def project(out, acts, weights):
                    total = sum(3 * wh.shape[1] for (_, _), (wh, _) in zip(acts, weights))
                    n = 0
                    for (ah, al), (wh, wl) in zip(acts, weights):
                        for aa, ww in ((ah, wh), (al, wh), (ah, wl)):
                            for k in range(wh.shape[1]):
                                last = nc.tensor.matmul(out, aa(k), ww[:, k, :], start=(n == 0), stop=(n == total - 1))
                                n += 1
                    return last

                def projection(j, kind):
                    n = 3 * j + "kvq".index(kind)
                    if n >= 3:
                        pe.wait_ge(proj_read, b * NPROJ + n - 2)
                    out = psP[n % 3]
                    whole = (lambda k: c_h[:, k, j * P:(j + 1) * P], lambda k: c_l[:, k, j * P:(j + 1) * P])
                    main = (lambda k: cm[0][:, k, :], lambda k: cm[1][:, k, :])
                    dca = (lambda k: cd[0][:, k, :], lambda k: cd[1][:, k, :])
                    if kind == "q":
                        pe.wait_ge(yl_done, b * TPB + j + 1)
                        last = project(out, [(lambda k: y_h[:, k, :], lambda k: y_l[:, k, :])], [w["q"]])
                    elif rope or j < TPB - 1:
                        last = project(out, [whole], [w[kind]])
                    elif kind == "k":
                        last = project(out, [main, dca], [w["k"], w["kd"]])
                    else:
                        last = project(out, [main], [w["v"]])
                    last.then_inc(proj_done, 1)

                def stack_transposes(m):
                    j, kind = divmod(m, 2)
                    pe.wait_ge(st_ready, b * 8 + m + 1)
                    if m:
                        pe.wait_ge(st_ev, b * NST + m)
                    for c in range(NCH):
                        last = nc.tensor.transpose(psB[:, c, :], stack_of(j, "kq"[kind])[:, c * P:(c + 1) * P],
                                                   env.id16[:])
                    last.then_inc(st_T, 1)

                def y_transposes(j):
                    pe.wait_ge(y_ready, b * TPB + j + 1)
                    for k in range(KD):
                        last = nc.tensor.transpose(pt[:, k, :], y[:, k * P:(k + 1) * P], env.id32[:])
                    last.then_inc(yt_done, 1)

                y_transposes(0)
                pe.wait_ge(batch_in, (b + 1) * n_ctx)
                projection(0, "k")
                projection(0, "v")
                for j in range(TPB):
                    projection(j, "q")
                    if j + 1 < TPB:
                        y_transposes(j + 1)
                        projection(j + 1, "k")
                        projection(j + 1, "v")
                    if j:
                        stack_transposes(2 * j - 1)
                    stack_transposes(2 * j)
                if not rope:
                    pe.wait_ge(proj_read, b * NPROJ + 10)
                    project(psS[:, 0, :], [(lambda k: cd[0][:, k, :], lambda k: cd[1][:, k, :])],
                            [w["vd"]]).then_inc(proj_done, 1)
                stack_transposes(2 * TPB - 1)

                def scores(n):
                    g, i, j = n // NMG, n // TPB % GH, n % TPB
                    if n >= 2:
                        pe.wait_ge(max_done, b * NM + n - 1)
                    h = g * GH + i
                    nc.tensor.matmul(psN[n % 2], QT[:, h if SK == P else h // 2, j * P:(j + 1) * P],
                                     KT[:, h, :], start=True, stop=True).then_inc(s_done, 1)

                def maxima_rows(g, issued):
                    pe.wait_ge(m_ready, b * NG + g + 1)
                    if not rope:
                        pe.wait_ge(max_done, b * NM + issued)
                    elif g >= 2:
                        pe.wait_ge(a_done, b * NG + g - 1)
                    for j in range(TPB):
                        for c in range(2):
                            last = nc.tensor.transpose(psG[:, c, j * P:(j + 1) * P],
                                                       stq[:, j, (2 * g + c) * P:(2 * g + c + 1) * P], env.id16[:])
                    last.then_inc(st_T, 1)

                def scores_t(n):
                    g, kt, p = units[n]
                    if kt == 0 and p == 0:
                        pe.wait_ge(st_ev, b * NST + 8 + g + 1)
                    if n >= 2:
                        pe.wait_ge(exp_done, b * NU + n - 1)
                    for i in range(2):
                        h = g * GH + 2 * p + i
                        last = nc.tensor.matmul(psS[:, 2 * (n % 2) + i, :], KT[:, h, kt * P:(kt + 1) * P],
                                                QT[:, h if SK == P else h // 2, :], start=True, stop=True)
                    last.then_inc(sT_done, 1)

                def group_transposes(g, i):
                    if i == 0:
                        pe.wait_ge(oT_done, b * NG + g + 1)
                    r = g * NOUT + i
                    if r:
                        pe.wait_ge(a_done, b * NG * NOUT + r)
                    for j in range(TPB):
                        last = nc.tensor.transpose(psT[:, j, :], oT[:, i, j * P:(j + 1) * P], env.id32[:])
                    last.then_inc(ot_T, 1)

                def values(n):
                    g, kt, p = units[n]
                    if kt == 0 and p == 0 and g:
                        pe.wait_ge(oT_done, b * NG + g)
                    pe.wait_ge(exp_done, b * NU + n + 1)
                    for i in range(2):
                        r = 2 * p + i
                        h = g * GH + r
                        last = nc.tensor.matmul(po[r * VC:(r + 1) * VC, :], V[:, kt, h, :],
                                                PT[:, n % PTB, i, :], start=(kt == 0), stop=(kt == TPB - 1))
                    if not rope and kt == TPB - 1:
                        if g:
                            pe.wait_ge(a_done, (b * NG + g) * NOUT)
                        for i in range(2):
                            last = nc.tensor.matmul(pd[i * VC:(i + 1) * VC, :], Vd[:, g * GH + i, :],
                                                    PT[:, n % PTB, i, :], start=True, stop=True)
                    last.then_inc(pv_done, 1)

                pe.wait_ge(st_ev, b * NST + 8)
                pe.wait_ge(proj_read, (b + 1) * NPROJ)
                for n in range(AHEAD):
                    scores(n)
                maxima_rows(0, AHEAD)
                scores_t(0)
                for n in range(NU):
                    g, u = divmod(n, UPG)
                    if n + 1 < NU:
                        scores_t(n + 1)
                    issued = min(NM, AHEAD + n * SPU)
                    more = range(issued, min(NM, issued + SPU))
                    rows = u == ROWS and g + 1 < NG
                    if rows and not rope:
                        maxima_rows(g + 1, issued)
                    if n:
                        values(n - 1)
                    if rows and more and not rope:
                        pe.wait_ge(st_ev, b * NST + 8 + g + 2)
                    for i in more:
                        scores(i)
                    if rows and rope:
                        maxima_rows(g + 1, issued)
                    for i in range(NOUT):
                        if g and u == 3 - NOUT + i:
                            group_transposes(g - 1, i)
                values(NU - 1)
                for i in range(NOUT):
                    group_transposes(NG - 1, i)
                def attention_transposes(j):
                    if j >= 2:
                        pe.wait_ge(al_done, b * TPB + j - 1)
                    out = (pt, psM[:, 0, :].rearrange("p (k q) -> p k q", q=P))[j % 2]
                    for k in range(KD):
                        last = nc.tensor.transpose(out[:, k, :], A[:, j, k * P:(k + 1) * P], env.id32[:])
                    last.then_inc(at_T, 1)
                pe.wait_ge(a_done, (b + 1) * NG * NOUT)
                attention_transposes(0)
                for j in range(TPB):
                    if j + 1 < TPB:
                        attention_transposes(j + 1)
                    pe.wait_ge(al_done, b * TPB + j + 1)
                    if j >= 2:
                        pe.wait_ge(x_done, b * TPB + j - 1)
                    a = a16[j % 2]
                    project(psS[:, j % 2, :], [(lambda k: a[:, 0, k, :], lambda k: a[:, 1, k, :])],
                            [w["o"]]).then_inc(wo_done, 1)
                pe.wait_ge(x_done, (b + 1) * TPB)

        @block.scalar
        def _(act):
            act.wait_ge(var_ready, 1)
            root(nc, rstd[:], agg[:, :, 1], env.eps5, P).then_inc(root_done, 1)
            if rope:
                act.wait_ge(angles, 1)
                act.wait_ge(zeroed, n_zero)
                nc.scalar.activation(sinr[:], sinr[:], ACT.Sin).then_inc(trig, 1)
                nc.scalar.activation(cosr[:], cosr[:], ACT.Sin).then_inc(trig, 1)
            act.wait_ge(zeroed, n_zero)
            with act.Fori(0, B) as b:
                def evacuate(m):
                    j, kind = divmod(m, 2)
                    act.wait_ge(st_T, b * NST + m + 1)
                    if kind:
                        nc.scalar.activation(QT[:, :, j * P:(j + 1) * P], psB, ACT.Copy).then_inc(st_ev, 1)
                    elif SK == P:
                        nc.scalar.activation(KT[:, :, j * P:(j + 1) * P], psB, ACT.Copy).then_inc(st_ev, 1)
                    else:
                        kv = KT[:].rearrange("p (c two) s -> p c two s", two=2)
                        nc.scalar.activation(kv[0:64, :, 0, j * P:(j + 1) * P], psB[0:64], ACT.Copy)
                        nc.scalar.activation(kv[64:P, :, 1, j * P:(j + 1) * P], psB[64:P], ACT.Copy).then_inc(st_ev, 1)

                def group_rows(g):
                    act.wait_ge(st_T, b * NST + 8 + g + 1)
                    nc.scalar.activation(QT[:, 2 * g:2 * g + 2, :], psG, ACT.Copy).then_inc(st_ev, 1)

                def y_high(j):
                    act.wait_ge(yt_done, b * TPB + j + 1)
                    if j:
                        act.wait_ge(proj_done, b * NPROJ + 3 * j)
                    nc.scalar.activation(y_h[:], pt[:], ACT.Copy, scale=SY).then_inc(yh_done, 1)

                y_high(0)
                for j in range(TPB):
                    for i, kind in enumerate("kq"):
                        n = 2 * j + i
                        if not rope:
                            act.wait_ge(c_done, b * 8 + n + 1)
                            nc.scalar.activation(sq, q2[i], ACT.Square).then_inc(sq_done, 1)
                            act.wait_ge(ss_done, b * 8 + n + 1)
                            nc.scalar.activation(ss[:], ss[:], ACT.Sqrt, bias=env.eps6[:, :],
                                                 scale=1.0 / HD).then_inc(rt_done, 1)
                        if n:
                            evacuate(n - 1)
                        act.wait_ge(q_final, b * 8 + n + 1)
                        dst = stack_of(j, kind).rearrange("p (h s) -> p h s", s=SK)
                        nc.scalar.activation(dst[:, :, 0:HD], heads(q2[i]), ACT.Copy).then_inc(qh_done, 1)
                        second = 2 * HD if kind == "k" else HD
                        nc.scalar.activation(dst[:, :, second:second + HD], heads(q2[i]), ACT.Copy
                                             ).then_inc(qh_done, 1)
                        if kind == "k" and j + 1 < TPB:
                            y_high(j + 1)
                evacuate(2 * TPB - 1)
                group_rows(0)

                def group_out(g):
                    act.wait_ge(pv_done, b * NU + (g + 1) * UPG)
                    if g:
                        act.wait_ge(ot_T, (b * NG + g) * NOUT)
                    if rope:
                        nc.scalar.activation(oT[:, 0, :], po[:], ACT.Copy).then_inc(oT_done, 1)
                    else:
                        nc.scalar.activation(oT[:, 0, :], po[:], ACT.Copy)
                        nc.scalar.activation(oT[:, 1, :], pd[:], ACT.Copy).then_inc(oT_done, 1)
                for n in range(NU):
                    g, u = divmod(n, UPG)
                    act.wait_ge(sT_done, b * NU + n + 1)
                    if n >= PTB:
                        act.wait_ge(pv_done, b * NU + n - PTB + 1)
                    nc.scalar.activation(PT[:, n % PTB, :, :], psS[:, 2 * (n % 2):2 * (n % 2) + 2, :], ACT.Exp,
                                         scale=SCALE / (SQK * SQK)).then_inc(exp_done, 1)
                    if u == 0 and g:
                        group_out(g - 1)
                    if u == ROWS and g + 1 < NG:
                        group_rows(g + 1)
                group_out(NG - 1)
                for j in range(TPB):
                    act.wait_ge(at_T, b * TPB + j + 1)
                    if j >= 2:
                        act.wait_ge(wo_done, b * TPB + j - 1)
                    src = (pt, psM[:, 0, :].rearrange("p (k q) -> p k q", q=P))[j % 2]
                    nc.scalar.activation(a16[j % 2][:, 0, :, :], src[:, :, :], ACT.Copy, scale=SA).then_inc(ah_done, 1)
                act.wait_ge(x_done, (b + 1) * TPB)

        @block.vector
        def _(dve):
            ch = Chain(dve, own)
            norm_statistics(nc, dve, env, stats, agg, ch, var_ready)
            dve.wait_ge(const_in, 16 * n_const if not rope else 32)
            if rope:
                for a in range(2):
                    for f in range(4):
                        ch.link(nc.vector.tensor_scalar(sinr[:, :, 4 * a + f], ang[:, :, a],
                                                        float(np.float32(10000.0) ** np.float32(-f / 4)), None, ALU.mult))
                two_pi = float(2 * np.pi)
                big = 12582912.0
                ch.link(nc.vector.tensor_scalar(cosr[:], sinr[:], float(np.pi / 2), None, ALU.add))
                for r in (sinr, cosr):
                    k = sq[:, 0:NT * 8].rearrange("p (t e) -> p t e", e=8)
                    ch.link(nc.vector.tensor_scalar(k, r[:], 1.0 / two_pi, None, ALU.mult))
                    ch.link(nc.vector.tensor_scalar(k, k, big, None, ALU.add))
                    ch.link(nc.vector.tensor_scalar(k, k, -big, None, ALU.add))
                    ch.link(nc.vector.scalar_tensor_tensor(out=r[:], in0=k, scalar=-two_pi, in1=r[:], op0=ALU.mult,
                                                           op1=ALU.add))
                    ch.link(nc.vector.tensor_scalar(r[:], r[:], float(np.float32(3.1415925)), float(np.float32(-3.1415925)),
                                                    ALU.min, ALU.max))
                dve.sem_inc(angles, 1)
            else:
                dve.wait_ge(zeroed, n_zero)
                for tile in (bq, bk, bkt):
                    t3 = heads(tile[:])
                    ch.link(nc.vector.tensor_reduce(bmean[:], t3, AX.X, ALU.add))
                    ch.link(nc.vector.tensor_scalar(bmean[:], bmean[:], 1.0 / HD, None, ALU.mult))
                    ch.link(nc.vector.tensor_tensor(t3, t3, bmean[:].unsqueeze(2).to_broadcast([P, H, HD]), ALU.subtract))
                for tile in (qwb, kwb, kdwb):
                    ch.link(nc.vector.tensor_scalar(tile[:], tile[:], SQK, None, ALU.mult))
                ch.link(nc.vector.tensor_scalar(bkt[:], bkt[:], mask[:, 1:2], None, ALU.mult))
                ch.link(nc.vector.scalar_tensor_tensor(out=bkt[:], in0=bk[:], scalar=mask[:, 0:1], in1=bkt[:],
                                                       op0=ALU.mult, op1=ALU.add))
                ch.link(nc.vector.tensor_scalar(kdwb[:], kdwb[:], mask[:, 1:2], None, ALU.mult))
                ch.link(nc.vector.scalar_tensor_tensor(out=kdwb[:], in0=kwb[:], scalar=mask[:, 0:1], in1=kdwb[:],
                                                       op0=ALU.mult, op1=ALU.add))
                ch.link(nc.vector.tensor_scalar(bvt[:], bvt[:], mask[:, 0:1], None, ALU.mult))
                ch.link(nc.vector.tensor_scalar(bvd[:], bvd[:], mask[:, 1:2], None, ALU.mult))
            ch.link(nc.vector.tensor_scalar(thc[:], th, 1.0 / (SA * SW), None, ALU.mult))
            ch.link(nc.vector.tensor_scalar(bo[:], bo[:], th, None, ALU.mult))
            dve.wait_ge(root_done, 1)
            ch.link(nc.vector.reciprocal(rstd[:], rstd[:]))
            if rope:
                dve.wait_ge(trig, 2)
            dve.wait_ge(zeroed, n_zero)
            before = ch.n
            per = 8 * 3 + NG + TPB if rope else 8 * 4 + NG * 3 + TPB
            with dve.Fori(0, B) as b:
                c = Chain(dve, own, before + b * per)

                def projected(j, kind):
                    n = 3 * j + "kvq".index(kind)
                    dve.wait_ge(proj_done, b * NPROJ + n + 1)
                    out = psP[n % 3]
                    s = 1.0 / ((SY if kind == "q" else SC) * SW)
                    if kind == "v":
                        dst = V[:, j, :, 0:HD]
                        if rope:
                            nc.vector.tensor_scalar(dst, heads(out), s, None, ALU.mult).then_inc(proj_read, 1)
                        else:
                            bias = bv if j < TPB - 1 else bvt
                            nc.vector.scalar_tensor_tensor(out=dst, in0=heads(out), scalar=s, in1=heads(bias[:]),
                                                           op0=ALU.mult, op1=ALU.add).then_inc(proj_read, 1)
                        return
                    m = 2 * j + "kq".index(kind)
                    q32 = q2[m % 2]
                    if m >= 2:
                        dve.wait_ge(st_ready, b * 8 + m - 1)
                    if rope:
                        ins_ = nc.vector.tensor_scalar(q32, out, s * SQK, None, ALU.mult)
                        ins_.then_inc(proj_read, 1)
                        dve.wait_ge(proj_read, b * NPROJ + n + 1)
                        v = q32.rearrange("p (h a two f) -> p (h a) two f", a=2, two=2, f=4)
                        o = rot.rearrange("p (h a two f) -> p (h a) two f", a=2, two=2, f=4)
                        o2 = sq.rearrange("p (h a two f) -> p (h a) two f", a=2, two=2, f=4)

                        def trig_of(tile):
                            t = tile[:, bass.ds(b * TPB + j, 1), :].rearrange("p a (x f) -> p (a x) f", f=4)
                            return t.unsqueeze(1).to_broadcast([P, H, 2, 4])

                        def four(ap):
                            return ap.rearrange("p (h a) f -> p h a f", a=2)
                        for i in range(2):
                            nc.vector.tensor_tensor(four(o[:, :, i, :]), four(v[:, :, i, :]), trig_of(cosr), ALU.mult)
                            last = nc.vector.tensor_tensor(four(o2[:, :, i, :]), four(v[:, :, 1 - i, :]), trig_of(sinr),
                                                           ALU.mult)
                        c.link(last)
                        c.link(nc.vector.tensor_tensor(v[:, :, 0, :], o[:, :, 0, :], o2[:, :, 0, :], ALU.subtract))
                        c.link(nc.vector.tensor_tensor(v[:, :, 1, :], o[:, :, 1, :], o2[:, :, 1, :], ALU.add))
                    else:
                        bias = bq if kind == "q" else (bk if j < TPB - 1 else bkt)
                        wb = qwb if kind == "q" else (kwb if j < TPB - 1 else kdwb)
                        nc.vector.scalar_tensor_tensor(out=q32, in0=out, scalar=s, in1=bias[:], op0=ALU.mult,
                                                       op1=ALU.add).then_inc(proj_read, 1)
                        dve.wait_ge(proj_read, b * NPROJ + n + 1)
                        dve.sem_inc(c_done, 1)
                        dve.wait_ge(sq_done, b * 8 + m + 1)
                        nc.vector.tensor_reduce(ss[:], heads(sq), AX.X, ALU.add).then_inc(ss_done, 1)
                        dve.wait_ge(rt_done, b * 8 + m + 1)
                        c.link(nc.vector.reciprocal(ss[:], ss[:]))
                        q3 = heads(q32)
                        c.link(nc.vector.tensor_tensor(q3, q3, ss[:].unsqueeze(2).to_broadcast([P, H, HD]), ALU.mult))
                        for i, op in ((0, ALU.mult), (1, ALU.add)):
                            c.link(nc.vector.tensor_tensor(q3, q3, wb[:, i:i + 1, :].to_broadcast([P, H, HD]), op))
                    dve.sem_inc(q_final, 1)

                def normalise(j):
                    t = b * TPB + j
                    if j:
                        dve.wait_ge(yt_done, b * TPB + j)
                    nc.vector.tensor_scalar(y, at(env.x, t), agg[:, bass.ds(t, 1), 0], rstd[:, bass.ds(t, 1)],
                                            ALU.subtract, ALU.mult).then_inc(y_ready, 1)

                def maximum(n):
                    g, i, j = n // NMG, n // TPB % GH, n % TPB
                    h = g * GH + i
                    dve.wait_ge(s_done, b * NM + n + 1)
                    sc = psN[n % 2]
                    last = nc.vector.tensor_reduce(nmax[:, j, h:h + 1, 0], sc[:, 0:MAIN], AX.X, ALU.max)
                    if not rope:
                        last = nc.vector.tensor_reduce(nmax[:, j, h:h + 1, 1], sc[:, MAIN:S], AX.X, ALU.max)
                    last.then_inc(max_done, 1)

                def maxima_rows(g):
                    dve.wait_ge(max_done, b * NM + (g + 1) * NMG)
                    rows = stq[:].rearrange("p j (h s) -> p j h s", s=SK)
                    for i in range(NOUT):
                        last = nc.vector.tensor_scalar(rows[:, :, g * GH:(g + 1) * GH, 3 * HD + i],
                                                       nmax[:, :, g * GH:(g + 1) * GH, i], -1.0 / SM, None, ALU.mult)
                    last.then_inc(m_ready, 1)

                def group_output(g, i):
                    dve.wait_ge(ot_T, (b * NG + g) * NOUT + i + 1)
                    av = A[:, :, g * GH * HD:(g + 1) * GH * HD].rearrange("p j (h d) -> p j h d", d=HD)
                    v = psT[:, :, :].rearrange("p j (h c) -> p j h c", c=VC)
                    c.link(nc.vector.reciprocal(rec[:, :, :, i], v[:, :, :, HD]))
                    spread = rec[:, :, :, i:i + 1].to_broadcast([P, TPB, GH, HD])
                    out = av if i == 0 else tmp[:]
                    product = nc.vector.tensor_tensor(out, v[:, :, :, 0:HD], spread, ALU.mult)
                    if i == 0:
                        product.then_inc(a_done, 1)
                        return
                    c.link(product)
                    nc.vector.tensor_tensor(av, av, tmp[:], ALU.add).then_inc(a_done, 1)

                normalise(0)
                for j in range(TPB):
                    dve.wait_ge(yh_done, b * TPB + j + 1)
                    nc.vector.scalar_tensor_tensor(out=y_l[:], in0=pt[:], scalar=SY, in1=y_h[:], op0=ALU.mult,
                                                   op1=ALU.subtract).then_inc(yl_done, 1)
                    projected(j, "k")
                    projected(j, "v")
                    if j + 1 < TPB:
                        normalise(j + 1)
                    projected(j, "q")
                if not rope:
                    dve.wait_ge(proj_done, (b + 1) * NPROJ)
                    nc.vector.scalar_tensor_tensor(out=Vd[:, :, 0:HD], in0=heads(psS[:, 0, :]),
                                                   scalar=1.0 / (SC * SW), in1=heads(bvd[:]), op0=ALU.mult,
                                                   op1=ALU.add).then_inc(proj_read, 1)
                for n in range(AHEAD):
                    if n == NMG:
                        maxima_rows(0)
                    maximum(n)
                for n in range(NU):
                    g, u = divmod(n, UPG)
                    if u == ROWS and g + 1 < NG:
                        maxima_rows(g + 1)
                    issued = AHEAD + n * SPU
                    for i in range(issued, min(NM, issued + SPU)):
                        maximum(i)
                    for i in range(NOUT):
                        if g and u == 3 - NOUT + i:
                            group_output(g - 1, i)
                for i in range(NOUT):
                    group_output(NG - 1, i)

                def attention_low(j):
                    dve.wait_ge(ah_done, b * TPB + j + 1)
                    src = (pt, psM[:, 0, :].rearrange("p (k q) -> p k q", q=P))[j % 2]
                    nc.vector.scalar_tensor_tensor(out=a16[j % 2][:, 1, :, :], in0=src[:, :, :], scalar=SA,
                                                   in1=a16[j % 2][:, 0, :, :], op0=ALU.mult,
                                                   op1=ALU.subtract).then_inc(al_done, 1)
                attention_low(0)
                for j in range(TPB):
                    if j + 1 < TPB:
                        attention_low(j + 1)
                    t = b * TPB + j
                    dve.wait_ge(wo_done, b * TPB + j + 1)
                    c.link(nc.vector.scalar_tensor_tensor(out=at(env.x, t), in0=psS[:, j % 2, :], scalar=thc[:],
                                                          in1=at(env.x, t), op0=ALU.mult, op1=ALU.add))
                    nc.vector.tensor_tensor(at(env.x, t), at(env.x, t), bo[:], ALU.add).then_inc(x_done, 1)
                assert c.n == per
                dve.wait_ge(x_done, (b + 1) * TPB)


def layer_attention(nc, env, index):
    ins = env.ins
    with ExitStack() as ctx:
        env.count += 1

        def pair(name, kk):
            return tuple(ctx.enter_context(nc.sbuf_tensor(f"{name}_{h}{env.count}", [P, kk, D], F16)) for h in "hl")
        if index == 0:
            names = [("q", "Wq0", KD, 32), ("k", "Wk0", KC, 32), ("kd", "Wkd0", KC, 32), ("v", "Wv0", KC, 0),
                     ("vd", "Wvd0", KC, 0), ("o", "Wo0", KD, 0)]
        else:
            names = [("q", "Wq3", KD, 0), ("k", "Wk3", KC, 0), ("v", "Wv3", KC, 0), ("o", "Wo3", KD, 0)]
        w = {key: pair(key, kk) for key, _, kk, _ in names}
        heads = 32 if index == 3 else 16

        def tile(name, shape, dt):
            return ctx.enter_context(nc.sbuf_tensor(f"{name}{env.count}", shape, dt))
        w["stq"] = tile("stq", [P, TPB, 2048], F16)
        w["stk"] = [tile(f"stk{i}_", [P, 2048], F16) for i in range(1 if index == 3 else 2)]
        w["KT"] = tile("KT", [P, heads, S], F16)
        w["V"] = tile("V", [P, TPB, heads, 1024 // heads], F32)
        clear = [w["V"], w["stq"], *w["stk"]]
        if index == 3:
            clear.append(w["KT"])
        else:
            w["Vd"] = tile("Vd", [P, heads, 1024 // heads], F32)
            clear.append(w["Vd"])
        split_weights_block(nc, env, [(ins[n], *w[key], hd) for key, n, _, hd in names], clear)
        w["bo"] = ins["bo0" if index == 0 else "bo3"]
        attention_block(nc, env, w, env.th[:, index:index + 1], index == 3)


def layer_xattn0(nc, env):
    layer_attention(nc, env, 0)


def layer_xattn3(nc, env):
    layer_attention(nc, env, 3)


def layer_xattn1(nc, env):
    ins = env.ins
    SQ, SAT = 64.0, 4096.0
    with ExitStack() as ctx:
        env.count += 1
        sb, ps = tiles_of(nc, ctx, f"x1{env.count}")
        y_hi, y_lo = sb("y_hi", [P, KD, T], F16), sb("y_lo", [P, KD, T], F16)
        norm_block(nc, env, y_hi, y_lo)
        w32, w_h, w_l = sb("w32", [P, 2, KC, P]), sb("wh", [P, 2, KC, P], F16), sb("wl", [P, 2, KC, P], F16)
        bias, thc = sb("bias", [P, 2]), sb("thc", [P, 1])
        qk, qk_h, qk_l = sb("qk", [P, 2, S]), sb("qkh", [P, 2, S], F16), sb("qkl", [P, 2, S], F16)
        nm, tot, prob = sb("nm", [P, 2]), sb("tot", [P, 2]), sb("prob", [P, 2, S])
        at_h, at_l = sb("ath", [P, TPB, S], F16), sb("atl", [P, TPB, S], F16)
        pq, pe_, pt, po = ps("q", [P, 2, S]), ps("e", [P, 2, S]), ps("t", [P, 2, 4, P]), ps("o", [P, 2, S])
        sem = env.sem
        w_in, w_hi, w_done, out_go, own = sem("w_in"), sem("w_hi"), sem("w_done"), sem("out_go"), sem("x1_dve")
        q_done, q_ev, qh_done, ql_done = sem("q_done"), sem("q_ev"), sem("q_hi"), sem("q_lo")
        e_done, m_done, p_done, n_done = sem("energy"), sem("rowmax"), sem("exp"), sem("normed")
        t_done, th_done, tl_done, o_done, x_done = sem("att_T"), sem("att_hi"), sem("att_lo"), sem("out"), sem("x_done")
        block = ctx.enter_context(nc.Block())

        @block.sync
        def _(sp):
            for i, n in enumerate(("Wq1", "Wk1")):
                sp.dma_start(w32[:, i, :, :], ins[n].rearrange("(k p) d -> p k d", p=P)).then_inc(w_in, 16)
            for i, n in enumerate(("bq1", "bk1")):
                sp.dma_start(bias[:, i:i + 1], ins[n]).then_inc(w_in, 16)

        @block.tensor
        def _(pe):
            pe.wait_ge(w_done, 1)
            with pe.Fori(0, B) as b:
                for i in range(2):
                    n = 0
                    for wt, c in ((w_h, env.ctx_hi), (w_h, env.ctx_lo), (w_l, env.ctx_hi)):
                        for k in range(KC):
                            last = nc.tensor.matmul(pq[:, i, :], wt[:, i, k, :], c[:, k, bass.ds(b * S, S)], start=(n == 0),
                                                    stop=(n == 3 * KC - 1))
                            n += 1
                last.then_inc(q_done, 1)
                pe.wait_ge(ql_done, b + 1)

                def energy(j):
                    if j >= 2:
                        pe.wait_ge(p_done, b * TPB + j - 1)
                    for n, (q, k) in enumerate(((qk_h, qk_h), (qk_l, qk_h), (qk_h, qk_l))):
                        last = nc.tensor.matmul(pe_[:, j % 2, :], q[:, 0, j * P:(j + 1) * P], k[:, 1, :],
                                                start=(n == 0), stop=(n == 2))
                    last.then_inc(e_done, 1)
                energy(0)
                for j in range(TPB):
                    if j + 1 < TPB:
                        energy(j + 1)
                    pe.wait_ge(n_done, b * TPB + j + 1)
                    if j >= 2:
                        pe.wait_ge(tl_done, b * TPB + j - 1)
                    for k in range(4):
                        last = nc.tensor.transpose(pt[:, j % 2, k, :], prob[:, j % 2, k * P:(k + 1) * P], env.id32[:])
                    last.then_inc(t_done, 1)
                pe.wait_ge(tl_done, (b + 1) * TPB)
                for j in range(TPB):
                    if j >= 2:
                        pe.wait_ge(x_done, b * TPB + j - 1)
                    pe.sem_inc(out_go, 1)
                    n = 0
                    for y, a in ((y_hi, at_h), (y_lo, at_h), (y_hi, at_l)):
                        for k in range(KD):
                            last = nc.tensor.matmul(po[:, j % 2, :], y[:, k, bass.ds(b * S + j * P, P)], a[:, k, :],
                                                    start=(n == 0), stop=(n == 3 * KD - 1))
                            n += 1
                    last.then_inc(o_done, 1)
                pe.wait_ge(x_done, (b + 1) * TPB)

        @block.scalar
        def _(act):
            act.wait_ge(w_in, 64)
            nc.scalar.activation(w_h[:], w32[:], ACT.Copy, scale=SW).then_inc(w_hi, 1)
            with act.Fori(0, B) as b:
                act.wait_ge(q_done, b + 1)
                for i in range(2):
                    last = nc.scalar.activation(qk[:, i, :], pq[:, i, :], ACT.Identity, bias=bias[:, i:i + 1],
                                                scale=1.0 / (SC * SW))
                last.then_inc(q_ev, 1)
                act.wait_ge(q_ev, b + 1)
                nc.scalar.activation(qk_h[:], qk[:], ACT.Copy, scale=SQ).then_inc(qh_done, 1)

                def exponentials(j):
                    act.wait_ge(m_done, b * TPB + j + 1)
                    if j >= 2:
                        act.wait_ge(t_done, b * TPB + j - 1)
                    nc.scalar.activation(prob[:, j % 2, :], pe_[:, j % 2, :], ACT.Exp, bias=nm[:, j % 2:j % 2 + 1],
                                         scale=1.0 / (SQ * SQ), accum_out=tot[:, j % 2:j % 2 + 1]).then_inc(p_done, 1)

                def high(j):
                    act.wait_ge(t_done, b * TPB + j + 1)
                    nc.scalar.activation(at_h[:, :, j * P:(j + 1) * P], pt[:, j % 2, :, :], ACT.Copy,
                                         scale=SAT).then_inc(th_done, 1)
                exponentials(0)
                for j in range(1, TPB):
                    exponentials(j)
                    high(j - 1)
                high(TPB - 1)
                act.wait_ge(x_done, (b + 1) * TPB)

        @block.vector
        def _(dve):
            ch = Chain(dve, own)
            dve.wait_ge(w_hi, 1)
            nc.vector.scalar_tensor_tensor(out=w_l[:], in0=w32[:], scalar=SW, in1=w_h[:], op0=ALU.mult,
                                           op1=ALU.subtract).then_inc(w_done, 1)
            ch.link(nc.vector.tensor_scalar(thc[:], env.th[:, 1:2], 1.0 / (SY * SAT), None, ALU.mult))
            base, per = ch.n, 2 * TPB
            with dve.Fori(0, B) as b:
                c = Chain(dve, own, base + b * per)
                dve.wait_ge(qh_done, b + 1)
                nc.vector.scalar_tensor_tensor(out=qk_l[:], in0=qk[:], scalar=SQ, in1=qk_h[:], op0=ALU.mult,
                                               op1=ALU.subtract).then_inc(ql_done, 1)

                def maximum(j):
                    dve.wait_ge(e_done, b * TPB + j + 1)
                    c.link(nc.vector.tensor_reduce(nm[:, j % 2:j % 2 + 1], pe_[:, j % 2, :], AX.X, ALU.max))
                    nc.vector.tensor_scalar(nm[:, j % 2:j % 2 + 1], nm[:, j % 2:j % 2 + 1], -1.0 / (SQ * SQ), None,
                                            ALU.mult).then_inc(m_done, 1)

                def low(j):
                    dve.wait_ge(th_done, b * TPB + j + 1)
                    nc.vector.scalar_tensor_tensor(out=at_l[:, :, j * P:(j + 1) * P], in0=pt[:, j % 2, :, :], scalar=SAT,
                                                   in1=at_h[:, :, j * P:(j + 1) * P], op0=ALU.mult,
                                                   op1=ALU.subtract).then_inc(tl_done, 1)
                maximum(0)
                for j in range(TPB):
                    if j + 1 < TPB:
                        if j:
                            dve.wait_ge(p_done, b * TPB + j)
                        maximum(j + 1)
                    dve.wait_ge(p_done, b * TPB + j + 1)
                    c.link(nc.vector.reciprocal(tot[:, j % 2:j % 2 + 1], tot[:, j % 2:j % 2 + 1]))
                    nc.vector.tensor_scalar(prob[:, j % 2, :], prob[:, j % 2, :], tot[:, j % 2:j % 2 + 1], None,
                                            ALU.mult).then_inc(n_done, 1)
                    if j:
                        low(j - 1)
                low(TPB - 1)
                for j in range(TPB):
                    dve.wait_ge(o_done, b * TPB + j + 1)
                    xt = at(env.x, b * TPB + j)
                    nc.vector.scalar_tensor_tensor(out=xt, in0=po[:, j % 2, :], scalar=thc[:], in1=xt, op0=ALU.mult,
                                                   op1=ALU.add).then_inc(x_done, 1)
                assert c.n == per
                dve.wait_ge(x_done, (b + 1) * TPB)


def layer_ffn1(nc, env):
    ins = env.ins
    BIG = 12582912.0
    with ExitStack() as ctx:
        env.count += 1
        sb, ps = tiles_of(nc, ctx, f"f1{env.count}")
        w8, w16 = sb("w8", [P, KD, D // 4], I32), sb("w16", [P, KD, D], F16)
        ws, bias = sb("ws", [P, D]), sb("bias", [P, D])
        stats, agg, rstd = sb("stats", [P, NT, 6]), sb("agg", [P, NT, 2]), sb("rstd", [P, NT])
        y, q = sb("y", [P, 2, D]), sb("q", [P, 2, D], F16)
        qT = sb("qT", [P, 2, KD, P], F16)
        sc, inv, least = sb("sc", [P, 2]), sb("inv", [P, 2]), sb("least", [P, 2])
        o32, o16 = sb("o32", [P, 2, D]), sb("o16", [P, 2, D], F16)
        pt = [ps(f"t{i}", [P, KD, P], F16) for i in range(2)]
        po = [ps(f"o{i}", [P, D]) for i in range(2)]
        sem = env.sem
        w_in, c_in, w_done, own = sem("w_in"), sem("consts_in"), sem("w_done"), sem("f1_dve")
        var_ready, root_done = sem("variances"), sem("roots")
        q_ready, t_done, t_ev, o_done, o_read = sem("q_ready"), sem("q_T"), sem("q_T_ev"), sem("out"), sem("out_read")
        scaled, biased = sem("scaled"), sem("biased")
        block = ctx.enter_context(nc.Block())

        @block.sync
        def _(sp):
            sp.dma_start(w8[:], ins["weight1"].rearrange("(k p) n -> p k n", p=P)).then_inc(w_in, 16)
            sp.dma_start(ws[:], row_of(ins["w_scale1"], D)).then_inc(c_in, 16)
            sp.dma_start(bias[:], row_of(ins["bias1"], D)).then_inc(c_in, 16)

        @block.gpsimd
        def _(pool):
            pool.wait_ge(c_in, 32)
            for t in range(NT):
                u = t % 2
                pool.wait_ge(scaled, t + 1)
                nc.gpsimd.tensor_tensor(o16[:, u, :], o32[:, u, :], bias[:], ALU.add).then_inc(biased, 1)

        @block.scalar
        def _(act):
            act.wait_ge(w_in, 16)
            nc.scalar.activation(w16[:], w8[:].bitcast(I8), ACT.Copy).then_inc(w_done, 1)
            act.wait_ge(var_ready, 1)
            root(nc, rstd[:], agg[:, :, 1], env.eps5, P).then_inc(root_done, 1)
            for t in range(NT):
                act.wait_ge(t_done, t + 1)
                nc.scalar.activation(qT[:, t % 2, :, :], pt[t % 2][:], ACT.Copy).then_inc(t_ev, 1)

        @block.tensor
        def _(pe):
            pe.wait_ge(w_done, 1)

            def product(t):
                u = t % 2
                pe.wait_ge(t_ev, t + 1)
                if t >= 2:
                    pe.wait_ge(scaled, t - 1)
                for k in range(KD):
                    last = nc.tensor.matmul(po[u][:], qT[:, u, k, :], w16[:, k, :], start=(k == 0), stop=(k == KD - 1))
                last.then_inc(o_done, 1)
            for t in range(NT):
                u = t % 2
                pe.wait_ge(q_ready, t + 1)
                if t >= 2:
                    pe.wait_ge(t_ev, t - 1)
                for k in range(KD):
                    last = nc.tensor.transpose(pt[u][:, k, :], q[:, u, k * P:(k + 1) * P], env.id16[:])
                last.then_inc(t_done, 1)
                if t:
                    product(t - 1)
            product(NT - 1)

        @block.vector
        def _(dve):
            c = Chain(dve, own)
            norm_statistics(nc, dve, env, stats, agg, c, var_ready)
            dve.wait_ge(root_done, 1)
            c.link(nc.vector.reciprocal(rstd[:], rstd[:]))
            dve.wait_ge(c_in, 32)

            def output(t):
                u = t % 2
                dve.wait_ge(o_done, t + 1)
                if t >= 2:
                    dve.wait_ge(biased, t - 1)
                nc.vector.scalar_tensor_tensor(out=o32[:, u, :], in0=po[u][:], scalar=sc[:, u:u + 1], in1=ws[:],
                                               op0=ALU.mult, op1=ALU.mult).then_inc(scaled, 1)

            def residual(t):
                u = t % 2
                dve.wait_ge(biased, t + 1)
                nc.vector.scalar_tensor_tensor(out=env.x[:, t, :], in0=o16[:, u, :], scalar=env.th[:, 5:6],
                                               in1=env.x[:, t, :], op0=ALU.mult, op1=ALU.add)
            for t in range(NT):
                u = t % 2
                c.link(nc.vector.tensor_scalar(y[:, u, :], env.x[:, t, :], agg[:, t, 0:1], rstd[:, t:t + 1],
                                               ALU.subtract, ALU.mult))
                if t >= 2:
                    output(t - 2)
                nc.vector.tensor_reduce(least[:, u:u + 1], y[:, u, :], AX.X, ALU.min)
                c.link(nc.vector.tensor_reduce(inv[:, u:u + 1], y[:, u, :], AX.X, ALU.max))
                c.link(nc.vector.scalar_tensor_tensor(out=inv[:, u:u + 1], in0=least[:, u:u + 1], scalar=-1.0,
                                                      in1=inv[:, u:u + 1], op0=ALU.mult, op1=ALU.max))
                if t >= 2:
                    dve.wait_ge(scaled, t - 1)
                c.link(nc.vector.tensor_scalar(sc[:, u:u + 1], inv[:, u:u + 1], 1e-7, 1.0 / 127.0, ALU.max, ALU.mult))
                c.link(nc.vector.reciprocal(inv[:, u:u + 1], sc[:, u:u + 1]))
                c.link(nc.vector.tensor_scalar(y[:, u, :], y[:, u, :], inv[:, u:u + 1], BIG, ALU.mult, ALU.add))
                if t >= 2:
                    dve.wait_ge(t_done, t - 1)
                nc.vector.tensor_scalar(q[:, u, :], y[:, u, :], -BIG, 127.0, ALU.add, ALU.min).then_inc(q_ready, 1)
                if t >= 3:
                    residual(t - 3)
            output(NT - 2)
            residual(NT - 3)
            output(NT - 1)
            residual(NT - 2)
            residual(NT - 1)


LOG1P = (0.33333319832513, 0.2000383545232939, 0.14116977575002837, 0.1343377665106373)


def ssm_prepare_block(nc, env, u, delta, du, bc, SB):
    ins = env.ins
    TAPS, R, NS = 4, 16, 16
    XD = R + 2 * NS
    c1, c2, c3, c4 = LOG1P
    with ExitStack() as ctx:
        env.count += 1
        sb, ps = tiles_of(nc, ctx, f"sp{env.count}")
        w32, cw = sb("w32", [P, KC, D]), sb("cw", [P, TAPS, D])
        wt = sb("wt", [P, KC, D])
        w_h, w_l = sb("wh", [P, TAPS, KC, D], F16), sb("wl", [P, TAPS, KC, D], F16)
        cb, dtb, dd = sb("cb", [P, KD]), sb("dtb", [P, KD]), sb("dd", [P, KD])
        xp, dtw = sb("xp", [P, KD, XD]), sb("dtw", [R, D])
        xd = sb("xd", [XD, S])
        t1, t2, two = sb("t1", [P, 2, S]), sb("t2", [P, 2, S]), sb("two", [P, 1])
        pu = [ps(f"u{i}", [P, S]) for i in range(2)]
        px = ps("x", [P, S])
        pd = ps("d", [P, KD, S])
        sem = env.sem
        c_in, w_ready, w_hi, w_done = sem("ssm_in"), sem("tap"), sem("tap_hi"), sem("tap_lo")
        zero, u_mm, u_ev, x_mm, x_ev, bch, bcl = (sem(n) for n in ("bc_zero", "u_mm", "u_ev", "x_mm", "x_ev", "bc_hi", "bc_lo"))
        d_mm, own, abs_in, z_done, s_done, q_done, du_done = (sem(n) for n in (
            "dt_mm", "sp_dve", "dt_raw", "exp_abs", "s_ready", "q_ready", "du_done"))
        inv_done, delta_done = sem("inverse"), sem("delta_done")
        block = ctx.enter_context(nc.Block())

        @block.sync
        def _(sp):
            sp.dma_start(w32[:], ins["in_proj"].rearrange("(k p) e -> p k e", p=P)).then_inc(c_in, 16)
            sp.dma_start(cw[:], row_of(ins["conv_w_t"], TAPS * D).rearrange("p (j e) -> p j e", e=D)).then_inc(c_in, 16)
            for tile, n in ((cb, "conv_b_t"), (dtb, "dt_b_t"), (dd, "D_t"), (dtw, "dt_w")):
                sp.dma_start(tile[:], ins[n]).then_inc(c_in, 16)
            sp.dma_start(xp[:], ins["x_proj"].rearrange("(k p) r -> p k r", p=P)).then_inc(c_in, 16)

        @block.gpsimd
        def _(pool):
            nc.gpsimd.memset(bc[:], 0.0).then_inc(zero, 1)
            nc.gpsimd.memset(two[:], 2.0).then_inc(zero, 1)
            pool.wait_ge(c_in, 112)
            for b in range(B):
                for h in range(2):
                    sl = slice(4 * b + 2 * h, 4 * b + 2 * h + 2)
                    pool.wait_ge(delta_done, 2 * b + h + 1)
                    nc.gpsimd.tensor_tensor(du[:, sl, :], delta[:, sl, :], u[:, sl, :], ALU.mult).then_inc(du_done, 1)
                    pool.wait_ge(du_done, 2 * b + h + 1)
                    pool.wait_ge(x_mm, b + 1)
                    for c in (2 * h, 2 * h + 1):
                        nc.gpsimd.tensor_scalar(u[:, 4 * b + c, :], u[:, 4 * b + c, :], dd[:, c:c + 1], None, ALU.mult)

        @block.tensor
        def _(pe):
            pe.wait_ge(w_done, TAPS)

            def convolution(b, c):
                m = b * KD + c
                if m >= 2:
                    pe.wait_ge(u_ev, m - 1)
                n = 0
                for j in range(TAPS - 1, -1, -1):
                    shift = TAPS - 1 - j
                    for ww, cc in ((w_h, env.ctx_hi), (w_h, env.ctx_lo), (w_l, env.ctx_hi)):
                        for k in range(KC):
                            last = nc.tensor.matmul(pu[m % 2][:, shift:S], ww[:, j, k, c * P:(c + 1) * P],
                                                    cc[:, k, b * S:(b + 1) * S - shift], start=(n == 0),
                                                    stop=(n == TAPS * 3 * KC - 1))
                            n += 1
                last.then_inc(u_mm, 1)
            for c in range(KD):
                convolution(0, c)
            for b in range(B):
                pe.wait_ge(u_ev, (b + 1) * KD)
                if b:
                    pe.wait_ge(bcl, b)
                for k in range(KD):
                    last = nc.tensor.matmul(px[0:XD, :], xp[:, k, :], u[:, b * KD + k, :], start=(k == 0), stop=(k == KD - 1))
                last.then_inc(x_mm, 1)
                if b + 1 < B:
                    convolution(b + 1, 0)
                pe.wait_ge(x_ev, b + 1)
                if b:
                    pe.wait_ge(abs_in, 2 * b)
                for c in range(KD):
                    last = nc.tensor.matmul(pd[:, c, :], dtw[:, c * P:(c + 1) * P], xd[0:R, :], start=True, stop=True)
                last.then_inc(d_mm, 1)
                if b + 1 < B:
                    for c in range(1, KD):
                        convolution(b + 1, c)

        @block.scalar
        def _(act):
            for j in range(TAPS):
                act.wait_ge(w_ready, j + 1)
                nc.scalar.activation(w_h[:, j, :, :], wt[:], ACT.Copy, scale=SW).then_inc(w_hi, 1)
            act.wait_ge(c_in, 112)
            act.wait_ge(zero, 2)

            def silu(b, c):
                m = b * KD + c
                act.wait_ge(u_mm, m + 1)
                nc.scalar.activation(u[:, m, :], pu[m % 2][:], ACT.Silu, bias=cb[:, c:c + 1],
                                     scale=1.0 / (SC * SW)).then_inc(u_ev, 1)

            def inverse(b, h):
                i = 2 * b + h
                act.wait_ge(abs_in, i + 1)
                z = du[:, 4 * b + 2 * h:4 * b + 2 * h + 2, :]
                nc.scalar.activation(z, delta[:, 4 * b + 2 * h:4 * b + 2 * h + 2, :], ACT.Abs).then_inc(z_done, 1)
                act.wait_ge(z_done, 2 * i + 1)
                nc.scalar.activation(z, z, ACT.Exp, scale=-1.0).then_inc(z_done, 1)
                act.wait_ge(z_done, 2 * i + 2)
                if i:
                    act.wait_ge(delta_done, i)
                nc.scalar.activation(t1[:], z, ACT.Ln, bias=two[:]).then_inc(inv_done, 1)
                act.wait_ge(inv_done, 2 * i + 1)
                nc.scalar.activation(t1[:], t1[:], ACT.Exp, scale=-1.0).then_inc(inv_done, 1)

            def square(b, h):
                act.wait_ge(s_done, 2 * b + h + 1)
                nc.scalar.activation(t2[:], t1[:], ACT.Square, scale=0.5).then_inc(q_done, 1)
            for c in range(KD):
                silu(0, c)
            for b in range(B):
                act.wait_ge(x_mm, b + 1)
                if b:
                    act.wait_ge(d_mm, b)
                nc.scalar.activation(xd[:], px[0:XD, :], ACT.Copy).then_inc(x_ev, 1)
                nc.scalar.activation(bc[0:XD, b, :], px[0:XD, :], ACT.Copy, scale=SB).then_inc(bch, 1)
                if b + 1 < B:
                    silu(b + 1, 0)
                    silu(b + 1, 1)
                for h in range(2):
                    inverse(b, h)
                    square(b, h)
                    if b + 1 < B:
                        silu(b + 1, 2 + h)

        @block.vector
        def _(dve):
            ch = Chain(dve, own)
            dve.wait_ge(c_in, 112)
            for j in range(TAPS):
                if j:
                    dve.wait_ge(w_done, j)
                nc.vector.tensor_tensor(wt[:], w32[:], cw[:, j:j + 1, :].to_broadcast([P, KC, D]), ALU.mult
                                        ).then_inc(w_ready, 1)
                dve.wait_ge(w_hi, j + 1)
                nc.vector.scalar_tensor_tensor(out=w_l[:, j, :, :], in0=wt[:], scalar=SW, in1=w_h[:, j, :, :],
                                               op0=ALU.mult, op1=ALU.subtract).then_inc(w_done, 1)
            for b in range(B):
                dve.wait_ge(bch, b + 1)
                nc.vector.scalar_tensor_tensor(out=bc[64:64 + XD, b, :], in0=px[0:XD, :], scalar=SB, in1=bc[0:XD, b, :],
                                               op0=ALU.mult, op1=ALU.subtract).then_inc(bcl, 1)
                dve.wait_ge(d_mm, b + 1)
                for c in range(KD):
                    last = nc.vector.tensor_scalar(delta[:, 4 * b + c, :], pd[:, c, :], dtb[:, c:c + 1], None, ALU.add)
                    if c % 2:
                        last.then_inc(abs_in, 1)
                for h in range(2):
                    i = 2 * b + h
                    sl = slice(4 * b + 2 * h, 4 * b + 2 * h + 2)
                    z, t = du[:, sl, :], delta[:, sl, :]
                    dve.wait_ge(inv_done, 2 * i + 2)
                    ch.link(nc.vector.scalar_tensor_tensor(out=t2[:], in0=z, scalar=2.0, in1=t1[:], op0=ALU.add,
                                                           op1=ALU.mult))
                    ch.link(nc.vector.scalar_tensor_tensor(out=t1[:], in0=t2[:], scalar=2.0, in1=t1[:], op0=ALU.subtract,
                                                           op1=ALU.mult))
                    nc.vector.scalar_tensor_tensor(out=t1[:], in0=z, scalar=-2.0, in1=t1[:], op0=ALU.mult, op1=ALU.mult
                                                   ).then_inc(s_done, 1)
                    dve.wait_ge(q_done, i + 1)
                    ch.link(nc.vector.tensor_scalar(z, t2[:], c4, None, ALU.mult))
                    for cc in (c3, c2, c1):
                        ch.link(nc.vector.scalar_tensor_tensor(out=z, in0=z, scalar=cc, in1=t2[:], op0=ALU.add,
                                                               op1=ALU.mult))
                    ch.link(nc.vector.scalar_tensor_tensor(out=z, in0=z, scalar=1.0, in1=t1[:], op0=ALU.add, op1=ALU.mult))
                    nc.vector.scalar_tensor_tensor(out=t, in0=t, scalar=0.0, in1=z, op0=ALU.max, op1=ALU.add
                                                   ).then_inc(delta_done, 1)


def ssm_scan_block(nc, env, u, delta, du, bc, SB):
    NS, R = 16, 16
    NU = NS * KD
    RA, RB, RH, RC = 4, 3, 4, 3
    with ExitStack() as ctx:
        env.count += 1
        sb, ps = tiles_of(nc, ctx, f"sc{env.count}")
        A = sb("A", [P, KD, NS])
        sel = sb("sel", [P, 2 * NS, P], F16)
        stats, agg, rstd = sb("stats", [P, NT, 6]), sb("agg", [P, NT, 2]), sb("rstd", [P, NT])
        dl = sb("dl", [P, KD, S])
        g = sb("g", [P, KD, D])
        dA, dB = sb("dA", [P, RA, S]), sb("dB", [P, RB, S])
        h, hc, cs = sb("h", [P, RH, S]), sb("hc", [P, RC, S]), sb("cs", [P, 2, S])
        bcb = sb("bcb", [P, S], F16)
        yt = dB[:, 0:2, :]
        py = ps("y", [P, KD, S])
        pb = [ps(f"b{i}", [P, S]) for i in range(2)]
        pc = [ps(f"c{i}", [P, S]) for i in range(2)]
        sem = env.sem
        a_in, a_done, sel_done, own = sem("A_in"), sem("A_exp"), sem("selectors"), sem("scan_dve")
        var_ready, root_done, copied = sem("variances"), sem("roots"), sem("batch_copy")
        z_done, g_done, b_mm, c_mm, c_ev = (sem(n) for n in ("z", "silu_z", "B_rows", "C_rows", "C_ev"))
        dA_done, dB_done, h_done, hc_done, y_mm = (sem(n) for n in ("decay", "input", "state", "stateC", "y_mm"))
        y_ev, yg_done, yt_done, x_done = (sem(n) for n in ("y_ev", "y_gated", "y_T", "x_done"))
        block = ctx.enter_context(nc.Block())

        @block.sync
        def _(sp):
            sp.dma_start(A[:], env.ins["A_log_t"].rearrange("(c p) n -> p c n", p=P)).then_inc(a_in, 16)

        @block.gpsimd
        def _(pool):
            nc.gpsimd.memset(sel[:], 0.0).then_inc(sel_done, 1)
            pool.wait_ge(sel_done, 1)
            for i, off in enumerate((R, 64 + R)):
                nc.gpsimd.affine_select(out=sel[:], in_=sel[:], compare_op=ALU.not_equal, fill=1.0 / SB, base=-off,
                                        pattern=[[-1, 2 * NS], [0, P]], channel_multiplier=1).then_inc(sel_done, 1)
                pool.wait_ge(sel_done, i + 2)
            with pool.Fori(0, B) as b:
                for n in range(NS):
                    for c in range(KD):
                        m = n * KD + c
                        if c == 0:
                            pool.wait_ge(c_ev, b * NS + n + 1)
                        pool.wait_ge(h_done, b * NU + m + 1)
                        if m >= RC:
                            pool.wait_ge(y_mm, b * NU + m - RC + 1)
                        nc.gpsimd.tensor_tensor(hc[:, m % RC, :], h[:, m % RH, :], cs[:, n % 2, :], ALU.mult
                                                ).then_inc(hc_done, 1)
                for c in range(KD):
                    pool.wait_ge(y_ev, b * KD + c + 1)
                    nc.gpsimd.tensor_tensor(yt[:, c % 2, :], yt[:, c % 2, :], g[:, c, :], ALU.mult).then_inc(yg_done, 1)
                pool.wait_ge(x_done, (b + 1) * KD)

        @block.tensor
        def _(pe):
            pe.wait_ge(sel_done, 3)
            with pe.Fori(0, B) as b:
                def rows(n):
                    if n >= 2:
                        pe.wait_ge(dB_done, b * NU + (n - 1) * KD)
                        pe.wait_ge(c_ev, b * NS + n - 1)
                    nc.tensor.matmul(pb[n % 2][:], sel[:, n, :], bcb[:], start=True, stop=True).then_inc(b_mm, 1)
                    nc.tensor.matmul(pc[n % 2][:], sel[:, NS + n, :], bcb[:], start=True, stop=True).then_inc(c_mm, 1)
                pe.wait_ge(copied, b * 2 + 1)
                rows(0)
                for n in range(NS):
                    if n + 1 < NS:
                        rows(n + 1)
                    for c in range(KD):
                        m = n * KD + c
                        pe.wait_ge(hc_done, b * NU + m + 1)
                        nc.tensor.matmul(py[:, c, :], env.id32[:], hc[:, m % RC, :], start=(n == 0),
                                         stop=(n == NS - 1)).then_inc(y_mm, 1)
                for c in range(KD):
                    pe.wait_ge(yg_done, b * KD + c + 1)
                    if c >= 2:
                        pe.wait_ge(x_done, b * KD + c - 1)
                    out = pb[c % 2][:].rearrange("p (t e) -> p t e", e=P)
                    for t in range(TPB):
                        last = nc.tensor.transpose(out[:, t, :], yt[:, c % 2, t * P:(t + 1) * P], env.id32[:])
                    last.then_inc(yt_done, 1)
                pe.wait_ge(x_done, (b + 1) * KD)

        @block.scalar
        def _(act):
            act.wait_ge(var_ready, 1)
            root(nc, rstd[:], agg[:, :, 1], env.eps5, P).then_inc(root_done, 1)
            act.wait_ge(a_in, 16)
            nc.scalar.activation(A[:], A[:], ACT.Exp).then_inc(a_done, 1)
            act.wait_ge(a_done, 2)
            with act.Fori(0, B) as b:
                act.wait_ge(z_done, b + 1)
                nc.scalar.activation(g[:], g[:], ACT.Silu).then_inc(g_done, 1)
                nc.scalar.activation(bcb[:], bc[:, bass.ds(b, 1), :].rearrange("p a s -> p (a s)"), ACT.Copy
                                     ).then_inc(copied, 1)
                nc.scalar.activation(dl[:], delta[:, bass.ds(b * KD, KD), :], ACT.Copy).then_inc(copied, 1)
                act.wait_ge(copied, (b + 1) * 2)
                for n in range(NS):
                    act.wait_ge(c_mm, b * NS + n + 1)
                    if n >= 2:
                        act.wait_ge(hc_done, b * NU + (n - 1) * KD)
                    nc.scalar.activation(cs[:, n % 2, :], pc[n % 2][:], ACT.Copy).then_inc(c_ev, 1)
                    for c in range(KD):
                        m = n * KD + c
                        if m >= RA:
                            act.wait_ge(h_done, b * NU + m - RA + 1)
                        nc.scalar.activation(dA[:, m % RA, :], dl[:, c, :], ACT.Exp, scale=A[:, c, n:n + 1]
                                             ).then_inc(dA_done, 1)
                act.wait_ge(x_done, (b + 1) * KD)

        def update(dve, b, c):
            dve.wait_ge(yt_done, b * KD + c + 1)
            dve.wait_ge(g_done, b + 1)
            xv = env.x[:, bass.ds(b * TPB, TPB), c * P:(c + 1) * P]
            nc.vector.scalar_tensor_tensor(out=xv, in0=pb[c % 2][:].rearrange("p (t e) -> p t e", e=P),
                                           scalar=env.th[:, 2:3], in1=xv, op0=ALU.mult, op1=ALU.add
                                           ).then_inc(x_done, 1)

        @block.vector
        def _(dve):
            ch = Chain(dve, own)
            norm_statistics(nc, dve, env, stats, agg, ch, var_ready)
            dve.wait_ge(a_done, 1)
            nc.vector.tensor_scalar(A[:], A[:], -1.0, None, ALU.mult).then_inc(a_done, 1)
            dve.wait_ge(root_done, 1)
            ch.link(nc.vector.reciprocal(rstd[:], rstd[:]))
            with dve.Fori(0, B) as b:
                for c in range(KD):
                    t = b * KD + c
                    last = nc.vector.tensor_scalar(g[:, c, :], at(env.x, t), agg[:, bass.ds(t, 1), 0], rstd[:, bass.ds(t, 1)],
                                                   ALU.subtract, ALU.mult)
                last.then_inc(z_done, 1)

                def inputs(m):
                    n, c = divmod(m, KD)
                    if c == 0:
                        dve.wait_ge(b_mm, b * NS + n + 1)
                    nc.vector.tensor_tensor(dB[:, m % RB, :], at(du, b * KD + c), pb[n % 2][:], ALU.mult
                                            ).then_inc(dB_done, 1)

                def scan(m):
                    dve.wait_ge(dB_done, b * NU + m + 1)
                    dve.wait_ge(dA_done, b * NU + m + 1)
                    if m >= RH:
                        dve.wait_ge(hc_done, b * NU + m - RH + 1)
                    nc.vector.tensor_tensor_scan(h[:, m % RH, :], dA[:, m % RA, :], dB[:, m % RB, :], 0.0, ALU.mult,
                                                 ALU.add).then_inc(h_done, 1)
                inputs(0)
                for m in range(NU):
                    if m + 1 < NU:
                        if m + 1 >= RB:
                            dve.wait_ge(h_done, b * NU + m + 2 - RB)
                        inputs(m + 1)
                    scan(m)
                dve.wait_ge(h_done, (b + 1) * NU)
                for c in range(KD):
                    dve.wait_ge(y_mm, b * NU + NU - KD + c + 1)
                    if c >= 2:
                        dve.wait_ge(yt_done, b * KD + c - 1)
                    nc.vector.tensor_tensor(yt[:, c % 2, :], py[:, c, :], at(u, b * KD + c), ALU.add).then_inc(y_ev, 1)
                    if c:
                        update(dve, b, c - 1)
                update(dve, b, KD - 1)
                dve.wait_ge(x_done, (b + 1) * KD)


def layer_xattn2(nc, env):
    SB = 64.0
    with ExitStack() as ctx:
        env.count += 1
        sb, _ = tiles_of(nc, ctx, f"ss{env.count}")
        u, delta, du = sb("u", [P, B * KD, S]), sb("delta", [P, B * KD, S]), sb("du", [P, B * KD, S])
        bc = sb("bc", [P, B, S], F16)
        ssm_prepare_block(nc, env, u, delta, du, bc, SB)
        ssm_scan_block(nc, env, u, delta, du, bc, SB)


def store_block(nc, env, out):
    with ExitStack() as ctx:
        stored = env.sem("out_stored")
        block = ctx.enter_context(nc.Block())

        @block.sync
        def _(sp):
            sp.dma_start(out.rearrange("(t p) d -> p t d", p=P), env.x[:]).then_inc(stored, 16)
            sp.wait_ge(stored, 16)


LAYERS = ("xattn0", "ffn0", "xattn1", "ffn1", "xattn2", "ffn2", "xattn3", "ffn3")


def build_program(nc, ins, out, layers=LAYERS):
    with ExitStack() as stack:
        env = Env(nc, stack, ins)
        env.count = 0
        nc.disable_value_cache = True
        setup_block(nc, env)
        for name in layers:
            {"xattn0": layer_xattn0, "ffn0": lambda n, e: layer_ffn(n, e, 0), "xattn1": layer_xattn1,
             "ffn1": layer_ffn1, "xattn2": layer_xattn2, "ffn2": lambda n, e: layer_ffn(n, e, 2),
             "xattn3": layer_xattn3, "ffn3": lambda n, e: layer_ffn(n, e, 3)}[name](nc, env)
            env.recycle()
        store_block(nc, env, out)


def laid_out(v):
    a = {k: np.asarray(x) for k, x in v.items()}
    t = np.ascontiguousarray
    HS = 256
    rope = np.arange(16).reshape(2, 4, 2).transpose(0, 2, 1).reshape(-1)
    perm = (np.arange(32)[:, None] * 16 + rope[None, :]).reshape(-1)
    kv = np.concatenate([a["L0_xattn_Wk"], a["L0_xattn_Wv"]], axis=1).reshape(C, 16, 2, 32)
    bkv = np.concatenate([a["L0_xattn_bk"], a["L0_xattn_bv"]]).reshape(16, 2, 32)
    return {
        "x": a["x"].reshape(T, D),
        "ctx_t": t(a["ctx_1024"].reshape(T, C).T),
        "g_xattn": a["g_xattn"], "g_ffn": a["g_ffn"],
        "up_weight_t": t(a["L0_ffn_up_weight"].reshape(-1, HS, D).transpose(0, 2, 1)),
        "down_weight_t": t(a["L0_ffn_down_weight"].reshape(D, -1, HS).transpose(1, 2, 0)),
        "up_scale_t": t(a["L0_ffn_up_scale"].reshape(-1, P).T),
        "down_scale": a["L0_ffn_down_scale"], "output_scale": a["L0_ffn_output_scale"],
        "gate_w_t": t(a["L2_ffn_gate_w"].T), "w_gate": a["L2_ffn_w_gate"], "w_up": a["L2_ffn_w_up"],
        "w_down": a["L2_ffn_w_down"],
        "W_router": a["L3_ffn_W_router"],
        "exp_up": np.concatenate([a["L3_ffn_Wsh_up"], a["L3_ffn_Wrt_up"]]),
        "exp_down": np.concatenate([a["L3_ffn_Wsh_down"], a["L3_ffn_Wrt_down"]]),
        "Wq0": a["L0_xattn_Wq"], "bq0": a["L0_xattn_bq"], "Wk0": t(kv[:, :, 0]).reshape(C, D), "bk0": t(bkv[:, 0]).reshape(D),
        "Wv0": t(kv[:, :, 1]).reshape(C, D), "bv0": t(bkv[:, 1]).reshape(D),
        "Wkd0": t(a["L0_xattn_Wkv_dca"][:, :D]), "Wvd0": t(a["L0_xattn_Wkv_dca"][:, D:]),
        "bkd0": t(a["L0_xattn_bkv_dca"][:D]), "bvd0": t(a["L0_xattn_bkv_dca"][D:]),
        "qn_w": a["L0_xattn_qn_w"], "qn_b": a["L0_xattn_qn_b"], "kn_w": a["L0_xattn_kn_w"],
        "kn_b": a["L0_xattn_kn_b"], "kd_w": a["L0_xattn_kn_dca_w"], "kd_b": a["L0_xattn_kn_dca_b"],
        "Wo0": a["L0_xattn_Wo"], "bo0": a["L0_xattn_bo"],
        "Wq1": t(a["L1_xattn_Wq"].T), "bq1": a["L1_xattn_bq"].reshape(P, 1), "Wk1": t(a["L1_xattn_Wk"].T),
        "bk1": a["L1_xattn_bk"].reshape(P, 1),
        "weight1": t(a["L1_ffn_weight"].T).view(np.int32),
        "w_scale1": t(a["L1_ffn_w_scale"][:, 0]), "bias1": a["L1_ffn_bias"],
        "in_proj": t(a["L2_xattn_in_proj_w"].T), "conv_w_t": t(a["L2_xattn_conv_w"].T).reshape(-1),
        "conv_b_t": t(a["L2_xattn_conv_b"].reshape(-1, P).T),
        "x_proj": t(a["L2_xattn_x_proj_w"].T), "dt_w": t(a["L2_xattn_dt_proj_w"].T),
        "dt_b_t": t(a["L2_xattn_dt_proj_b"].reshape(-1, P).T), "A_log_t": a["L2_xattn_A_log"],
        "D_t": t(a["L2_xattn_D"].reshape(-1, P).T),
        "fside": a["fside_BxSx2_0"].reshape(T, 2),
        "Wq3": t(a["L3_xattn_Wq"][:, perm]), "Wk3": t(a["L3_xattn_Wkv"][:, :D][:, perm]),
        "Wv3": t(a["L3_xattn_Wkv"][:, D:]), "Wo3": a["L3_xattn_Wout"], "bo3": a["L3_xattn_bout"],
    }


def kernel(**inputs):
    import concourse.bacc as bacc
    from concourse.bass_utils import run_bass_kernel_spmd

    nc = bacc.Bacc("TRN2", target_bir_lowering=False, num_devices=1)
    arrays, ins = {}, {}
    for name, a in laid_out(inputs).items():
        arrays[f"in_{name}"] = a
        ins[name] = nc.dram_tensor(f"in_{name}", a.shape, mybir.dt.from_np(a.dtype), kind="ExternalInput").ap()
    out = nc.dram_tensor("out_x", (T, D), F32, kind="ExternalOutput").ap()
    build_program(nc, ins, out)
    r = run_bass_kernel_spmd(nc, [arrays], core_ids=[0])
    return r.results[0]["out_x"].reshape(B, S, D)
```
